# Optimizing a Trainium2 kernel written in Bass

```python
import numpy as np
import jax
import jax.numpy as jnp

def _softmax(x, axis=-1):
    return jax.nn.softmax(x, axis=axis)

def _gelu(x):
    return jax.nn.gelu(x, approximate=True)

def _silu(x):
    return jax.nn.silu(x)

def _sigmoid(x):
    return jax.nn.sigmoid(x)

def _layernorm(x, axis=-1, eps=1e-05):
    m = jnp.mean(x, axis=axis, keepdims=True)
    v = jnp.var(x, axis=axis, keepdims=True)
    return (x - m) / jnp.sqrt(v + eps)

def _scatter_add(tgt, idx, src, axis=0):
    return tgt.at[idx].add(src)

def _segment_sum(src, seg, n):
    return jax.ops.segment_sum(src, seg, n)
kernel_name = 'mk_gnn_resnorm_d2_gnn_r64_c28e3c'

def setup_inputs(seed: int=0):
    np.random.seed(seed)
    _w = jnp.asarray

    def _rec_inputs():
        import jax
        import jax.numpy as jnp
        _gk = jax.random.key(seed)
        x = -0.0001074 + 0.9999 * jax.random.normal(jax.random.fold_in(_gk, 1), (50000, 256), jnp.float32)
        src = jax.random.randint(jax.random.fold_in(_gk, 2), (12500,), 0, 50000, jnp.int32)
        dst = jnp.minimum((50000 * jax.random.uniform(jax.random.fold_in(_gk, 3), (12500,)) ** 2.0).astype(jnp.int32), 49999)
        _o = jnp.argsort(dst, stable=True)
        src = src[_o]
        dst = dst[_o]
        edge_attr_256 = 9.41057e-06 + 1 * jax.random.normal(jax.random.fold_in(_gk, 11), (12500, 256), jnp.float32)
        return (x, src, dst, edge_attr_256)
    x, src, dst, edge_attr_256 = _rec_inputs()

    def _L0_gnn_setup():
        import jax, jax.numpy as jnp
        import numpy as np
        N_ENT = 50000
        N_EDGE = 500000
        D = 256
        H1, C1 = (8, 64)
        NEG_SLOPE = 0.2
        LN_EPS = 1e-05

        def _gat_conv(x, edge_index, W, att_src, att_dst, bias, heads, out_ch, concat):
            n = x.shape[0]
            loops = jnp.arange(n)
            src = jnp.concatenate([edge_index[0], loops])
            dst = jnp.concatenate([edge_index[1], loops])
            h = (x @ W).reshape(n, heads, out_ch)
            a_src = jnp.sum(h * att_src[None], axis=-1)
            a_dst = jnp.sum(h * att_dst[None], axis=-1)
            e = jax.nn.leaky_relu(a_src[src] + a_dst[dst], NEG_SLOPE)
            m = jax.lax.stop_gradient(jax.ops.segment_max(e, dst, num_segments=n))
            p = jnp.exp(e - m[dst])
            denom = jax.ops.segment_sum(p, dst, num_segments=n)
            alpha = p / denom[dst]
            out = jax.ops.segment_sum(h[src] * alpha[..., None], dst, num_segments=n)
            out = out.reshape(n, heads * out_ch) if concat else out.mean(axis=1)
            return out + bias
        key = jax.random.key(seed)
        ks = jax.random.split(key, 12)
        s = 0.05
        return {'edge_index': jax.random.randint(ks[0], (2, N_EDGE), 0, N_ENT), 'x': jax.random.normal(ks[1], (N_ENT, D), dtype=jnp.float32), 'ln_w': jnp.ones((D,), jnp.float32), 'ln_b': jnp.zeros((D,), jnp.float32), 'W1': jax.random.normal(ks[2], (D, H1 * C1), dtype=jnp.float32) * s, 'att_src1': jax.random.normal(ks[3], (H1, C1), dtype=jnp.float32) * s, 'att_dst1': jax.random.normal(ks[4], (H1, C1), dtype=jnp.float32) * s, 'b1': jnp.zeros((H1 * C1,), jnp.float32), 'W2': jax.random.normal(ks[5], (H1 * C1, D), dtype=jnp.float32) * s, 'att_src2': jax.random.normal(ks[6], (1, D), dtype=jnp.float32) * s, 'att_dst2': jax.random.normal(ks[7], (1, D), dtype=jnp.float32) * s, 'b2': jnp.zeros((D,), jnp.float32)}
    _L0_gnn_all = _L0_gnn_setup()
    _L0_gnn_in = {k: v for k, v in _L0_gnn_all.items() if k in ('ln_w', 'ln_b', 'W1', 'att_src1', 'att_dst1', 'b1', 'W2', 'att_src2', 'att_dst2', 'b2')}
    del _L0_gnn_all

    def _L1_gnn_setup():
        import jax, jax.numpy as jnp
        import numpy as np
        HIDDEN = 256

        def _layernorm(h, gamma, beta, eps=1e-05):
            mu = jnp.mean(h, axis=-1, keepdims=True)
            var = jnp.mean(jnp.square(h - mu), axis=-1, keepdims=True)
            return (h - mu) * jax.lax.rsqrt(var + eps) * gamma + beta
        key = jax.random.key(seed)
        ks = jax.random.split(key, 8)
        N, E, C = (50000, 12500, HIDDEN)
        x = jax.random.normal(ks[0], (N, C), dtype=jnp.float32)
        edge_index = jax.random.randint(ks[1], (2, E), 0, N, dtype=jnp.int64)
        edge_attr = jax.random.normal(ks[2], (E, C), dtype=jnp.float32)
        s = 1.0 / np.sqrt(C)
        W1 = jax.random.uniform(ks[3], (C, C), jnp.float32, -s, s)
        b1 = jax.random.uniform(ks[4], (C,), jnp.float32, -s, s)
        W2 = jax.random.uniform(ks[5], (C, C), jnp.float32, -s, s)
        b2 = jax.random.uniform(ks[6], (C,), jnp.float32, -s, s)
        gamma = jnp.ones((C,), jnp.float32)
        beta = jnp.zeros((C,), jnp.float32)
        return {'x': x, 'edge_index': edge_index, 'edge_attr': edge_attr, 'W1': W1, 'b1': b1, 'W2': W2, 'b2': b2, 'gamma': gamma, 'beta': beta}
    _L1_gnn_all = _L1_gnn_setup()
    _L1_gnn_in = {k: v for k, v in _L1_gnn_all.items() if k in ('W1', 'b1', 'W2', 'b2', 'gamma', 'beta')}
    del _L1_gnn_all
    return {'x': x, 'src': src, 'dst': dst, 'edge_attr_256': edge_attr_256, 'L0_gnn_ln_w': _L0_gnn_in['ln_w'], 'L0_gnn_ln_b': _L0_gnn_in['ln_b'], 'L0_gnn_W1': _L0_gnn_in['W1'], 'L0_gnn_att_src1': _L0_gnn_in['att_src1'], 'L0_gnn_att_dst1': _L0_gnn_in['att_dst1'], 'L0_gnn_b1': _L0_gnn_in['b1'], 'L0_gnn_W2': _L0_gnn_in['W2'], 'L0_gnn_att_src2': _L0_gnn_in['att_src2'], 'L0_gnn_att_dst2': _L0_gnn_in['att_dst2'], 'L0_gnn_b2': _L0_gnn_in['b2'], 'L1_gnn_W1': _L1_gnn_in['W1'], 'L1_gnn_b1': _L1_gnn_in['b1'], 'L1_gnn_W2': _L1_gnn_in['W2'], 'L1_gnn_b2': _L1_gnn_in['b2'], 'L1_gnn_gamma': _L1_gnn_in['gamma'], 'L1_gnn_beta': _L1_gnn_in['beta']}

def reference(x, src, dst, edge_attr_256, L0_gnn_ln_w, L0_gnn_ln_b, L0_gnn_W1, L0_gnn_att_src1, L0_gnn_att_dst1, L0_gnn_b1, L0_gnn_W2, L0_gnn_att_src2, L0_gnn_att_dst2, L0_gnn_b2, L1_gnn_W1, L1_gnn_b1, L1_gnn_W2, L1_gnn_b2, L1_gnn_gamma, L1_gnn_beta):
    import jax
    import jax.numpy as jnp

    def _L0_gnn_ref(edge_index, x, ln_w, ln_b, W1, att_src1, att_dst1, b1, W2, att_src2, att_dst2, b2):
        import jax, jax.numpy as jnp
        import numpy as np
        N_ENT = 50000
        N_EDGE = 500000
        D = 256
        H1, C1 = (8, 64)
        NEG_SLOPE = 0.2
        LN_EPS = 1e-05

        def _gat_conv(x, edge_index, W, att_src, att_dst, bias, heads, out_ch, concat):
            n = x.shape[0]
            loops = jnp.arange(n)
            src = jnp.concatenate([edge_index[0], loops])
            dst = jnp.concatenate([edge_index[1], loops])
            h = (x @ W).reshape(n, heads, out_ch)
            a_src = jnp.sum(h * att_src[None], axis=-1)
            a_dst = jnp.sum(h * att_dst[None], axis=-1)
            e = jax.nn.leaky_relu(a_src[src] + a_dst[dst], NEG_SLOPE)
            m = jax.lax.stop_gradient(jax.ops.segment_max(e, dst, num_segments=n))
            p = jnp.exp(e - m[dst])
            denom = jax.ops.segment_sum(p, dst, num_segments=n)
            alpha = p / denom[dst]
            out = jax.ops.segment_sum(h[src] * alpha[..., None], dst, num_segments=n)
            out = out.reshape(n, heads * out_ch) if concat else out.mean(axis=1)
            return out + bias
        mu = jnp.mean(x, axis=-1, keepdims=True)
        var = jnp.var(x, axis=-1, keepdims=True)
        h = (x - mu) / jnp.sqrt(var + LN_EPS) * ln_w + ln_b
        h = jax.nn.elu(_gat_conv(h, edge_index, W1, att_src1, att_dst1, b1, H1, C1, True))
        return _gat_conv(h, edge_index, W2, att_src2, att_dst2, b2, 1, D, False)

    def _L1_gnn_ref(x, edge_index, edge_attr, W1, b1, W2, b2, gamma, beta):
        import jax, jax.numpy as jnp
        import numpy as np
        HIDDEN = 256

        def _layernorm(h, gamma, beta, eps=1e-05):
            mu = jnp.mean(h, axis=-1, keepdims=True)
            var = jnp.mean(jnp.square(h - mu), axis=-1, keepdims=True)
            return (h - mu) * jax.lax.rsqrt(var + eps) * gamma + beta
        N = x.shape[0]
        src, dst = (edge_index[0], edge_index[1])
        msg = jax.nn.relu(x[src] + edge_attr)
        aggr = jax.ops.segment_sum(msg, dst, num_segments=N)
        z = x + aggr
        h = jax.nn.relu(z @ W1 + b1) @ W2 + b2
        return _layernorm(x + jax.nn.relu(h), gamma, beta)
    edge_index = jnp.stack([src, dst])
    x = _layernorm(x + _L0_gnn_ref(edge_index, x, L0_gnn_ln_w, L0_gnn_ln_b, L0_gnn_W1, L0_gnn_att_src1, L0_gnn_att_dst1, L0_gnn_b1, L0_gnn_W2, L0_gnn_att_src2, L0_gnn_att_dst2, L0_gnn_b2), axis=-1)
    x = _layernorm(x + _L1_gnn_ref(x, edge_index, edge_attr_256, L1_gnn_W1, L1_gnn_b1, L1_gnn_W2, L1_gnn_b2, L1_gnn_gamma, L1_gnn_beta), axis=-1)
    return x

_drawn_inputs = setup_inputs


def setup_inputs(seed=0):
    import zlib

    import numpy as np

    out = dict(_drawn_inputs(seed))
    spreads = {'L0_gnn_ln_w': (1.0, 0.2),
     'L0_gnn_ln_b': (0.0, 0.1),
     'L0_gnn_b1': (0.0, 0.1),
     'L0_gnn_b2': (0.0, 0.1),
     'L1_gnn_gamma': (1.0, 0.2),
     'L1_gnn_beta': (0.0, 0.1)}
    factors = {'L0_gnn_att_src1': 3.105,
     'L0_gnn_att_dst1': 23.181,
     'L0_gnn_att_dst2': 31.144,
     'L1_gnn_b1': 8.0,
     'L1_gnn_b2': 4.51}
    for name, (base, spread) in spreads.items():
        noise = np.random.default_rng([zlib.crc32(name.encode()), seed]).standard_normal(out[name].shape)
        drawn = base * np.exp(spread * noise) if base else spread * noise
        out[name] = jnp.asarray(drawn.astype(out[name].dtype))
    for name, factor in factors.items():
        out[name] = (out[name] * factor).astype(out[name].dtype)
    return out
```

```python
from contextlib import ExitStack

import numpy as np

import concourse.bass as bass
from concourse import mybir

ALU = mybir.AluOpType
ACT = mybir.ActivationFunctionType
F32 = mybir.dt.float32
BF16 = mybir.dt.bfloat16
I32 = mybir.dt.int32
AX_X = mybir.AxisListType.X

P = 128
LN_EPS = 1e-5
NEG_SLOPE = 0.2
NO_NODE = 1 << 20
LOW = -1.0e30


class Item:

    def __init__(self, i, c, per):
        self.i, self.c, self.per = i, c, per

    def index(self, more=0):
        k = self.c + more
        if self.i is None:
            return k
        return self.i * self.per + k if k else self.i * self.per

    def slot(self, ring):
        return self.c % ring

    def uses(self, ring):
        k = self.c // ring + 1
        if self.i is None:
            return k
        base = self.i if self.per == ring else self.i * (self.per // ring)
        return base + k if k else base

    def follows(self, k):
        return self.i is not None or self.c >= k

    def __sub__(self, k):
        return Item(self.i, self.c - k, self.per)


class Ring(list):

    def at(self, item):
        return self[item.slot(len(self))]

    def count(self, item, inc=1):
        n = item.uses(len(self))
        return n if inc == 1 else n * inc


def apart(engine, k):
    engine.sem_inc(k.waits_passed[0], 1)


def done(instruction, sems, item, inc=1):
    instruction.then_inc(sems[item.slot(len(sems))], inc)


def run(engine, steps, per, first, last, step):
    for c in range(min(first, steps)):
        step(None, c)
    if last > first:
        with engine.Fori(first // per, last // per) as i:
            for c in range(per):
                step(i, c)
    for c in range(max(last, first), steps):
        step(None, c)


def each_item(engine, items, per, *stages):

    def step(i, c):
        for lag, stage in enumerate(stages):
            if i is not None or 0 <= c - lag < items:
                stage(Item(i, c - lag, per))

    run(engine, items + len(stages) - 1, per, 2 * per, (items - 1) // per * per, step)


class Shared:
    pass


def build(nc, x, src, dst, edge_attr, ln_w, ln_b, g_w1, att_src1, att_dst1, g_b1, g_w2, att_src2,
          att_dst2, g_b2, m_w1, m_b1, m_w2, m_b2, gamma, beta, out):
    N, D = x.shape
    (E,) = src.shape
    H, C = att_src1.shape
    HC = H * C
    KC = D // P
    MC = HC // P
    T = (E + P - 1) // P
    LAST = E - (T - 1) * P
    assert D == 256 and HC == 512 and LAST < P and T <= P

    ctx = ExitStack()
    k = Shared()
    k.N, k.D, k.E, k.H, k.C, k.HC, k.KC, k.MC, k.T, k.LAST = N, D, E, H, C, HC, KC, MC, T, LAST
    with ctx:
        def sb(name, shape, dt=F32):
            return ctx.enter_context(nc.sbuf_tensor(name, shape, dt))

        k.psum = [ctx.enter_context(nc.psum_tensor(f"bank{b}", [P, 512], F32)) for b in range(8)]
        k.ht_dram = nc.dram_tensor("ht_dram", [T, P, 2 * D], F32).ap()
        k.dst_dram = nc.dram_tensor("dst_dram", [T, P], F32).ap()
        k.fix_dram = nc.dram_tensor("fix_dram", [T, P, D], F32).ap()
        k.fix1_dram = nc.dram_tensor("fix1_dram", [T, P, D], F32).ap()
        k.h2_dram = nc.dram_tensor("h2_dram", [N, D], F32).ap()
        k.x1_dram = nc.dram_tensor("x1_dram", [N, D], F32).ap()
        k.ident = sb("ident", [P, P])
        k.half = sb("minus_half", [P, 2])
        k.eps = sb("eps", [P, 2])
        k.waits_passed = [ctx.enter_context(nc.semaphore("waits_passed"))]
        k.w1 = sb("w1", [P, KC, HC])
        k.w2 = sb("w2", [P, MC, D])
        k.mw1 = sb("mw1", [P, KC, D])
        k.mw2 = sb("mw2", [P, KC, D])
        k.a1 = sb("a1", [P, KC, 2 * H])
        k.a1_const = sb("a1_const", [P, 2 * H])
        k.bias1 = sb("bias1", [P, HC])
        k.bias_parts = sb("bias_parts", [3, HC + 3 * D], BF16)
        k.ones3 = sb("ones3", [3, 2 * P], BF16)
        k.gamma = sb("gamma", [P, D])
        k.beta = sb("beta", [P, D])
        k.att2 = sb("att2", [P, 2, D])
        k.att2_const = sb("att2_const", [P, 1])
        k.src_idx = sb("src_idx", [P, T], I32)
        k.dst_idx = sb("dst_idx", [P, T], I32)
        k.last_idx = sb("last_idx", [P, T], I32)
        k.dst_col = sb("dst_col", [P, T])
        k.prev_col = sb("prev_col", [P, T])
        k.cut_first = sb("cut_first", [T, P])
        k.cut_last = sb("cut_last", [T, P])
        k.is_last = sb("is_last", [T, P])
        k.not_last = sb("not_last", [T, P])
        k.p1 = sb("p1", [P, T, H])
        k.ps1 = sb("ps1", [P, T, H])
        k.p2 = sb("p2", [P, T])
        k.ps2 = sb("ps2", [P, T])
        k.terms2 = sb("terms2", [P, 3, T])
        prepare(nc, k, src, dst, ln_w, ln_b, g_w1, att_src1, att_dst1, g_b1, g_w2, att_src2,
                att_dst2, g_b2, m_w1, m_b1, m_w2, m_b2, gamma, beta)
        with ExitStack() as inner:
            k.terms1 = inner.enter_context(nc.sbuf_tensor("terms1", [P, T, 2, 2 * H], F32))
            gat1_scores(nc, k, x)
            gat1_softmax(nc, k)
        gat1_messages(nc, k)
        dense(nc, k, x, out)
        gat2_replace(nc, k)
        gat2_scores(nc, k)
        gat2_softmax(nc, k)
        gat2_messages(nc, k, x)
        gine(nc, k, edge_attr, out)


def phase(nc, tag):
    ctx = ExitStack()
    made = []

    def clear():
        nc.clear_and_free_semaphores(made)
        nc.all_engine_barrier()

    ctx.callback(clear)

    def sb(name, shape, dt=F32):
        return ctx.enter_context(nc.sbuf_tensor(f"{tag}_{name}", shape, dt))

    def sem(name, ring=1):
        new = Ring(nc.alloc_semaphore(f"{tag}_{name}_{j}") for j in range(ring))
        made.extend(new)
        return new

    return ctx, sb, sem


def prepare(nc, k, src, dst, ln_w, ln_b, g_w1, att_src1, att_dst1, g_b1, g_w2, att_src2, att_dst2,
            g_b2, m_w1, m_b1, m_w2, m_b2, gamma, beta):
    H, C, HC, D, KC, MC, T, E, LAST = k.H, k.C, k.HC, k.D, k.KC, k.MC, k.T, k.E, k.LAST
    NB = HC + 3 * D
    ctx, sb, sem = phase(nc, "prepare")
    with ctx:
        w_in, tab_in, tab_set = sem("w_in"), sem("tab_in"), sem("tab_set")
        ident_set, ones_set, prev_set = sem("ident_set"), sem("ones_set"), sem("prev_set")
        dv, beta_ps, tr_ps, col_set, parts_in, dst_out = (
            sem("dv_step"), sem("beta_ps"), sem("tr_ps"), sem("col_set"), sem("parts_in"), sem("dst_out"))
        prev_in = sem("prev_in")
        lnw = sb("lnw", [P, KC])
        lnb = sb("lnb", [P, KC])
        lnb_cols = sb("lnb_cols", [P, KC, P])
        att = sb("att", [P, 2, HC])
        prod = sb("prod", [P, HC])
        bias = sb("bias", [1, NB])
        b1row = sb("b1row", [P, HC])
        b2row = sb("b2row", [P, D])
        betaw = sb("betaw", [P, HC])
        rest = sb("rest", [1, NB])
        parts = [sb(f"part{j}", [1, NB], BF16) for j in range(3)]
        rows = sb("rows", [T, 4, P], I32)
        rows_f = sb("rows_f", [T, 4, P])
        idx_f = sb("idx_f", [T, 3, P])
        flag = sb("flag", [T, P])

        block = ctx.enter_context(nc.Block())

        def row(a):
            return a.rearrange("(a n) -> a n", a=1)

        n_w = 18

        @block.sync
        def _(sp):
            with nc.allow_non_contiguous_dma(reason="columns of gains, last rows"):
                loads = [
                    (k.w1[:, :, :], g_w1.rearrange("(c p) n -> p c n", p=P)),
                    (k.w2[:, :, :], g_w2.rearrange("(c p) n -> p c n", p=P)),
                    (k.mw1[:, :, :], m_w1.rearrange("(c p) n -> p c n", p=P)),
                    (k.mw2[:, :, :], m_w2.rearrange("(c p) n -> p c n", p=P)),
                    (lnw[:, :], ln_w.rearrange("(c p) -> p c", p=P)),
                    (lnb[:, :], ln_b.rearrange("(c p) -> p c", p=P)),
                    (att[:, 0, :], att_src1.rearrange("h c -> (h c)").partition_broadcast(P)),
                    (att[:, 1, :], att_dst1.rearrange("h c -> (h c)").partition_broadcast(P)),
                    (b1row[:, :], g_b1.partition_broadcast(P)),
                    (b2row[:, :], g_b2.partition_broadcast(P)),
                    (k.gamma[:, :], gamma.partition_broadcast(P)),
                    (k.beta[:, :], beta.partition_broadcast(P)),
                    (k.att2[:, 0, :], att_src2.rearrange("a c -> (a c)").partition_broadcast(P)),
                    (k.att2[:, 1, :], att_dst2.rearrange("a c -> (a c)").partition_broadcast(P)),
                    (bias[:, HC:HC + D], row(g_b2)),
                    (bias[:, HC + D:HC + 2 * D], row(m_b1)),
                    (bias[:, HC + 2 * D:NB], row(m_b2)),
                ]
                assert len(loads) == n_w - 1
                for to, of in loads:
                    sp.dma_start(to, of).then_inc(w_in[0], 16)
                sp.dma_start(bias[:, 0:HC], row(g_b1)).then_inc(w_in[0], 16)
                sp.wait_ge(tab_set[0], 1)
                full = (T - 1) * P
                tables = [
                    (rows[0:T - 1, 0, :], src[0:full].rearrange("(t e) -> t e", e=P)),
                    (rows[T - 1:T, 0, 0:LAST], row(src[full:E])),
                    (rows[0:T - 1, 1, :], dst[0:full].rearrange("(t e) -> t e", e=P)),
                    (rows[T - 1:T, 1, 0:LAST], row(dst[full:E])),
                    (rows[0:T - 1, 2, :], dst[1:full + 1].rearrange("(t e) -> t e", e=P)),
                    (rows[T - 1:T, 2, 0:LAST - 1], row(dst[full + 1:E])),
                    (rows[0:1, 3, 1:P], row(dst[0:P - 1])),
                    (rows[1:T - 1, 3, :], dst[P - 1:full - 1].rearrange("(t e) -> t e", e=P)),
                    (rows[T - 1:T, 3, 0:LAST + 1], row(dst[full - 1:E])),
                ]
                for to, of in tables:
                    sp.dma_start(to, of).then_inc(tab_in[0], 16)
                sp.wait_ge(dv[0], 1)
                sp.dma_start(k.dst_dram[:, :], rows_f[:, 1, :]).then_inc(dst_out[0], 16)
                sp.wait_ge(dst_out[0], 16)
                sp.wait_ge(prev_set[0], 1)
                sp.dma_start(k.prev_col[P - 1:P, 1:T], k.dst_dram[0:T - 1, P - 1:P].rearrange("t a -> a t"))\
                    .then_inc(prev_in[0], 16)
                sp.wait_ge(prev_in[0], 16)
                sp.wait_ge(col_set[0], 1)
                for j in range(3):
                    sp.dma_start(k.bias_parts[j:j + 1, :], parts[j][:, :]).then_inc(parts_in[0], 16)
                sp.wait_ge(parts_in[0], 48)

        @block.gpsimd
        def _(pool):
            nc.gpsimd.memset(rows[:, 0, :], 0)
            nc.gpsimd.memset(rows[:, 1:3, :], NO_NODE)
            nc.gpsimd.memset(rows[:, 3, :], NO_NODE).then_inc(tab_set[0], 1)
            nc.gpsimd.memset(k.ident[:, :], 0.0).then_inc(ident_set[0], 1)
            pool.wait_ge(ident_set[0], 1)
            nc.gpsimd.affine_select(out=k.ident[:, :], in_=k.ident[:, :], compare_op=ALU.not_equal,
                                    fill=1.0, base=0, pattern=[[-1, P]], channel_multiplier=1)\
                .then_inc(ident_set[0], 1)
            nc.gpsimd.memset(k.half[:, :], -0.5)
            nc.gpsimd.memset(k.eps[:, :], LN_EPS)
            nc.gpsimd.memset(k.ones3[:, :], 1.0).then_inc(ones_set[0], 1)
            nc.gpsimd.memset(k.prev_col[:, :], -1.0).then_inc(prev_set[0], 1)

        @block.vector
        def _(dve):
            v = nc.vector
            n = [0]

            def link(ins):
                n[0] += 1
                ins.then_inc(dv[0], 1)
                dve.wait_ge(dv[0], n[0])

            dve.wait_ge(tab_in[0], 9 * 16)
            link(v.tensor_copy(rows_f[:, :, :], rows[:, :, :]))
            link(v.memset(rows_f[0:1, 3, 0:1], -1.0))
            nodes, after, prev = rows_f[:, 1, :], rows_f[:, 2, :], rows_f[:, 3, :]
            v.tensor_tensor(flag[:, :], nodes, prev, ALU.not_equal)
            v.tensor_tensor(k.is_last[:, :], nodes, after, ALU.not_equal)
            link(v.tensor_tensor(k.not_last[:, :], nodes, after, ALU.is_equal))
            v.tensor_scalar(k.cut_first[:, :], flag[:, :], LOW, None, ALU.mult)
            v.tensor_scalar(k.cut_last[:, :], k.is_last[:, :], LOW, None, ALU.mult)
            v.tensor_copy(idx_f[:, 0, :], rows_f[:, 0, :])
            v.tensor_scalar(idx_f[:, 1, :], nodes, float(k.N), None, ALU.is_lt)
            link(v.tensor_scalar(idx_f[:, 2, :], k.not_last[:, :], float(NO_NODE), None, ALU.mult))
            v.tensor_tensor(idx_f[:, 1, :], idx_f[:, 1, :], nodes, ALU.mult)
            link(v.tensor_tensor(idx_f[:, 2, :], idx_f[:, 2, :], nodes, ALU.add))
            dve.wait_ge(tr_ps[0], 1)
            v.tensor_copy(k.src_idx[:, :], k.psum[0][:, 0:T])
            v.tensor_copy(k.dst_idx[:, :], k.psum[1][:, 0:T])
            v.tensor_copy(k.last_idx[:, :], k.psum[2][:, 0:T])
            link(v.tensor_copy(k.dst_col[:, :], k.psum[3][:, 0:T]))

            dve.wait_ge(w_in[0], n_w * 16)
            for c in range(KC):
                v.tensor_copy(lnb_cols[:, c, :], lnb[:, c:c + 1].broadcast_to([P, P]))
            link(v.tensor_copy(betaw[:, :], b1row[:, :]))
            dve.wait_ge(beta_ps[0], 1)
            link(v.tensor_copy(betaw[:, :], k.psum[4][:, :]))
            v.tensor_tensor(k.bias1[:, :], betaw[:, :], b1row[:, :], ALU.add)
            for c in range(KC):
                link(v.tensor_scalar(k.w1[:, c, :], k.w1[:, c, :], lnw[:, c:c + 1], None, ALU.mult))
            for j in range(2):
                for c in range(KC + 1):
                    of = betaw[:, :] if c == KC else k.w1[:, c, :]
                    to = k.a1_const[:, j * H:(j + 1) * H] if c == KC else k.a1[:, c, j * H:(j + 1) * H]
                    link(v.tensor_tensor(prod[:, :], of, att[:, j, :], ALU.mult))
                    link(v.tensor_reduce(to, prod[:, :].rearrange("p (h c) -> p h c", h=H), AX_X, ALU.add))
            link(v.tensor_tensor(prod[:, 0:D], k.att2[:, 0, :], k.att2[:, 1, :], ALU.add))
            link(v.tensor_tensor(prod[:, 0:D], prod[:, 0:D], b2row[:, :], ALU.mult))
            link(v.tensor_reduce(prod[:, D:D + 1], prod[:, 0:D], AX_X, ALU.add))
            link(v.tensor_scalar(k.att2_const[:, :], prod[:, D:D + 1], -1.0, None, ALU.mult))
            link(v.tensor_copy(bias[:, 0:HC], k.bias1[0:1, :]))
            link(v.tensor_copy(parts[0][:, :], bias[:, :]))
            link(v.tensor_tensor(rest[:, :], bias[:, :], parts[0][:, :], ALU.subtract))
            link(v.tensor_copy(parts[1][:, :], rest[:, :]))
            link(v.tensor_tensor(rest[:, :], rest[:, :], parts[1][:, :], ALU.subtract))
            v.tensor_copy(parts[2][:, :], rest[:, :]).then_inc(col_set[0], 1)

        @block.tensor
        def _(pe):
            pe.wait_ge(ident_set[0], 2)
            pe.wait_ge(dv[0], 5)
            for j in range(3):
                nc.tensor.transpose(k.psum[j][:, 0:T], idx_f[:, j, :], k.ident[0:T, 0:T])
            nc.tensor.transpose(k.psum[3][:, 0:T], rows_f[:, 1, :], k.ident[0:T, 0:T]).then_inc(tr_ps[0], 1)
            pe.wait_ge(dv[0], 7)
            for c in range(KC):
                last = nc.tensor.matmul(k.psum[4][:, :], lnb_cols[:, c, :], k.w1[:, c, :],
                                        start=(c == 0), stop=(c == KC - 1))
            last.then_inc(beta_ps[0], 1)


def norm_stats(dve, k, sems, item, data, stats, mv):
    rows = data.shape[1]
    for r in range(rows):
        last = dve.bn_stats(stats[:, r, :], data[:, r, :])
    last.then_inc(sems[0].at(item), 1)
    dve.wait_ge(sems[0].at(item), sems[0].count(item))
    apart(dve, k)
    for r in range(rows):
        last = dve.bn_aggr(mv[:, r, :], stats[:, r, :])
    last.then_inc(sems[1].at(item), 1)


def norm_rstd(pool, k, sems, item, mv, ve, rstd):
    p, rows = ve.shape
    pool.wait_ge(sems[0].at(item), sems[0].count(item))
    pool.tensor_tensor(ve, mv[:, :, 1], k.eps[0:p, 0:rows], ALU.add)\
        .then_inc(sems[1].at(item), 1)
    pool.wait_ge(sems[1].at(item), sems[1].count(item))
    pool.tensor_tensor(rstd, ve, k.half[0:p, 0:rows], ALU.pow)\
        .then_inc(sems[2].at(item), 1)


def norm_apply(dve, rstd_done, item, data, mv, rstd, to):
    dve.wait_ge(rstd_done.at(item), rstd_done.count(item))
    for r in range(data.shape[1]):
        last = dve.tensor_scalar(to[:, r, :], data[:, r, :], mv[:, r, 0:1], rstd[:, r:r + 1],
                                 ALU.subtract, ALU.mult)
    return last


def gat1_scores(nc, k, x):
    H, D, KC, T = k.H, k.D, k.KC, k.T
    PER = 2
    ctx, sb, sem = phase(nc, "gat1_scores")
    with ctx:
        idx_set, rows_in = sem("idx_set"), sem("rows_in", 2)
        st_done, mv_done, ve_done, rs_done = sem("st_done"), sem("mv_done"), sem("ve_done"), sem("rs_done")
        normed, turned, ht_set, ht_out = sem("normed"), sem("turned"), sem("ht_set"), sem("ht_out", 2)
        prods, terms_set = sem("prods"), sem("terms_set")
        idx = [[sb(f"idx{s}{j}", [P, 1], I32) for j in range(2)] for s in range(2)]
        rows = [sb(f"rows{s}", [P, 2, D]) for s in range(2)]
        ht = [sb(f"ht{s}", [P, 2, KC, P]) for s in range(2)]
        stats = [sb(f"stats{s}", [P, 2, 6]) for s in range(2)]
        mv = [sb(f"mv{s}", [P, 2, 2]) for s in range(2)]
        ve = [sb(f"ve{s}", [P, 2]) for s in range(2)]
        rstd = [sb(f"rstd{s}", [P, 2]) for s in range(2)]
        turn_ps = k.psum[0:2]
        prod_ps = k.psum[2:4]
        block = ctx.enter_context(nc.Block())

        @block.gpsimd
        def _(pool):
            def gather(item):
                s = item.slot(2)
                if item.follows(2):
                    pool.wait_ge(rows_in.at(item - 2), rows_in.count(item - 2, 32))
                if item.follows(2):
                    pool.wait_ge(turned.at(item - 2), turned.count(item - 2))
                pool.tensor_copy(idx[s][0][:, :], k.src_idx[:, bass.ds(item.index(), 1)])
                pool.tensor_copy(idx[s][1][:, :], k.dst_idx[:, bass.ds(item.index(), 1)])\
                    .then_inc(idx_set.at(item), 1)
                pool.wait_ge(idx_set.at(item), idx_set.count(item))
                apart(pool, k)
                for j in range(2):
                    pool.indirect_dma_start(
                        out=rows[s][:, j, :], out_offset=None, in_=x[:, :],
                        in_offset=bass.IndirectOffsetOnAxis(idx[s][j][:, :], 0),
                        bounds_check=k.N - 1, oob_is_err=True)\
                        .then_inc(rows_in.at(item), 16)

            def body(item):
                s = item.slot(2)
                norm_rstd(pool, k, (mv_done, ve_done, rs_done), item, mv[s], ve[s][:, :], rstd[s][:, :])

            each_item(pool, T, PER, gather, body)

        @block.vector
        def _(dve):
            def body(item):
                s = item.slot(2)
                dve.wait_ge(rows_in.at(item), rows_in.count(item, 32))
                norm_stats(dve, k, (st_done, mv_done), item, rows[s], stats[s], mv[s])
                norm_apply(dve, rs_done, item, rows[s], mv[s], rstd[s], rows[s])\
                    .then_inc(normed.at(item), 1)
                dve.wait_ge(prods.at(item), prods.count(item))
                to = k.terms1[:, bass.ds(item.index(), 1), :, :].rearrange("p t j h -> p (t j) h")
                const = k.a1_const[:, :].unsqueeze(1).broadcast_to([P, 2, 2 * H])
                dve.tensor_tensor(to, prod_ps[s][:, 0:4 * H].rearrange("p (j h) -> p j h", j=2),
                                       const, ALU.add)\
                    .then_inc(terms_set.at(item), 1)

            each_item(dve, T, PER, body)

        @block.tensor
        def _(pe):
            def body(item):
                s = item.slot(2)
                pe.wait_ge(normed.at(item), normed.count(item))
                if item.follows(2):
                    pe.wait_ge(ht_set.at(item - 2), ht_set.count(item - 2))
                for j in range(2):
                    for c in range(KC):
                        last = pe.transpose(turn_ps[s][:, (j * KC + c) * P:(j * KC + c + 1) * P],
                                            rows[s][:, j, c * P:(c + 1) * P], k.ident[:, :])
                last.then_inc(turned.at(item), 1)
                pe.wait_ge(ht_set.at(item), ht_set.count(item))
                if item.follows(2):
                    pe.wait_ge(terms_set.at(item - 2), terms_set.count(item - 2))
                for j in range(2):
                    for c in range(KC):
                        last = pe.matmul(prod_ps[s][:, j * 2 * H:(j + 1) * 2 * H], ht[s][:, j, c, :],
                                         k.a1[:, c, :], start=(c == 0), stop=(c == KC - 1))
                last.then_inc(prods.at(item), 1)

            each_item(pe, T, PER, body)

        @block.scalar
        def _(act):
            def body(item):
                s = item.slot(2)
                act.wait_ge(turned.at(item), turned.count(item))
                if item.follows(2):
                    act.wait_ge(ht_out.at(item - 2), ht_out.count(item - 2, 16))
                if item.follows(2):
                    act.wait_ge(prods.at(item - 2), prods.count(item - 2))
                act.activation(ht[s][:, :, :, :].rearrange("p j c e -> p (j c e)"), turn_ps[s][:, :],
                                    ACT.Copy)\
                    .then_inc(ht_set.at(item), 1)

            each_item(act, T, PER, body)

        @block.sync
        def _(sp):
            def body(item):
                s = item.slot(2)
                sp.wait_ge(ht_set.at(item), ht_set.count(item))
                sp.dma_start(k.ht_dram[bass.ds(item.index(), 1), :, :].rearrange("t p n -> (t p) n"),
                                  ht[s][:, :, :, :].rearrange("p j c e -> p (j c e)"))\
                    .then_inc(ht_out.at(item), 16)

            each_item(sp, T, PER, body)
            for back in range(2):
                sp.wait_ge(ht_out.at(Item(None, T - 1 - back, PER)), ht_out.count(Item(None, T - 1 - back, PER), 16))


class Link:

    def __init__(self, dve, sem):
        self.dve, self.sem, self.n = dve, sem, 0

    def __call__(self, ins):
        self.n += 1
        ins.then_inc(self.sem[0], 1)
        self.dve.wait_ge(self.sem[0], self.n)


class Segments:

    def __init__(self, k, lines, sb, sem, ps_tile, ps_back):
        T = k.T
        self.k, self.lines, self.ps_tile, self.ps_back = k, lines, ps_tile, ps_back
        self.ends_set, self.ends_turned = sem("ends_set"), sem("ends_turned")
        self.carry_set, self.carry_turned = sem("carry_set"), sem("carry_turned")
        self.ends = sb("ends", [T, 2, lines])
        self.cut_t = sb("cut_t", [lines, T])
        self.carry_t = sb("carry_t", [lines, T + 1])
        self.low = sb("low", [T, 1])
        self.carry = sb("carry", [T, lines])
        self.scans = 0

    def scan(self, dve, link, cut, values, into, ops, start, back):
        T, lines = self.k.T, self.lines
        self.scans += 1

        def way(ap):
            return ap[:, ::-1] if back else ap

        for h in range(lines):
            last = dve.tensor_tensor_scan(way(into[:, h, :]), way(cut), way(values[:, h, :]), start, *ops)
        dve.tensor_reduce(self.low[:, :], cut, AX_X, ALU.min)
        link(dve.memset(self.carry_t[:, :], start))
        dve.tensor_copy(self.ends[:, 0, :], into[:, :, 0 if back else P - 1])
        dve.tensor_copy(self.ends[:, 1, :], self.low[:, 0:1].broadcast_to([T, lines])).then_inc(self.ends_set[0], 1)
        dve.wait_ge(self.ends_turned[0], self.scans)
        link(dve.tensor_copy(self.cut_t[:, :], self.ps_tile[0:lines, P:P + T]))
        to = self.carry_t[:, 0:T] if back else self.carry_t[:, 1:T + 1]
        dve.tensor_tensor_scan(way(to), way(self.cut_t[:, :]), way(self.ps_tile[0:lines, 0:T]), start, *ops)\
            .then_inc(self.carry_set[0], 1)
        dve.wait_ge(self.carry_turned[0], self.scans)
        link(dve.tensor_copy(self.carry[:, :], self.ps_back[0:T, 0:lines]))
        for h in range(lines):
            last = dve.tensor_tensor_scan(way(into[:, h, :]), way(cut), way(values[:, h, :]),
                                          self.carry[:, h:h + 1], *ops)
        link(last)

    def turn(self, pe, scans, backs):
        k, T, lines = self.k, self.k.T, self.lines
        for n in range(scans):
            pe.wait_ge(self.ends_set[0], n + 1)
            pe.transpose(self.ps_tile[0:lines, 0:T], self.ends[:, 0, :], k.ident[0:T, 0:T])
            pe.transpose(self.ps_tile[0:lines, P:P + T], self.ends[:, 1, :], k.ident[0:T, 0:T])\
                .then_inc(self.ends_turned[0], 1)
            pe.wait_ge(self.carry_set[0], n + 1)
            of = self.carry_t[:, 1:T + 1] if backs[n] else self.carry_t[:, 0:T]
            pe.transpose(self.ps_back[0:T, 0:lines], of, k.ident[0:lines, 0:lines])\
                .then_inc(self.carry_turned[0], 1)


def gat1_softmax(nc, k):
    H, T = k.H, k.T
    HB = 4
    ctx, sb, sem = phase(nc, "gat1_softmax")
    with ctx:
        link_sem, raw_set, raw_turned = sem("link"), sem("raw_set"), sem("raw_turned")
        maxima_turned, shifted, exps_set = sem("maxima_turned"), sem("shifted"), sem("exps_set")
        raw = sb("raw", [P, 2, H, T])
        scores, run_max, maxima = (sb(n, [T, H, P]) for n in ("scores", "run_max", "maxima"))
        top = sb("top", [P, H, T])
        seg = Segments(k, H, sb, sem, k.psum[2], k.psum[3])
        block = ctx.enter_context(nc.Block())

        @block.vector
        def _(dve):
            link = Link(dve, link_sem)
            for j in range(2):
                last = dve.tensor_tensor(raw[:, j, :, :], k.terms1[:, :, j, 0:H].rearrange("p t h -> p h t"),
                                         k.terms1[:, :, 1, H:2 * H].rearrange("p t h -> p h t"), ALU.add)
            link(last)
            flat = raw[:, :, :, :].rearrange("p j h t -> p (j h t)")
            dve.scalar_tensor_tensor(flat, flat, NEG_SLOPE, flat, ALU.mult, ALU.max).then_inc(raw_set[0], 1)
            dve.wait_ge(raw_turned[0], 1)
            for b in range(H // HB):
                last = dve.tensor_copy(scores[:, HB * b:HB * (b + 1), :].rearrange("t h e -> t (h e)"),
                                       k.psum[b][0:T, :])
            link(last)
            seg.scan(dve, link, k.cut_first[:, :], scores, run_max, (ALU.add, ALU.max), LOW, False)
            seg.scan(dve, link, k.cut_last[:, :], run_max, maxima, (ALU.add, ALU.max), LOW, True)
            dve.wait_ge(maxima_turned[0], 1)
            for b in range(H // HB):
                of = k.psum[4 + b][:, :].rearrange("p (h e) -> p h e", h=HB)[:, :, 0:T]
                last = dve.tensor_tensor(top[:, HB * b:HB * (b + 1), :], of, raw[:, 1, HB * b:HB * (b + 1), :], ALU.max)
            link(last)
            for j in range(2):
                last = dve.tensor_tensor(raw[:, j, :, :], raw[:, j, :, :], top[:, :, :], ALU.subtract)
            last.then_inc(shifted[0], 1)

        @block.tensor
        def _(pe):
            pe.wait_ge(raw_set[0], 1)
            for h in range(H):
                last = pe.transpose(k.psum[h // HB][0:T, h % HB * P:(h % HB + 1) * P], raw[:, 0, h, :], k.ident[:, :])
            last.then_inc(raw_turned[0], 1)
            seg.turn(pe, 2, (False, True))
            pe.wait_ge(link_sem[0], 2 + 2 * 4)
            for h in range(H):
                last = pe.transpose(k.psum[4 + h // HB][:, h % HB * P:h % HB * P + T], maxima[:, h, :], k.ident[0:T, 0:T])
            last.then_inc(maxima_turned[0], 1)

        @block.scalar
        def _(act):
            act.wait_ge(shifted[0], 1)
            for to, j in ((k.p1, 0), (k.ps1, 1)):
                act.activation(to[:, :, :].rearrange("p t h -> p h t"), raw[:, j, :, :], ACT.Exp).then_inc(exps_set[0], 1)
            act.wait_ge(exps_set[0], 2)


def same_and_carry(dve, item, k, dst_row, same, carry):
    at = bass.ds(item.index(), 1)
    dve.tensor_scalar(same, dst_row, k.dst_col[:, at], None, ALU.is_equal)
    return dve.tensor_scalar(carry, dst_row, k.prev_col[:, at], None, ALU.is_equal)


def gat1_messages(nc, k):
    H, C, HC, D, KC, MC, T = k.H, k.C, k.HC, k.D, k.KC, k.MC, k.T
    PER = 2
    ctx, sb, sem = phase(nc, "gat1_messages")
    with ctx:
        ht_in, same_set = sem("ht_in", 2), sem("same_set")
        h_ps, msg_p_set, msg_set, own_set = sem("h_ps"), sem("msg_p_set"), sem("msg_set"), sem("own_set")
        sum_ps, sum_set, inv_set = sem("sum_ps"), sem("sum_set"), sem("inv_set")
        whole_set, scaled, y_set, exp_set, neg_set, elu_set = (
            sem("whole_set"), sem("scaled"), sem("y_set"), sem("exp_set"), sem("neg_set"), sem("elu_set"))
        turned, et_set, fix_ps, fix_set, fix_out = (
            sem("turned"), sem("et_set"), sem("fix_ps"), sem("fix_set"), sem("fix_out", 2))
        zero_set, den_set = sem("zero_set"), sem("den_set")
        ht = [sb(f"ht{s}", [P, 2, KC, P]) for s in range(2)]
        dst_row = [sb(f"dst_row{s}", [P, P]) for s in range(2)]
        same = [sb(f"same{s}", [P, P]) for s in range(2)]
        carry = [sb(f"carry{s}", [P, P]) for s in range(2)]
        msg = [sb(f"msg{s}", [P, HC + H]) for s in range(2)]
        sums = [sb(f"sums{s}", [P, HC + H]) for s in range(2)]
        inv = [sb(f"inv{s}", [P, H]) for s in range(2)]
        y = [sb(f"y{s}", [P, HC]) for s in range(2)]
        neg = [sb(f"neg{s}", [P, HC]) for s in range(2)]
        et = [sb(f"et{s}", [P, MC, P]) for s in range(2)]
        fix = [sb(f"fix{s}", [P, D]) for s in range(2)]
        src_ps, dst_ps, msum_ps, psum_ps, turn_ps, w2_ps = k.psum[0:6]
        block = ctx.enter_context(nc.Block())

        def heads(ap):
            return ap.rearrange("p (h c) -> p h c", h=H)

        def per_head(ap):
            return ap.unsqueeze(2).broadcast_to([P, H, C])

        @block.sync
        def _(sp):
            def body(item):
                s = item.slot(2)
                if item.follows(2):
                    sp.wait_ge(h_ps.at(item - 2), h_ps.count(item - 2))
                if item.follows(2):
                    sp.wait_ge(same_set.at(item - 2), same_set.count(item - 2))
                t = bass.ds(item.index(), 1)
                sp.dma_start(ht[s][:, :, :, :].rearrange("p j c e -> p (j c e)"),
                                  k.ht_dram[t, :, :].rearrange("t p n -> (t p) n"))\
                    .then_inc(ht_in.at(item), 16)
                sp.dma_start(dst_row[s][:, :], k.dst_dram[t, :].broadcast_to([P, P]))\
                    .then_inc(ht_in.at(item), 16)

            each_item(sp, T, PER, body)

        @block.tensor
        def _(pe):
            def body(item):
                s = item.slot(2)
                pe.wait_ge(ht_in.at(item), ht_in.count(item, 32))
                if item.follows(1):
                    pe.wait_ge(own_set.at(item - 1), own_set.count(item - 1))
                for j, ps in enumerate((src_ps, dst_ps)):
                    for c in range(KC):
                        last = pe.matmul(ps[:, :], ht[s][:, j, c, :], k.w1[:, c, :], start=(c == 0), stop=(c == KC - 1))
                last.then_inc(h_ps.at(item), 1)
                pe.wait_ge(msg_set.at(item), msg_set.count(item))
                if not item.follows(1):
                    pe.wait_ge(zero_set[0], 1)
                if item.follows(1):
                    pe.wait_ge(sum_set.at(item - 1), sum_set.count(item - 1))
                before = sums[(item.slot(2) + 1) % 2]
                for ps, lo, hi in ((msum_ps, 0, HC), (psum_ps, HC, HC + H)):
                    pe.matmul(ps[:, 0:hi - lo], same[s][:, :], msg[s][:, lo:hi], start=True, stop=False)
                    last = pe.matmul(ps[:, 0:hi - lo], carry[s][:, :], before[:, lo:hi], start=False, stop=True)
                last.then_inc(sum_ps.at(item), 1)

            def after(item):
                s = item.slot(2)
                pe.wait_ge(elu_set.at(item), elu_set.count(item))
                if item.follows(1):
                    pe.wait_ge(et_set.at(item - 1), et_set.count(item - 1))
                for m in range(MC):
                    last = pe.transpose(turn_ps[:, m * P:(m + 1) * P], y[s][:, m * P:(m + 1) * P], k.ident[:, :])
                last.then_inc(turned.at(item), 1)
                pe.wait_ge(et_set.at(item), et_set.count(item))
                if item.follows(1):
                    pe.wait_ge(fix_set.at(item - 1), fix_set.count(item - 1))
                pe.matmul(w2_ps[:, 0:D], k.ones3[:, 0:P], k.bias_parts[:, HC:HC + D], start=True, stop=False)
                for m in range(MC):
                    last = pe.matmul(w2_ps[:, 0:D], et[s][:, m, :], k.w2[:, m, :], start=False, stop=(m == MC - 1))
                last.then_inc(fix_ps.at(item), 1)

            each_item(pe, T, PER, body, after)

        @block.vector
        def _(dve):
            dve.memset(sums[1][:, :], 0.0)\
                .then_inc(zero_set.at(Item(None, 0, 1)), 1)

            def body(item):
                s = item.slot(2)
                t = item.index()
                p_t = k.p1[:, bass.ds(t, 1), :].rearrange("p t h -> p (t h)")
                ps_t = k.ps1[:, bass.ds(t, 1), :].rearrange("p t h -> p (t h)")
                dve.wait_ge(ht_in.at(item), ht_in.count(item, 32))
                if item.follows(2):
                    dve.wait_ge(sum_ps.at(item - 2), sum_ps.count(item - 2))
                same_and_carry(dve, item, k, dst_row[s][:, :], same[s][:, :], carry[s][:, :])\
                    .then_inc(same_set.at(item), 1)
                dve.tensor_copy(msg[s][:, HC:HC + H], p_t)
                dve.wait_ge(h_ps.at(item), h_ps.count(item))
                dve.tensor_tensor(heads(msg[s][:, 0:HC]), heads(src_ps[:, :]), per_head(p_t), ALU.mult)\
                    .then_inc(msg_set.at(item), 1)
                if item.follows(2):
                    dve.wait_ge(turned.at(item - 2), turned.count(item - 2))
                dve.tensor_tensor(heads(y[s][:, :]), heads(dst_ps[:, :]), per_head(ps_t), ALU.mult)\
                    .then_inc(own_set.at(item), 1)

            def after(item):
                s = item.slot(2)
                ps_t = k.ps1[:, bass.ds(item.index(), 1), :].rearrange("p t h -> p (t h)")
                dve.wait_ge(sum_set.at(item), sum_set.count(item))
                dve.tensor_tensor(inv[s][:, :], sums[s][:, HC:HC + H], ps_t, ALU.add)\
                    .then_inc(den_set.at(item), 1)
                dve.tensor_tensor(y[s][:, :], y[s][:, :], sums[s][:, 0:HC], ALU.add).then_inc(whole_set[0], 1)
                dve.wait_ge(den_set.at(item), den_set.count(item))
                dve.reciprocal(inv[s][:, :], inv[s][:, :])\
                    .then_inc(inv_set.at(item), 1)
                dve.wait_ge(whole_set.at(item), whole_set.count(item))
                dve.wait_ge(inv_set.at(item), inv_set.count(item))
                dve.tensor_tensor(heads(y[s][:, :]), heads(y[s][:, :]), per_head(inv[s][:, :]), ALU.mult)\
                    .then_inc(scaled.at(item), 1)
                dve.wait_ge(scaled.at(item), scaled.count(item))
                dve.tensor_tensor(y[s][:, :], y[s][:, :], k.bias1[:, :], ALU.add)\
                    .then_inc(y_set.at(item), 1)
                dve.wait_ge(neg_set.at(item), neg_set.count(item))
                dve.tensor_tensor(y[s][:, :], y[s][:, :], neg[s][:, :], ALU.max)\
                    .then_inc(elu_set.at(item), 1)

            each_item(dve, T, PER, body, after)

        @block.gpsimd
        def _(pool):
            def body(item):
                s = item.slot(2)
                pool.wait_ge(exp_set.at(item), exp_set.count(item))
                apart(pool, k)
                pool.tensor_scalar(neg[s][:, :], neg[s][:, :], 1.0, -1.0, ALU.min, ALU.add)\
                    .then_inc(neg_set.at(item), 1)

            each_item(pool, T, PER, body)

        @block.scalar
        def _(act):
            def body(item):
                s = item.slot(2)
                act.wait_ge(sum_ps.at(item), sum_ps.count(item))
                if item.follows(2):
                    act.wait_ge(whole_set.at(item - 2), whole_set.count(item - 2))
                act.activation(sums[s][:, 0:HC], msum_ps[:, :], ACT.Copy)
                act.activation(sums[s][:, HC:HC + H], psum_ps[:, 0:H], ACT.Copy)\
                    .then_inc(sum_set.at(item), 1)

            def after(item):
                s = item.slot(2)
                act.wait_ge(y_set.at(item), y_set.count(item))
                if item.follows(2):
                    act.wait_ge(elu_set.at(item - 2), elu_set.count(item - 2))
                act.activation(neg[s][:, :], y[s][:, :], ACT.Exp)\
                    .then_inc(exp_set.at(item), 1)
                act.wait_ge(turned.at(item), turned.count(item))
                if item.follows(2):
                    act.wait_ge(fix_ps.at(item - 2), fix_ps.count(item - 2))
                act.activation(et[s][:, :, :].rearrange("p m e -> p (m e)"), turn_ps[:, :], ACT.Copy)\
                    .then_inc(et_set.at(item), 1)
                act.wait_ge(fix_ps.at(item), fix_ps.count(item))
                if item.follows(2):
                    act.wait_ge(fix_out.at(item - 2), fix_out.count(item - 2, 16))
                act.activation(fix[s][:, :], w2_ps[:, 0:D], ACT.Copy)\
                    .then_inc(fix_set.at(item), 1)
                act.wait_ge(fix_set.at(item), fix_set.count(item))
                act.dma_start(k.fix_dram[bass.ds(item.index(), 1), :, :].rearrange("t p d -> (t p) d"),
                                   fix[s][:, :])\
                    .then_inc(fix_out.at(item), 16)

            each_item(act, T, PER, body, after)
            for back in range(2):
                act.wait_ge(fix_out.at(Item(None, T - 1 - back, PER)), fix_out.count(Item(None, T - 1 - back, PER), 16))


def dense(nc, k, x, out):
    N, D, HC, KC, MC = k.N, k.D, k.HC, k.KC, k.MC
    PER = 3
    R = 2
    G = R * P
    full = N // G
    rest = (N - full * G) // R
    groups = full + 1
    assert rest * R == N - full * G and 0 < rest < P and full % PER == 0
    ctx, sb, sem = phase(nc, "dense")
    with ctx:
        x_in = sem("x_in", PER)
        st = {n: (sem(f"{n}_st"), sem(f"{n}_mv"), sem(f"{n}_ve"), sem(f"{n}_rstd")) for n in ("x", "y", "v", "s")}
        xn_set, xn_turned, xt_set = sem("xn_set"), sem("xn_turned"), sem("xt_set")
        h_ps, exp_set, neg_set, elu_set = (
            [sem(f"{n}{j}") for j in range(2)] for n in ("h_ps", "exp_set", "neg_set", "elu_set"))
        h2_ps, h2_set, y_set, h2_out = sem("h2_ps"), sem("h2_set"), sem("y_set"), sem("h2_out", PER)
        x1_set, x1_out, x1_turned, zt_set, x1b_set = (
            sem("x1_set"), sem("x1_out", PER), sem("x1_turned"), sem("zt_set"), sem("x1b_set"))
        hid_ps, hid_set, mlp_ps, v_set, a_set, s_set, o_set, o_out = (
            sem("hid_ps"), sem("hid_set"), sem("mlp_ps"), sem("v_set"), sem("a_set"), sem("s_set"),
            sem("o_set"), sem("o_out", PER))

        def ring(name, shape):
            return [sb(f"{name}{s}", shape) for s in range(PER)]

        xs, xn, y, x1b, v = (ring(n, [P, R, D]) for n in ("x", "xn", "y", "x1b", "v"))
        xt, zt, hid = (ring(n, [P, KC, R, P]) for n in ("xt", "zt", "hid"))
        elu = ring("elu", [P, MC, R, P])
        h2 = ring("h2", [P, R, D])
        stats = {n: ring(f"{n}_stats", [P, R, 6]) for n in "xyvs"}
        mv = {n: ring(f"{n}_mv", [P, R, 2]) for n in "xyvs"}
        ve = {n: ring(f"{n}_ve", [P, R]) for n in "xyvs"}
        rstd = {n: ring(f"{n}_rstd", [P, R]) for n in "xyvs"}
        xt_ps, zt_ps, h2_bank, hid_bank, mlp_bank = k.psum[0], k.psum[1], k.psum[4], k.psum[5], k.psum[6]
        h_bank = k.psum[2:4]
        block = ctx.enter_context(nc.Block())

        def in_group(i, c, stage):
            g = c - stage
            if i is None and not 0 <= g < groups:
                return None, 0
            return Item(i, g, PER), rest if i is None and g == full else P

        def steps(engine, step):
            run(engine, groups + 2, PER, 2 * PER, (full - 1) // PER * PER, step)

        def rows(a, item, p):
            return a[bass.ds(item.index() * G, R * p), :].rearrange("(p r) d -> p r d", r=R)

        def flat(a, p):
            return a[0:p, :, :].rearrange("p r d -> p (r d)")

        def cols(t, m, p):
            return t[:, m, :, 0:p]

        @block.sync
        def _(sp):
            def load(item, p):
                if item is not None:
                    if item.follows(PER):
                        sp.wait_ge(y_set.at(item - PER), y_set.count(item - PER))
                    sp.dma_start(xs[item.slot(PER)][0:p, :, :], rows(x, item, p))\
                        .then_inc(x_in.at(item), 16)

            def step(i, c):
                if i is None and c == 0:
                    for g in range(2):
                        load(Item(None, g, PER), P)
                load(*in_group(i, c, -2))
                item, p = in_group(i, c, 1)
                if item is not None:
                    sp.wait_ge(x1_set.at(item), x1_set.count(item))
                    sp.dma_start(rows(k.x1_dram, item, p), y[item.slot(PER)][0:p, :, :])\
                        .then_inc(x1_out.at(item), 16)
                item, p = in_group(i, c, 2)
                if item is not None:
                    sp.wait_ge(o_set.at(item), o_set.count(item))
                    sp.dma_start(rows(out, item, p), v[item.slot(PER)][0:p, :, :])\
                        .then_inc(o_out.at(item), 16)
                item, p = in_group(i, c, 0)
                if item is not None:
                    sp.wait_ge(h2_set.at(item), h2_set.count(item))
                    sp.dma_start(rows(k.h2_dram, item, p), h2[item.slot(PER)][0:p, :, :])\
                        .then_inc(h2_out.at(item), 16)

            steps(sp, step)
            for sems in (h2_out, x1_out, o_out):
                for back in range(PER):
                    sp.wait_ge(sems.at(Item(None, groups - 1 - back, PER)), sems.count(Item(None, groups - 1 - back, PER), 16))

        @block.tensor
        def _(pe):
            def turn(of, ps, item, p):
                for r in range(R):
                    for c in range(KC):
                        at = (c * R + r) * P
                        last = pe.transpose(ps[:, at:at + p], of[0:p, r, c * P:(c + 1) * P], k.ident[0:p, 0:p])
                return last

            def turn_x(item, p):
                pe.wait_ge(xn_set.at(item), xn_set.count(item))
                if item.follows(1):
                    pe.wait_ge(xt_set.at(item - 1), xt_set.count(item - 1))
                turn(xn[item.slot(PER)], xt_ps, item, p)\
                    .then_inc(xn_turned.at(item), 1)

            def gat1_half(item, p, j):
                s = item.slot(PER)
                pe.wait_ge(xt_set.at(item), xt_set.count(item))
                if item.follows(1):
                    pe.wait_ge(elu_set[j].at(item - 1), elu_set[j].count(item - 1))
                bank = h_bank[j][:, :].rearrange("q (m r p) -> q m r p", m=MC // 2, r=R)
                ones = k.ones3[:, :].rearrange("q (r p) -> q r p", r=R)[:, :, 0:p]
                for m in range(MC // 2):
                    ch = (j * MC // 2 + m) * P
                    pe.matmul(cols(bank, m, p), k.bias_parts[:, ch:ch + P], ones, start=True, stop=False)
                    for c in range(KC):
                        last = pe.matmul(cols(bank, m, p), k.w1[:, c, ch:ch + P], xt[s][:, c, :, 0:p],
                                         start=False, stop=(c == KC - 1))
                last.then_inc(h_ps[j].at(item), 1)

            def rows_product(item, p, bank, bias_at, left, weights, chunks, ready, ps_done):
                for r in range(R):
                    to = bank[0:p, r * D:(r + 1) * D]
                    pe.matmul(to, k.ones3[:, 0:p], k.bias_parts[:, bias_at:bias_at + D], start=True, stop=False)
                    for m in range(chunks):
                        if r == 0 and m in ready:
                            pe.wait_ge(ready[m].at(item), ready[m].count(item))
                        last = pe.matmul(to, left[:, m, r, 0:p], weights[:, m, :], start=False, stop=(m == chunks - 1))
                last.then_inc(ps_done.at(item), 1)

            def gat2_in(item, p):
                if item.follows(1):
                    pe.wait_ge(y_set.at(item - 1), y_set.count(item - 1))
                rows_product(item, p, h2_bank, HC, elu[item.slot(PER)], k.w2, MC,
                             {0: elu_set[0], MC // 2: elu_set[1]}, h2_ps)

            def mlp_hidden(item, p):
                s = item.slot(PER)
                pe.wait_ge(zt_set.at(item), zt_set.count(item))
                if item.follows(1):
                    pe.wait_ge(hid_set.at(item - 1), hid_set.count(item - 1))
                bank = hid_bank[:, :].rearrange("q (m r p) -> q m r p", m=KC, r=R)
                ones = k.ones3[:, :].rearrange("q (r p) -> q r p", r=R)[:, :, 0:p]
                for m in range(KC):
                    at = HC + D + m * P
                    pe.matmul(cols(bank, m, p), k.bias_parts[:, at:at + P], ones, start=True, stop=False)
                    for c in range(KC):
                        last = pe.matmul(cols(bank, m, p), k.mw1[:, c, m * P:(m + 1) * P], zt[s][:, c, :, 0:p],
                                         start=False, stop=(c == KC - 1))
                last.then_inc(hid_ps.at(item), 1)

            def mlp_out(item, p):
                pe.wait_ge(hid_set.at(item), hid_set.count(item))
                if item.follows(1):
                    pe.wait_ge(v_set.at(item - 1), v_set.count(item - 1))
                rows_product(item, p, mlp_bank, HC + 2 * D, hid[item.slot(PER)], k.mw2, KC, {}, mlp_ps)

            def step(i, c):
                if i is None and c == 0:
                    turn_x(Item(None, 0, PER), P)
                now, p = in_group(i, c, 0)
                was, q = in_group(i, c, 1)
                soon, o = in_group(i, c, -1)
                if now is not None:
                    gat1_half(now, p, 0)
                if was is not None:
                    pe.wait_ge(x1_set.at(was), x1_set.count(was))
                    if was.follows(1):
                        pe.wait_ge(zt_set.at(was - 1), zt_set.count(was - 1))
                    turn(y[was.slot(PER)], zt_ps, was, q).then_inc(x1_turned.at(was), 1)
                if now is not None:
                    gat1_half(now, p, 1)
                if was is not None:
                    mlp_hidden(was, q)
                if soon is not None:
                    turn_x(soon, o)
                if now is not None:
                    gat2_in(now, p)
                if was is not None:
                    mlp_out(was, q)

            steps(pe, step)

        @block.scalar
        def _(act):
            def copy_turned(ps, to, p):
                return act.activation(to[:, :, :, 0:p], ps[:, :].rearrange("q (c r p) -> q c r p", c=KC, r=R)[:, :, :, 0:p], ACT.Copy)

            def copy_xt(item, p):
                act.wait_ge(xn_turned.at(item), xn_turned.count(item))
                if item.follows(PER):
                    act.wait_ge(h_ps[1].at(item - PER), h_ps[1].count(item - PER))
                copy_turned(xt_ps, xt[item.slot(PER)], p).then_inc(xt_set.at(item), 1)

            def exp_half(item, p, j):
                act.wait_ge(h_ps[j].at(item), h_ps[j].count(item))
                if item.follows(PER):
                    act.wait_ge(h2_ps.at(item - PER), h2_ps.count(item - PER))
                half = elu[item.slot(PER)][:, j * MC // 2:(j + 1) * MC // 2, :, 0:p]
                bank = h_bank[j][:, :].rearrange("q (m r p) -> q m r p", m=MC // 2, r=R)[:, :, :, 0:p]
                act.activation(half, bank, ACT.Exp).then_inc(exp_set[j].at(item), 1)

            def step(i, c):
                if i is None and c == 0:
                    copy_xt(Item(None, 0, PER), P)
                now, p = in_group(i, c, 0)
                was, q = in_group(i, c, 1)
                soon, o = in_group(i, c, -1)
                if now is not None:
                    exp_half(now, p, 0)
                if was is not None:
                    act.wait_ge(x1_turned.at(was), x1_turned.count(was))
                    if was.follows(PER):
                        act.wait_ge(hid_ps.at(was - PER), hid_ps.count(was - PER))
                    copy_turned(zt_ps, zt[was.slot(PER)], q).then_inc(zt_set.at(was), 1)
                if now is not None:
                    exp_half(now, p, 1)
                if was is not None:
                    act.wait_ge(hid_ps.at(was), hid_ps.count(was))
                    if was.follows(PER):
                        act.wait_ge(mlp_ps.at(was - PER), mlp_ps.count(was - PER))
                    bank = hid_bank[:, :].rearrange("q (m r p) -> q m r p", m=KC, r=R)[:, :, :, 0:q]
                    act.activation(hid[was.slot(PER)][:, :, :, 0:q], bank, ACT.Relu)\
                        .then_inc(hid_set.at(was), 1)
                if soon is not None:
                    copy_xt(soon, o)
                if now is not None:
                    act.wait_ge(h2_ps.at(now), h2_ps.count(now))
                    if now.follows(PER):
                        act.wait_ge(h2_out.at(now - PER), h2_out.count(now - PER, 16))
                    act.activation(flat(h2[now.slot(PER)], p), h2_bank[0:p, :], ACT.Copy)\
                        .then_inc(h2_set.at(now), 1)

            steps(act, step)

        def stats_of(n, item, p, data):
            s = item.slot(PER)
            return (st[n][0], st[n][1]), item, data[s][0:p, :, :], stats[n][s][0:p], mv[n][s][0:p]

        def apply_of(n, item, p, data):
            s = item.slot(PER)
            return st[n][3], item, data[s][0:p, :, :], mv[n][s][0:p], rstd[n][s][0:p], data[s][0:p, :, :]

        @block.gpsimd
        def _(pool):
            def rstd_of(n, item, p):
                if item is not None:
                    s = item.slot(PER)
                    norm_rstd(pool, k, st[n][1:4], item, mv[n][s][0:p], ve[n][s][0:p, :], rstd[n][s][0:p, :])

            def neg_half(item, p, j):
                if item is not None:
                    pool.wait_ge(exp_set[j].at(item), exp_set[j].count(item))
                    apart(pool, k)
                    half = elu[item.slot(PER)][:, j * MC // 2:(j + 1) * MC // 2, :, 0:p]
                    pool.tensor_scalar(half, half, 1.0, -1.0, ALU.min, ALU.add)\
                        .then_inc(neg_set[j].at(item), 1)

            def step(i, c):
                if i is None and c == 0:
                    rstd_of("x", Item(None, 0, PER), P)
                now, p = in_group(i, c, 0)
                was, q = in_group(i, c, 1)
                old, o = in_group(i, c, 2)
                rstd_of("y", was, q)
                rstd_of("v", old, o)
                rstd_of("x", *in_group(i, c, -1))
                neg_half(now, p, 0)
                if was is not None:
                    pool.wait_ge(x1_set.at(was), x1_set.count(was))
                    if was.follows(PER):
                        pool.wait_ge(s_set.at(was - PER), s_set.count(was - PER))
                    s = was.slot(PER)
                    beta = k.beta[0:q, :].unsqueeze(1).broadcast_to([q, R, D])
                    pool.tensor_tensor(x1b[s][0:q, :, :], y[s][0:q, :, :], beta, ALU.add)\
                        .then_inc(x1b_set.at(was), 1)
                neg_half(now, p, 1)
                rstd_of("s", old, o)

            steps(pool, step)

        @block.vector
        def _(dve):
            def elu_half(item, p, j):
                if item is not None:
                    dve.wait_ge(neg_set[j].at(item), neg_set[j].count(item))
                    half = elu[item.slot(PER)][:, j * MC // 2:(j + 1) * MC // 2, :, 0:p]
                    bank = h_bank[j][:, :].rearrange("q (m r p) -> q m r p", m=MC // 2, r=R)[:, :, :, 0:p]
                    dve.tensor_tensor(half, bank, half, ALU.max)\
                        .then_inc(elu_set[j].at(item), 1)

            def norm_x(item, p):
                if item is not None:
                    s = item.slot(PER)
                    if item.follows(PER):
                        dve.wait_ge(xn_turned.at(item - PER), xn_turned.count(item - PER))
                    how = st["x"][3], item, xs[s][0:p, :, :], mv["x"][s][0:p], rstd["x"][s][0:p], xn[s][0:p, :, :]
                    norm_apply(dve, *how).then_inc(xn_set.at(item), 1)

            def stats_x(item, p):
                if item is not None:
                    dve.wait_ge(x_in.at(item), x_in.count(item, 16))
                    norm_stats(dve, k, *stats_of("x", item, p, xs))

            def step(i, c):
                if i is None and c == 0:
                    stats_x(Item(None, 0, PER), P)
                    norm_x(Item(None, 0, PER), P)
                now, p = in_group(i, c, 0)
                was, q = in_group(i, c, 1)
                old, o = in_group(i, c, 2)
                soon, u = in_group(i, c, -1)
                if was is not None:
                    s = was.slot(PER)
                    dve.wait_ge(h2_set.at(was), h2_set.count(was))
                    if was.follows(PER):
                        dve.wait_ge(x1_out.at(was - PER), x1_out.count(was - PER, 16))
                    if was.follows(PER):
                        dve.wait_ge(x1_turned.at(was - PER), x1_turned.count(was - PER))
                    if was.follows(PER):
                        dve.wait_ge(x1b_set.at(was - PER), x1b_set.count(was - PER))
                    dve.tensor_tensor(flat(y[s], q), h2_bank[0:q, :], flat(xs[s], q), ALU.add)\
                        .then_inc(y_set.at(was), 1)
                    dve.wait_ge(y_set.at(was), y_set.count(was))
                    norm_stats(dve, k, *stats_of("y", was, q, y))
                if old is not None:
                    s = old.slot(PER)
                    dve.wait_ge(mlp_ps.at(old), mlp_ps.count(old))
                    if old.follows(PER):
                        dve.wait_ge(o_out.at(old - PER), o_out.count(old - PER, 16))
                    dve.scalar_tensor_tensor(flat(v[s], o), mlp_bank[0:o, :], 0.0, flat(y[s], o), ALU.max, ALU.add)\
                        .then_inc(v_set.at(old), 1)
                if was is not None:
                    norm_apply(dve, *apply_of("y", was, q, y)).then_inc(x1_set.at(was), 1)
                if old is not None:
                    dve.wait_ge(v_set.at(old), v_set.count(old))
                    norm_stats(dve, k, *stats_of("v", old, o, v))
                stats_x(soon, u)
                if old is not None:
                    s = old.slot(PER)
                    dve.wait_ge(st["v"][1].at(old), st["v"][1].count(old))
                    for r in range(R):
                        last = dve.scalar_tensor_tensor(v[s][0:o, r, :], v[s][0:o, r, :], mv["v"][s][0:o, r, 0:1],
                                                        k.gamma[0:o, :], ALU.subtract, ALU.mult)
                    last.then_inc(a_set.at(old), 1)
                norm_x(soon, u)
                elu_half(now, p, 0)
                if old is not None:
                    s = old.slot(PER)
                    dve.wait_ge(a_set.at(old), a_set.count(old))
                    dve.wait_ge(st["v"][3].at(old), st["v"][3].count(old))
                    dve.wait_ge(x1b_set.at(old), x1b_set.count(old))
                    for r in range(R):
                        last = dve.scalar_tensor_tensor(v[s][0:o, r, :], v[s][0:o, r, :], rstd["v"][s][0:o, r:r + 1],
                                                        x1b[s][0:o, r, :], ALU.mult, ALU.add)
                    last.then_inc(s_set.at(old), 1)
                    dve.wait_ge(s_set.at(old), s_set.count(old))
                    norm_stats(dve, k, *stats_of("s", old, o, v))
                elu_half(now, p, 1)
                if old is not None:
                    norm_apply(dve, *apply_of("s", old, o, v)).then_inc(o_set.at(old), 1)

            steps(dve, step)


def gat2_replace(nc, k):
    D, T = k.D, k.T
    PER = 2
    ctx, sb, sem = phase(nc, "gat2_replace")
    with ctx:
        fix_in, idx_set, fix_out = sem("fix_in", 2), sem("idx_set"), sem("fix_out", 2)
        prod_set, term_set = sem("prod_set"), sem("term_set")
        fix = [sb(f"fix{s}", [P, D]) for s in range(2)]
        idx = [sb(f"idx{s}", [P, 1], I32) for s in range(2)]
        prod = [sb(f"prod{s}", [P, 2, D]) for s in range(2)]
        block = ctx.enter_context(nc.Block())

        @block.sync
        def _(sp):
            def body(item):
                s = item.slot(2)
                if item.follows(2):
                    sp.wait_ge(fix_out.at(item - 2), fix_out.count(item - 2, 16))
                if item.follows(2):
                    sp.wait_ge(prod_set.at(item - 2), prod_set.count(item - 2))
                sp.dma_start(fix[s][:, :], k.fix_dram[bass.ds(item.index(), 1), :, :].rearrange("t p d -> (t p) d"))\
                    .then_inc(fix_in.at(item), 16)

            each_item(sp, T, PER, body)

        @block.gpsimd
        def _(pool):
            def body(item):
                s = item.slot(2)
                if item.follows(2):
                    pool.wait_ge(fix_out.at(item - 2), fix_out.count(item - 2, 16))
                pool.tensor_copy(idx[s][:, :], k.last_idx[:, bass.ds(item.index(), 1)])\
                    .then_inc(idx_set.at(item), 1)
                pool.wait_ge(idx_set.at(item), idx_set.count(item))
                pool.wait_ge(fix_in.at(item), fix_in.count(item, 16))
                apart(pool, k)
                pool.indirect_dma_start(out=k.h2_dram[:, :], out_offset=bass.IndirectOffsetOnAxis(idx[s][:, :], 0),
                                             in_=fix[s][:, :], in_offset=None, bounds_check=k.N - 1,
                                             oob_is_err=False)\
                    .then_inc(fix_out.at(item), 16)

            each_item(pool, T, PER, body)
            for back in range(2):
                pool.wait_ge(fix_out.at(Item(None, T - 1 - back, PER)), fix_out.count(Item(None, T - 1 - back, PER), 16))

        @block.vector
        def _(dve):
            def body(item):
                s = item.slot(2)
                dve.wait_ge(fix_in.at(item), fix_in.count(item, 16))
                row = fix[s][:, :].unsqueeze(1).broadcast_to([P, 2, D])
                dve.tensor_tensor(prod[s][:, :, :], row, k.att2[:, :, :], ALU.mult)\
                    .then_inc(prod_set.at(item), 1)
                dve.wait_ge(prod_set.at(item), prod_set.count(item))
                dve.tensor_reduce(k.terms2[:, 1:3, bass.ds(item.index(), 1)], prod[s][:, :, :], AX_X, ALU.add)\
                    .then_inc(term_set.at(item), 1)

            each_item(dve, T, PER, body)


def gat2_scores(nc, k):
    D, T = k.D, k.T
    PER = 2
    ctx, sb, sem = phase(nc, "gat2_scores")
    with ctx:
        rows_in, idx_set, prod_set, term_set = sem("rows_in", 2), sem("idx_set"), sem("prod_set"), sem("term_set")
        rows = [sb(f"rows{s}", [P, D]) for s in range(2)]
        idx = [sb(f"idx{s}", [P, 1], I32) for s in range(2)]
        prod = [sb(f"prod{s}", [P, D]) for s in range(2)]
        block = ctx.enter_context(nc.Block())

        @block.gpsimd
        def _(pool):
            def body(item):
                s = item.slot(2)
                if item.follows(2):
                    pool.wait_ge(rows_in.at(item - 2), rows_in.count(item - 2, 16))
                if item.follows(2):
                    pool.wait_ge(prod_set.at(item - 2), prod_set.count(item - 2))
                pool.tensor_copy(idx[s][:, :], k.src_idx[:, bass.ds(item.index(), 1)])\
                    .then_inc(idx_set.at(item), 1)
                pool.wait_ge(idx_set.at(item), idx_set.count(item))
                apart(pool, k)
                pool.indirect_dma_start(out=rows[s][:, :], out_offset=None, in_=k.h2_dram[:, :],
                                             in_offset=bass.IndirectOffsetOnAxis(idx[s][:, :], 0),
                                             bounds_check=k.N - 1, oob_is_err=True)\
                    .then_inc(rows_in.at(item), 16)

            each_item(pool, T, PER, body)

        @block.vector
        def _(dve):
            def body(item):
                s = item.slot(2)
                dve.wait_ge(rows_in.at(item), rows_in.count(item, 16))
                dve.tensor_tensor(prod[s][:, :], rows[s][:, :], k.att2[:, 0, :], ALU.mult)\
                    .then_inc(prod_set.at(item), 1)
                dve.wait_ge(prod_set.at(item), prod_set.count(item))
                dve.tensor_reduce(k.terms2[:, 0, bass.ds(item.index(), 1)], prod[s][:, :], AX_X, ALU.add)\
                    .then_inc(term_set.at(item), 1)

            each_item(dve, T, PER, body)


def gat2_softmax(nc, k):
    T = k.T
    ctx, sb, sem = phase(nc, "gat2_softmax")
    with ctx:
        link_sem, rows_turned, shifted, exps_set, exps_turned, tables_set = (
            sem("link"), sem("rows_turned"), sem("shifted"), sem("exps_set"), sem("exps_turned"), sem("tables_set"))
        const = k.att2_const
        rows = sb("rows", [T, 3, P])
        spread = sb("spread", [T, 2, P])
        score = sb("score", [T, 2, P])
        run_max, maxima = sb("run_max", [T, 1, P]), sb("maxima", [T, 1, P])

        def names(tag):
            return (lambda n, shape, dt=F32: sb(f"{tag}_{n}", shape, dt)), (lambda n, ring=1: sem(f"{tag}_{n}", ring))

        seg_sum = Segments(k, 2, *names("spread"), k.psum[1], k.psum[2])
        seg_max = Segments(k, 1, *names("max"), k.psum[3], k.psum[4])
        block = ctx.enter_context(nc.Block())

        @block.vector
        def _(dve):
            link = Link(dve, link_sem)
            dve.wait_ge(rows_turned[0], 1)
            link(dve.tensor_copy(rows[:, :, :].rearrange("t n e -> t (n e)"), k.psum[0][0:T, 0:3 * P]))
            for j in range(2):
                last = dve.tensor_tensor(rows[:, 1 + j, :], rows[:, 1 + j, :], k.is_last[:, :], ALU.mult)
            link(last)
            seg_sum.scan(dve, link, k.not_last[:, :], rows[:, 1:3, :], spread, (ALU.mult, ALU.add), 0.0, True)
            dve.tensor_tensor(score[:, 0, :], rows[:, 0, :], spread[:, 1, :], ALU.add)
            link(dve.tensor_tensor(score[:, 1, :], spread[:, 0, :], spread[:, 1, :], ALU.add))
            flat = score[:, :, :].rearrange("t j e -> t (j e)")
            link(dve.tensor_scalar(flat, flat, const[0:T, :], None, ALU.add))
            link(dve.scalar_tensor_tensor(flat, flat, NEG_SLOPE, flat, ALU.mult, ALU.max))
            seg_max.scan(dve, link, k.cut_first[:, :], score[:, 0:1, :], run_max, (ALU.add, ALU.max), LOW, False)
            seg_max.scan(dve, link, k.cut_last[:, :], run_max, maxima, (ALU.add, ALU.max), LOW, True)
            link(dve.tensor_tensor(maxima[:, 0, :], maxima[:, 0, :], score[:, 1, :], ALU.max))
            for j in range(2):
                last = dve.tensor_tensor(score[:, j, :], score[:, j, :], maxima[:, 0, :], ALU.subtract)
            last.then_inc(shifted[0], 1)
            dve.wait_ge(exps_turned[0], 1)
            dve.tensor_copy(k.p2[:, :], k.psum[5][:, 0:T])
            dve.tensor_copy(k.ps2[:, :], k.psum[5][:, P:P + T]).then_inc(tables_set[0], 1)

        @block.scalar
        def _(act):
            act.wait_ge(shifted[0], 1)
            flat = score[:, :, :].rearrange("t j e -> t (j e)")
            act.activation(flat, flat, ACT.Exp).then_inc(exps_set[0], 1)

        @block.tensor
        def _(pe):
            for j in range(3):
                last = pe.transpose(k.psum[0][0:T, j * P:(j + 1) * P], k.terms2[:, j, :], k.ident[:, :])
            last.then_inc(rows_turned[0], 1)
            seg_sum.turn(pe, 1, (True,))
            seg_max.turn(pe, 2, (False, True))
            pe.wait_ge(exps_set[0], 1)
            for j in range(2):
                last = pe.transpose(k.psum[5][:, j * P:j * P + T], score[:, j, :], k.ident[0:T, 0:T])
            last.then_inc(exps_turned[0], 1)


def gat2_messages(nc, k, x):
    D, T = k.D, k.T
    PER = 2
    ctx, sb, sem = phase(nc, "gat2_messages")
    with ctx:
        idx_set, src_in, own_in, same_set, msg_set = (
            sem("idx_set"), sem("src_in", 2), sem("own_in", 2), sem("same_set"), sem("msg_set"))
        sum_ps, sum_set, zero_set = sem("sum_ps"), sem("sum_set"), sem("zero_set")
        den_set, inv_set, num_set, y_set = sem("den_set"), sem("inv_set"), sem("num_set"), sem("y_set")
        st = [sem(n) for n in ("st_done", "mv_done", "ve_done", "rs_done")]
        x1_set, x1_out, copy_out = sem("x1_set"), sem("x1_out", 2), sem("copy_out", 2)
        idx = [[sb(f"idx{s}{j}", [P, 1], I32) for j in range(3)] for s in range(2)]
        h2_src = [sb(f"h2_src{s}", [P, D]) for s in range(2)]
        x_own = [sb(f"x_own{s}", [P, D]) for s in range(2)]
        fix = [sb(f"fix{s}", [P, D]) for s in range(2)]
        dst_row = [sb(f"dst_row{s}", [P, P]) for s in range(2)]
        same = [sb(f"same{s}", [P, P]) for s in range(2)]
        carry = [sb(f"carry{s}", [P, P]) for s in range(2)]
        msg = [sb(f"msg{s}", [P, D + 1]) for s in range(2)]
        sums = [sb(f"sums{s}", [P, D + 1]) for s in range(2)]
        inv = [sb(f"inv{s}", [P, 1]) for s in range(2)]
        y = [sb(f"y{s}", [P, 1, D]) for s in range(2)]
        stats, mv = [sb(f"stats{s}", [P, 1, 6]) for s in range(2)], [sb(f"mv{s}", [P, 1, 2]) for s in range(2)]
        ve, rstd = [sb(f"ve{s}", [P, 1]) for s in range(2)], [sb(f"rstd{s}", [P, 1]) for s in range(2)]
        sum_bank = k.psum[0:2]
        block = ctx.enter_context(nc.Block())

        @block.sync
        def _(sp):
            def body(item):
                s = item.slot(2)
                t = bass.ds(item.index(), 1)
                if item.follows(2):
                    sp.wait_ge(y_set.at(item - 2), y_set.count(item - 2))
                if item.follows(2):
                    sp.wait_ge(same_set.at(item - 2), same_set.count(item - 2))
                sp.dma_start(fix[s][:, :], k.fix_dram[t, :, :].rearrange("t p d -> (t p) d"))\
                    .then_inc(own_in.at(item), 16)
                sp.dma_start(dst_row[s][:, :], k.dst_dram[t, :].broadcast_to([P, P]))\
                    .then_inc(own_in.at(item), 16)

            def store(item):
                sp.wait_ge(x1_set.at(item), x1_set.count(item))
                sp.dma_start(k.fix1_dram[bass.ds(item.index(), 1), :, :].rearrange("t p d -> (t p) d"),
                                  y[item.slot(2)][:, 0, :])\
                    .then_inc(copy_out.at(item), 16)

            each_item(sp, T, PER, body, store)
            for back in range(2):
                sp.wait_ge(copy_out.at(Item(None, T - 1 - back, PER)), copy_out.count(Item(None, T - 1 - back, PER), 16))

        @block.gpsimd
        def _(pool):
            def gather(item):
                s = item.slot(2)
                t = bass.ds(item.index(), 1)
                if item.follows(2):
                    pool.wait_ge(src_in.at(item - 2), src_in.count(item - 2, 32))
                if item.follows(2):
                    pool.wait_ge(x1_out.at(item - 2), x1_out.count(item - 2, 16))
                if item.follows(2):
                    pool.wait_ge(msg_set.at(item - 2), msg_set.count(item - 2))
                if item.follows(2):
                    pool.wait_ge(y_set.at(item - 2), y_set.count(item - 2))
                for j, table in enumerate((k.src_idx, k.dst_idx, k.last_idx)):
                    last = pool.tensor_copy(idx[s][j][:, :], table[:, t])
                last.then_inc(idx_set.at(item), 1)
                pool.wait_ge(idx_set.at(item), idx_set.count(item))
                apart(pool, k)
                pool.indirect_dma_start(out=h2_src[s][:, :], out_offset=None, in_=k.h2_dram[:, :],
                                             in_offset=bass.IndirectOffsetOnAxis(idx[s][0][:, :], 0),
                                             bounds_check=k.N - 1, oob_is_err=True)\
                    .then_inc(src_in.at(item), 16)
                pool.indirect_dma_start(out=x_own[s][:, :], out_offset=None, in_=x[:, :],
                                             in_offset=bass.IndirectOffsetOnAxis(idx[s][1][:, :], 0),
                                             bounds_check=k.N - 1, oob_is_err=True)\
                    .then_inc(src_in.at(item), 16)

            def norm(item):
                s = item.slot(2)
                norm_rstd(pool, k, st[1:4], item, mv[s], ve[s][:, :], rstd[s][:, :])
                pool.wait_ge(x1_set.at(item), x1_set.count(item))
                apart(pool, k)
                pool.indirect_dma_start(out=k.x1_dram[:, :], out_offset=bass.IndirectOffsetOnAxis(idx[s][2][:, :], 0),
                                             in_=y[s][:, 0, :], in_offset=None, bounds_check=k.N - 1,
                                             oob_is_err=False)\
                    .then_inc(x1_out.at(item), 16)

            each_item(pool, T, PER, gather, norm)
            for back in range(2):
                pool.wait_ge(x1_out.at(Item(None, T - 1 - back, PER)), x1_out.count(Item(None, T - 1 - back, PER), 16))

        @block.tensor
        def _(pe):
            def body(item):
                s = item.slot(2)
                pe.wait_ge(msg_set.at(item), msg_set.count(item))
                if not item.follows(1):
                    pe.wait_ge(zero_set[0], 1)
                if item.follows(1):
                    pe.wait_ge(sum_set.at(item - 1), sum_set.count(item - 1))
                pe.matmul(sum_bank[s][:, 0:D + 1], same[s][:, :], msg[s][:, :], start=True, stop=False)
                pe.matmul(sum_bank[s][:, 0:D + 1], carry[s][:, :], sums[(s + 1) % 2][:, :], start=False, stop=True)\
                    .then_inc(sum_ps.at(item), 1)

            each_item(pe, T, PER, body)

        @block.scalar
        def _(act):
            def body(item):
                s = item.slot(2)
                act.wait_ge(sum_ps.at(item), sum_ps.count(item))
                if item.follows(2):
                    act.wait_ge(num_set.at(item - 2), num_set.count(item - 2))
                act.activation(sums[s][:, :], sum_bank[s][:, 0:D + 1], ACT.Copy)\
                    .then_inc(sum_set.at(item), 1)

            each_item(act, T, PER, body)

        @block.vector
        def _(dve):
            dve.memset(sums[1][:, :], 0.0)\
                .then_inc(zero_set.at(Item(None, 0, 1)), 1)

            def front(item):
                s = item.slot(2)
                t = bass.ds(item.index(), 1)
                dve.wait_ge(own_in.at(item), own_in.count(item, 32))
                if item.follows(2):
                    dve.wait_ge(sum_ps.at(item - 2), sum_ps.count(item - 2))
                same_and_carry(dve, item, k, dst_row[s][:, :], same[s][:, :], carry[s][:, :])\
                    .then_inc(same_set.at(item), 1)
                dve.tensor_copy(msg[s][:, D:D + 1], k.p2[:, t])
                dve.wait_ge(src_in.at(item), src_in.count(item, 32))
                dve.tensor_scalar(msg[s][:, 0:D], h2_src[s][:, :], k.p2[:, t], None, ALU.mult)\
                    .then_inc(msg_set.at(item), 1)

            def after(item):
                s = item.slot(2)
                ps_t = k.ps2[:, bass.ds(item.index(), 1)]
                dve.wait_ge(sum_set.at(item), sum_set.count(item))
                if item.follows(2):
                    dve.wait_ge(x1_out.at(item - 2), x1_out.count(item - 2, 16))
                if item.follows(2):
                    dve.wait_ge(copy_out.at(item - 2), copy_out.count(item - 2, 16))
                dve.tensor_tensor(inv[s][:, :], sums[s][:, D:D + 1], ps_t, ALU.add)\
                    .then_inc(den_set.at(item), 1)
                dve.scalar_tensor_tensor(y[s][:, 0, :], fix[s][:, :], ps_t, sums[s][:, 0:D], ALU.mult, ALU.add)\
                    .then_inc(num_set.at(item), 1)
                dve.wait_ge(den_set.at(item), den_set.count(item))
                dve.reciprocal(inv[s][:, :], inv[s][:, :])\
                    .then_inc(inv_set.at(item), 1)
                dve.wait_ge(inv_set.at(item), inv_set.count(item))
                dve.scalar_tensor_tensor(y[s][:, 0, :], y[s][:, 0, :], inv[s][:, 0:1], x_own[s][:, :],
                                              ALU.mult, ALU.add)\
                    .then_inc(y_set.at(item), 1)
                dve.wait_ge(y_set.at(item), y_set.count(item))
                norm_stats(dve, k, (st[0], st[1]), item, y[s], stats[s], mv[s])
                norm_apply(dve, st[3], item, y[s], mv[s], rstd[s], y[s])\
                    .then_inc(x1_set.at(item), 1)

            each_item(dve, T, PER, front, after)


def gine(nc, k, edge_attr, out):
    D, KC, HC, T, E, LAST = k.D, k.KC, k.HC, k.T, k.E, k.LAST
    PER = 2
    ctx, sb, sem = phase(nc, "gine")
    with ctx:
        idx_set, src_in, own_in, same_set = sem("idx_set"), sem("src_in", 2), sem("own_in", 2), sem("same_set")
        edge_set, msg_set, sum_ps, sum_set, zero_set = (
            sem("edge_set"), sem("msg_set"), sem("sum_ps"), sem("sum_set"), sem("zero_set"))
        z_set, z_turned, zt_set, hid_ps, hid_set, mlp_ps = (
            sem("z_set"), sem("z_turned"), sem("zt_set"), sem("hid_ps"), sem("hid_set"), sem("mlp_ps"))
        v_set, a_set, b_set, s_set, o_set, o_out = (
            sem("v_set"), sem("a_set"), sem("b_set"), sem("s_set"), sem("o_set"), sem("o_out", 2))
        st_v = [sem(f"v_{n}") for n in ("st", "mv", "ve", "rstd")]
        st_s = [sem(f"s_{n}") for n in ("st", "mv", "ve", "rstd")]
        idx = [[sb(f"idx{s}{j}", [P, 1], I32) for j in range(2)] for s in range(2)]
        x1_src = [sb(f"x1_src{s}", [P, D]) for s in range(2)]
        attr = [sb(f"attr{s}", [P, D]) for s in range(2)]
        x1_own = [sb(f"x1_own{s}", [P, D]) for s in range(2)]
        x1b = [sb(f"x1b{s}", [P, D]) for s in range(2)]
        dst_row = [sb(f"dst_row{s}", [P, P]) for s in range(2)]
        same = [sb(f"same{s}", [P, P]) for s in range(2)]
        carry = [sb(f"carry{s}", [P, P]) for s in range(2)]
        sums = [sb(f"sums{s}", [P, D]) for s in range(2)]
        z = [sb(f"z{s}", [P, D]) for s in range(2)]
        zt = [sb(f"zt{s}", [P, KC, P]) for s in range(2)]
        hid = [sb(f"hid{s}", [P, KC, P]) for s in range(2)]
        v = [sb(f"v{s}", [P, 1, D]) for s in range(2)]

        def small(n, w):
            return [sb(f"{n}{s}", [P, 1, w]) for s in range(2)]

        v_stats, v_mv, s_stats, s_mv = small("v_stats", 6), small("v_mv", 2), small("s_stats", 6), small("s_mv", 2)
        v_ve, v_rstd, s_ve, s_rstd = ([sb(f"{n}{s}", [P, 1]) for s in range(2)]
                                      for n in ("v_ve", "v_rstd", "s_ve", "s_rstd"))
        sum_bank, turn_bank, hid_bank, mlp_bank = k.psum[0:2], k.psum[2], k.psum[3], k.psum[4]
        block = ctx.enter_context(nc.Block())

        @block.sync
        def _(sp):
            def body(item):
                s = item.slot(2)
                t = bass.ds(item.index(), 1)
                if item.follows(2):
                    sp.wait_ge(same_set.at(item - 2), same_set.count(item - 2))
                if item.follows(2):
                    sp.wait_ge(edge_set.at(item - 2), edge_set.count(item - 2))
                if item.follows(2):
                    sp.wait_ge(v_set.at(item - 2), v_set.count(item - 2))
                if item.follows(2):
                    sp.wait_ge(b_set.at(item - 2), b_set.count(item - 2))
                n = LAST if item.i is None and item.c == T - 1 else P
                sp.dma_start(attr[s][0:n, :], edge_attr[bass.ds(item.index() * P, n), :])\
                    .then_inc(own_in.at(item), 16)
                sp.dma_start(x1_own[s][:, :], k.fix1_dram[t, :, :].rearrange("t p d -> (t p) d"))\
                    .then_inc(own_in.at(item), 16)
                sp.dma_start(dst_row[s][:, :], k.dst_dram[t, :].broadcast_to([P, P]))\
                    .then_inc(own_in.at(item), 16)

            each_item(sp, T, PER, body)

        @block.gpsimd
        def _(pool):
            def gather(item):
                s = item.slot(2)
                t = bass.ds(item.index(), 1)
                if item.follows(2):
                    pool.wait_ge(o_out.at(item - 2), o_out.count(item - 2, 16))
                if item.follows(2):
                    pool.wait_ge(msg_set.at(item - 2), msg_set.count(item - 2))
                if item.follows(2):
                    pool.wait_ge(sum_ps.at(item - 2), sum_ps.count(item - 2))
                pool.tensor_copy(idx[s][0][:, :], k.src_idx[:, t])
                pool.tensor_copy(idx[s][1][:, :], k.last_idx[:, t])\
                    .then_inc(idx_set.at(item), 1)
                pool.wait_ge(idx_set.at(item), idx_set.count(item))
                apart(pool, k)
                pool.indirect_dma_start(out=x1_src[s][:, :], out_offset=None, in_=k.x1_dram[:, :],
                                             in_offset=bass.IndirectOffsetOnAxis(idx[s][0][:, :], 0),
                                             bounds_check=k.N - 1, oob_is_err=True)\
                    .then_inc(src_in.at(item), 16)

            def norms(item):
                s = item.slot(2)
                pool.wait_ge(own_in.at(item), own_in.count(item, 48))
                if item.follows(2):
                    pool.wait_ge(s_set.at(item - 2), s_set.count(item - 2))
                pool.tensor_tensor(x1b[s][:, :], x1_own[s][:, :], k.beta[:, :], ALU.add)\
                    .then_inc(b_set.at(item), 1)
                norm_rstd(pool, k, st_v[1:4], item, v_mv[s], v_ve[s][:, :], v_rstd[s][:, :])
                norm_rstd(pool, k, st_s[1:4], item, s_mv[s], s_ve[s][:, :], s_rstd[s][:, :])
                pool.wait_ge(o_set.at(item), o_set.count(item))
                apart(pool, k)
                pool.indirect_dma_start(out=out[:, :], out_offset=bass.IndirectOffsetOnAxis(idx[s][1][:, :], 0),
                                             in_=v[s][:, 0, :], in_offset=None, bounds_check=k.N - 1,
                                             oob_is_err=False)\
                    .then_inc(o_out.at(item), 16)

            each_item(pool, T, PER, gather, norms)
            for back in range(2):
                pool.wait_ge(o_out.at(Item(None, T - 1 - back, PER)), o_out.count(Item(None, T - 1 - back, PER), 16))

        @block.tensor
        def _(pe):
            def body(item):
                s = item.slot(2)
                pe.wait_ge(msg_set.at(item), msg_set.count(item))
                if not item.follows(1):
                    pe.wait_ge(zero_set[0], 1)
                if item.follows(1):
                    pe.wait_ge(sum_set.at(item - 1), sum_set.count(item - 1))
                pe.matmul(sum_bank[s][:, 0:D], same[s][:, :], x1_src[s][:, :], start=True, stop=False)
                pe.matmul(sum_bank[s][:, 0:D], carry[s][:, :], sums[(s + 1) % 2][:, :], start=False, stop=True)\
                    .then_inc(sum_ps.at(item), 1)

            def mlp(item):
                s = item.slot(2)
                pe.wait_ge(z_set.at(item), z_set.count(item))
                if item.follows(1):
                    pe.wait_ge(zt_set.at(item - 1), zt_set.count(item - 1))
                for c in range(KC):
                    last = pe.transpose(turn_bank[:, c * P:(c + 1) * P], z[s][:, c * P:(c + 1) * P], k.ident[:, :])
                last.then_inc(z_turned.at(item), 1)
                pe.wait_ge(zt_set.at(item), zt_set.count(item))
                if item.follows(1):
                    pe.wait_ge(hid_set.at(item - 1), hid_set.count(item - 1))
                for m in range(KC):
                    to, at = hid_bank[:, m * P:(m + 1) * P], HC + D + m * P
                    pe.matmul(to, k.bias_parts[:, at:at + P], k.ones3[:, 0:P], start=True, stop=False)
                    for c in range(KC):
                        last = pe.matmul(to, k.mw1[:, c, m * P:(m + 1) * P], zt[s][:, c, :], start=False, stop=(c == KC - 1))
                last.then_inc(hid_ps.at(item), 1)
                pe.wait_ge(hid_set.at(item), hid_set.count(item))
                if item.follows(1):
                    pe.wait_ge(v_set.at(item - 1), v_set.count(item - 1))
                pe.matmul(mlp_bank[:, 0:D], k.ones3[:, 0:P], k.bias_parts[:, HC + 2 * D:HC + 3 * D], start=True, stop=False)
                for c in range(KC):
                    last = pe.matmul(mlp_bank[:, 0:D], hid[s][:, c, :], k.mw2[:, c, :], start=False, stop=(c == KC - 1))
                last.then_inc(mlp_ps.at(item), 1)

            each_item(pe, T, PER, body, mlp)

        @block.scalar
        def _(act):
            def front(item):
                s = item.slot(2)
                act.wait_ge(edge_set.at(item), edge_set.count(item))
                act.activation(x1_src[s][:, :], x1_src[s][:, :], ACT.Relu)\
                    .then_inc(msg_set.at(item), 1)
                act.wait_ge(sum_ps.at(item), sum_ps.count(item))
                if item.follows(2):
                    act.wait_ge(z_set.at(item - 2), z_set.count(item - 2))
                act.activation(sums[s][:, :], sum_bank[s][:, 0:D], ACT.Copy)\
                    .then_inc(sum_set.at(item), 1)

            def after(item):
                s = item.slot(2)
                act.wait_ge(z_turned.at(item), z_turned.count(item))
                if item.follows(2):
                    act.wait_ge(hid_ps.at(item - 2), hid_ps.count(item - 2))
                act.activation(zt[s][:, :, :].rearrange("p c e -> p (c e)"), turn_bank[:, 0:D], ACT.Copy)\
                    .then_inc(zt_set.at(item), 1)
                act.wait_ge(hid_ps.at(item), hid_ps.count(item))
                if item.follows(2):
                    act.wait_ge(mlp_ps.at(item - 2), mlp_ps.count(item - 2))
                act.activation(hid[s][:, :, :].rearrange("p c e -> p (c e)"), hid_bank[:, 0:D], ACT.Relu)\
                    .then_inc(hid_set.at(item), 1)

            each_item(act, T, PER, front, after)

        @block.vector
        def _(dve):
            dve.memset(sums[1][:, :], 0.0)\
                .then_inc(zero_set.at(Item(None, 0, 1)), 1)

            def front(item):
                s = item.slot(2)
                dve.wait_ge(own_in.at(item), own_in.count(item, 48))
                if item.follows(2):
                    dve.wait_ge(sum_ps.at(item - 2), sum_ps.count(item - 2))
                same_and_carry(dve, item, k, dst_row[s][:, :], same[s][:, :], carry[s][:, :])\
                    .then_inc(same_set.at(item), 1)
                dve.wait_ge(src_in.at(item), src_in.count(item, 16))
                dve.tensor_tensor(x1_src[s][:, :], x1_src[s][:, :], attr[s][:, :], ALU.add)\
                    .then_inc(edge_set.at(item), 1)

            def after(item):
                s = item.slot(2)
                dve.wait_ge(sum_set.at(item), sum_set.count(item))
                if item.follows(2):
                    dve.wait_ge(z_turned.at(item - 2), z_turned.count(item - 2))
                dve.tensor_tensor(z[s][:, :], sums[s][:, :], x1_own[s][:, :], ALU.add)\
                    .then_inc(z_set.at(item), 1)
                dve.wait_ge(mlp_ps.at(item), mlp_ps.count(item))
                if item.follows(2):
                    dve.wait_ge(o_out.at(item - 2), o_out.count(item - 2, 16))
                dve.scalar_tensor_tensor(v[s][:, 0, :], mlp_bank[:, 0:D], 0.0, x1_own[s][:, :], ALU.max, ALU.add)\
                    .then_inc(v_set.at(item), 1)
                dve.wait_ge(v_set.at(item), v_set.count(item))
                norm_stats(dve, k, (st_v[0], st_v[1]), item, v[s], v_stats[s], v_mv[s])
                dve.wait_ge(st_v[1].at(item), st_v[1].count(item))
                dve.scalar_tensor_tensor(v[s][:, 0, :], v[s][:, 0, :], v_mv[s][:, 0, 0:1], k.gamma[:, :],
                                              ALU.subtract, ALU.mult)\
                    .then_inc(a_set.at(item), 1)
                dve.wait_ge(a_set.at(item), a_set.count(item))
                dve.wait_ge(st_v[3].at(item), st_v[3].count(item))
                dve.wait_ge(b_set.at(item), b_set.count(item))
                dve.scalar_tensor_tensor(v[s][:, 0, :], v[s][:, 0, :], v_rstd[s][:, 0:1], x1b[s][:, :],
                                              ALU.mult, ALU.add)\
                    .then_inc(s_set.at(item), 1)
                dve.wait_ge(s_set.at(item), s_set.count(item))
                norm_stats(dve, k, (st_s[0], st_s[1]), item, v[s], s_stats[s], s_mv[s])
                norm_apply(dve, st_s[3], item, v[s], s_mv[s], s_rstd[s], v[s])\
                    .then_inc(o_set.at(item), 1)

            each_item(dve, T, PER, front, after)


_INS = ["x", "src", "dst", "edge_attr_256", "L0_gnn_ln_w", "L0_gnn_ln_b", "L0_gnn_W1", "L0_gnn_att_src1",
        "L0_gnn_att_dst1", "L0_gnn_b1", "L0_gnn_W2", "L0_gnn_att_src2", "L0_gnn_att_dst2", "L0_gnn_b2",
        "L1_gnn_W1", "L1_gnn_b1", "L1_gnn_W2", "L1_gnn_b2", "L1_gnn_gamma", "L1_gnn_beta"]


def kernel(**inputs):
    import numpy as _np
    import concourse.bacc as _bacc
    from concourse import mybir as _mybir
    from concourse.bass_utils import run_bass_kernel_spmd as _run

    nc = _bacc.Bacc("TRN2", target_bir_lowering=False, num_devices=1)
    arrays, args = {}, []
    for name in _INS:
        a = _np.ascontiguousarray(inputs[name])
        arrays[f"in_{name}"] = a
        args.append(nc.dram_tensor(f"in_{name}", a.shape, _mybir.dt.from_np(a.dtype), kind="ExternalInput").ap())
    args.append(nc.dram_tensor("out_0", arrays["in_x"].shape, _mybir.dt.float32, kind="ExternalOutput").ap())
    build(nc, *args)
    r = _run(nc, [arrays], core_ids=[0])
    return r.results[0]["out_0"]
```

```python
from contextlib import ExitStack

import numpy as np

import concourse.bass as bass
from concourse import mybir

ALU = mybir.AluOpType
ACT = mybir.ActivationFunctionType
F32 = mybir.dt.float32
F32R = mybir.dt.float32r
BF16 = mybir.dt.bfloat16
I32 = mybir.dt.int32
AX_X = mybir.AxisListType.X

P = 128
LN_EPS = 1e-5
NEG_SLOPE = 0.2
NO_NODE = 1 << 20
LOW = -1.0e30


class Item:

    def __init__(self, i, c, per):
        self.i, self.c, self.per = i, c, per

    def index(self, more=0):
        k = self.c + more
        if self.i is None:
            return k
        return self.i * self.per + k if k else self.i * self.per

    def slot(self, ring):
        return self.c % ring

    def uses(self, ring):
        k = self.c // ring + 1
        if self.i is None:
            return k
        base = self.i if self.per == ring else self.i * (self.per // ring)
        return base + k if k else base

    def follows(self, k):
        return self.i is not None or self.c >= k

    def __sub__(self, k):
        return Item(self.i, self.c - k, self.per)


class Ring(list):

    def at(self, item):
        return self[item.slot(len(self))]

    def count(self, item, inc=1):
        n = item.uses(len(self))
        return n if inc == 1 else n * inc


def apart(engine, k):
    engine.sem_inc(k.waits_passed[0], 1)


def done(instruction, sems, item, inc=1):
    instruction.then_inc(sems[item.slot(len(sems))], inc)


def run(engine, steps, per, first, last, step):
    for c in range(min(first, steps)):
        step(None, c)
    if last > first:
        with engine.Fori(first // per, last // per) as i:
            for c in range(per):
                step(i, c)
    for c in range(max(last, first), steps):
        step(None, c)


def each_item(engine, items, per, *stages):

    def step(i, c):
        for lag, stage in enumerate(stages):
            if i is not None or 0 <= c - lag < items:
                stage(Item(i, c - lag, per))

    run(engine, items + len(stages) - 1, per, 2 * per, (items - 1) // per * per, step)


def each_item_lagged(engine, items, per, *stages):
    behind = max(lag for lag, _ in stages)

    def step(i, c):
        for lag, stage in stages:
            if i is not None or 0 <= c - lag < items:
                stage(Item(i, c - lag, per))

    run(engine, items + behind, per, (behind + 2 * per - 1) // per * per, (items - 1) // per * per, step)


class Shared:
    pass


def build(nc, x, src, dst, edge_attr, ln_w, ln_b, g_w1, att_src1, att_dst1, g_b1, g_w2, att_src2,
          att_dst2, g_b2, m_w1, m_b1, m_w2, m_b2, gamma, beta, out):
    N, D = x.shape
    (E,) = src.shape
    H, C = att_src1.shape
    HC = H * C
    KC = D // P
    MC = HC // P
    T = (E + P - 1) // P
    LAST = E - (T - 1) * P
    assert D == 256 and HC == 512 and LAST < P and T <= P

    ctx = ExitStack()
    k = Shared()
    k.N, k.D, k.E, k.H, k.C, k.HC, k.KC, k.MC, k.T, k.LAST = N, D, E, H, C, HC, KC, MC, T, LAST
    with ctx:
        def sb(name, shape, dt=F32):
            return ctx.enter_context(nc.sbuf_tensor(name, shape, dt))

        k.psum = [ctx.enter_context(nc.psum_tensor(f"bank{b}", [P, 512], F32)) for b in range(8)]
        k.ht_dram = nc.dram_tensor("ht_dram", [T, P, 2 * D], F32).ap()
        k.dst_dram = nc.dram_tensor("dst_dram", [T, P], F32).ap()
        k.x_own_dram = nc.dram_tensor("x_own_dram", [T, P, D], F32).ap()
        k.h2_src_dram = nc.dram_tensor("h2_src_dram", [T, P, D], F32).ap()
        k.fix_dram = nc.dram_tensor("fix_dram", [T, P, D], F32).ap()
        k.fix1_dram = nc.dram_tensor("fix1_dram", [T, P, D], F32).ap()
        k.h2_dram = nc.dram_tensor("h2_dram", [N, D], F32).ap()
        k.x1_dram = nc.dram_tensor("x1_dram", [N, D], F32).ap()
        k.ident = sb("ident", [P, P])
        k.half = sb("minus_half", [P, 2])
        k.eps = sb("eps", [P, 2])
        k.waits_passed = [ctx.enter_context(nc.semaphore("waits_passed"))]
        k.w1 = sb("w1", [P, KC, HC])
        k.w2 = sb("w2", [P, MC, D])
        k.mw1 = sb("mw1", [P, KC, D])
        k.mw2 = sb("mw2", [P, KC, D])
        k.w1_p, k.w2_p, k.mw1_p, k.mw2_p = (
            [sb(f"{n}_part{j}", [P, ch, w], F32R) for j in range(2)]
            for n, ch, w in (("w1", KC, HC), ("w2", MC, D), ("mw1", KC, D), ("mw2", KC, D)))
        k.a1 = sb("a1", [P, KC, 2 * H])
        k.a1_const = sb("a1_const", [P, 2 * H])
        k.bias1 = sb("bias1", [P, HC])
        k.bias_parts = sb("bias_parts", [3, HC + 3 * D], BF16)
        k.ones3 = sb("ones3", [3, 2 * P], BF16)
        k.gamma = sb("gamma", [P, D])
        k.beta = sb("beta", [P, D])
        k.att2 = sb("att2", [P, 2, D])
        k.att2_const = sb("att2_const", [P, 1])
        k.src_idx = sb("src_idx", [P, T], I32)
        k.dst_idx = sb("dst_idx", [P, T], I32)
        k.last_idx = sb("last_idx", [P, T], I32)
        k.dst_col = sb("dst_col", [P, T])
        k.prev_col = sb("prev_col", [P, T])
        k.cut_first = sb("cut_first", [T, P])
        k.cut_last = sb("cut_last", [T, P])
        k.is_last = sb("is_last", [T, P])
        k.not_last = sb("not_last", [T, P])
        k.p1 = sb("p1", [P, T, H])
        k.ps1 = sb("ps1", [P, T, H])
        k.p2 = sb("p2", [P, T])
        k.ps2 = sb("ps2", [P, T])
        k.terms2 = sb("terms2", [P, 3, T])
        prepare(nc, k, src, dst, ln_w, ln_b, g_w1, att_src1, att_dst1, g_b1, g_w2, att_src2,
                att_dst2, g_b2, m_w1, m_b1, m_w2, m_b2, gamma, beta)
        with ExitStack() as inner:
            k.terms1 = inner.enter_context(nc.sbuf_tensor("terms1", [P, T, 2, 2 * H], F32))
            gat1_scores(nc, k, x)
            gat1_softmax(nc, k)
        gat1_messages(nc, k)
        dense(nc, k, x, out)
        gat2_replace(nc, k)
        gat2_scores(nc, k)
        gat2_softmax(nc, k)
        gat2_messages(nc, k)
        gine(nc, k, edge_attr, out)


def phase(nc, tag):
    ctx = ExitStack()
    made = []

    def clear():
        nc.clear_and_free_semaphores(made)
        nc.all_engine_barrier()

    ctx.callback(clear)

    def sb(name, shape, dt=F32):
        return ctx.enter_context(nc.sbuf_tensor(f"{tag}_{name}", shape, dt))

    def sem(name, ring=1):
        new = Ring(nc.alloc_semaphore(f"{tag}_{name}_{j}") for j in range(ring))
        made.extend(new)
        return new

    return ctx, sb, sem


def prepare(nc, k, src, dst, ln_w, ln_b, g_w1, att_src1, att_dst1, g_b1, g_w2, att_src2, att_dst2,
            g_b2, m_w1, m_b1, m_w2, m_b2, gamma, beta):
    H, C, HC, D, KC, MC, T, E, LAST = k.H, k.C, k.HC, k.D, k.KC, k.MC, k.T, k.E, k.LAST
    NB = HC + 3 * D
    ctx, sb, sem = phase(nc, "prepare")
    with ctx:
        w_in, tab_in, tab_set = sem("w_in"), sem("tab_in"), sem("tab_set")
        ident_set, ones_set, prev_set = sem("ident_set"), sem("ones_set"), sem("prev_set")
        dv, beta_ps, tr_ps, col_set, parts_in, dst_out = (
            sem("dv_step"), sem("beta_ps"), sem("tr_ps"), sem("col_set"), sem("parts_in"), sem("dst_out"))
        prev_in = sem("prev_in")
        lnw = sb("lnw", [P, KC])
        lnb = sb("lnb", [P, KC])
        lnb_cols = sb("lnb_cols", [P, KC, P])
        att = sb("att", [P, 2, HC])
        prod = sb("prod", [P, HC])
        bias = sb("bias", [1, NB])
        b1row = sb("b1row", [P, HC])
        b2row = sb("b2row", [P, D])
        betaw = sb("betaw", [P, HC])
        rest = sb("rest", [1, NB])
        parts = [sb(f"part{j}", [1, NB], BF16) for j in range(3)]
        rows = sb("rows", [T, 4, P], I32)
        rows_f = sb("rows_f", [T, 4, P])
        idx_f = sb("idx_f", [T, 3, P])
        flag = sb("flag", [T, P])

        block = ctx.enter_context(nc.Block())

        def row(a):
            return a.rearrange("(a n) -> a n", a=1)

        n_w = 18

        @block.sync
        def _(sp):
            with nc.allow_non_contiguous_dma(reason="columns of gains, last rows"):
                loads = [
                    (k.w1[:, :, :], g_w1.rearrange("(c p) n -> p c n", p=P)),
                    (k.w2[:, :, :], g_w2.rearrange("(c p) n -> p c n", p=P)),
                    (k.mw1[:, :, :], m_w1.rearrange("(c p) n -> p c n", p=P)),
                    (k.mw2[:, :, :], m_w2.rearrange("(c p) n -> p c n", p=P)),
                    (lnw[:, :], ln_w.rearrange("(c p) -> p c", p=P)),
                    (lnb[:, :], ln_b.rearrange("(c p) -> p c", p=P)),
                    (att[:, 0, :], att_src1.rearrange("h c -> (h c)").partition_broadcast(P)),
                    (att[:, 1, :], att_dst1.rearrange("h c -> (h c)").partition_broadcast(P)),
                    (b1row[:, :], g_b1.partition_broadcast(P)),
                    (b2row[:, :], g_b2.partition_broadcast(P)),
                    (k.gamma[:, :], gamma.partition_broadcast(P)),
                    (k.beta[:, :], beta.partition_broadcast(P)),
                    (k.att2[:, 0, :], att_src2.rearrange("a c -> (a c)").partition_broadcast(P)),
                    (k.att2[:, 1, :], att_dst2.rearrange("a c -> (a c)").partition_broadcast(P)),
                    (bias[:, HC:HC + D], row(g_b2)),
                    (bias[:, HC + D:HC + 2 * D], row(m_b1)),
                    (bias[:, HC + 2 * D:NB], row(m_b2)),
                ]
                assert len(loads) == n_w - 1
                for to, of in loads:
                    sp.dma_start(to, of).then_inc(w_in[0], 16)
                sp.dma_start(bias[:, 0:HC], row(g_b1)).then_inc(w_in[0], 16)
                sp.wait_ge(tab_set[0], 1)
                full = (T - 1) * P
                tables = [
                    (rows[0:T - 1, 0, :], src[0:full].rearrange("(t e) -> t e", e=P)),
                    (rows[T - 1:T, 0, 0:LAST], row(src[full:E])),
                    (rows[0:T - 1, 1, :], dst[0:full].rearrange("(t e) -> t e", e=P)),
                    (rows[T - 1:T, 1, 0:LAST], row(dst[full:E])),
                    (rows[0:T - 1, 2, :], dst[1:full + 1].rearrange("(t e) -> t e", e=P)),
                    (rows[T - 1:T, 2, 0:LAST - 1], row(dst[full + 1:E])),
                    (rows[0:1, 3, 1:P], row(dst[0:P - 1])),
                    (rows[1:T - 1, 3, :], dst[P - 1:full - 1].rearrange("(t e) -> t e", e=P)),
                    (rows[T - 1:T, 3, 0:LAST + 1], row(dst[full - 1:E])),
                ]
                for to, of in tables:
                    sp.dma_start(to, of).then_inc(tab_in[0], 16)
                sp.wait_ge(dv[0], 1)
                sp.dma_start(k.dst_dram[:, :], rows_f[:, 1, :]).then_inc(dst_out[0], 16)
                sp.wait_ge(dst_out[0], 16)
                sp.wait_ge(prev_set[0], 1)
                sp.dma_start(k.prev_col[P - 1:P, 1:T], k.dst_dram[0:T - 1, P - 1:P].rearrange("t a -> a t"))\
                    .then_inc(prev_in[0], 16)
                sp.wait_ge(prev_in[0], 16)
                sp.wait_ge(col_set[0], 1)
                for j in range(3):
                    sp.dma_start(k.bias_parts[j:j + 1, :], parts[j][:, :]).then_inc(parts_in[0], 16)
                sp.wait_ge(parts_in[0], 48)

        @block.gpsimd
        def _(pool):
            nc.gpsimd.memset(rows[:, 0, :], 0)
            nc.gpsimd.memset(rows[:, 1:3, :], NO_NODE)
            nc.gpsimd.memset(rows[:, 3, :], NO_NODE).then_inc(tab_set[0], 1)
            nc.gpsimd.memset(k.ident[:, :], 0.0).then_inc(ident_set[0], 1)
            pool.wait_ge(ident_set[0], 1)
            nc.gpsimd.affine_select(out=k.ident[:, :], in_=k.ident[:, :], compare_op=ALU.not_equal,
                                    fill=1.0, base=0, pattern=[[-1, P]], channel_multiplier=1)\
                .then_inc(ident_set[0], 1)
            nc.gpsimd.memset(k.half[:, :], -0.5)
            nc.gpsimd.memset(k.eps[:, :], LN_EPS)
            nc.gpsimd.memset(k.ones3[:, :], 1.0).then_inc(ones_set[0], 1)
            nc.gpsimd.memset(k.prev_col[:, :], -1.0).then_inc(prev_set[0], 1)

        @block.vector
        def _(dve):
            v = nc.vector
            n = [0]

            def link(ins):
                n[0] += 1
                ins.then_inc(dv[0], 1)
                dve.wait_ge(dv[0], n[0])

            dve.wait_ge(tab_in[0], 9 * 16)
            link(v.tensor_copy(rows_f[:, :, :], rows[:, :, :]))
            link(v.memset(rows_f[0:1, 3, 0:1], -1.0))
            nodes, after, prev = rows_f[:, 1, :], rows_f[:, 2, :], rows_f[:, 3, :]
            v.tensor_tensor(flag[:, :], nodes, prev, ALU.not_equal)
            v.tensor_tensor(k.is_last[:, :], nodes, after, ALU.not_equal)
            link(v.tensor_tensor(k.not_last[:, :], nodes, after, ALU.is_equal))
            v.tensor_scalar(k.cut_first[:, :], flag[:, :], LOW, None, ALU.mult)
            v.tensor_scalar(k.cut_last[:, :], k.is_last[:, :], LOW, None, ALU.mult)
            v.tensor_copy(idx_f[:, 0, :], rows_f[:, 0, :])
            v.tensor_scalar(idx_f[:, 1, :], nodes, float(k.N), None, ALU.is_lt)
            link(v.tensor_scalar(idx_f[:, 2, :], k.not_last[:, :], float(NO_NODE), None, ALU.mult))
            v.tensor_tensor(idx_f[:, 1, :], idx_f[:, 1, :], nodes, ALU.mult)
            link(v.tensor_tensor(idx_f[:, 2, :], idx_f[:, 2, :], nodes, ALU.add))
            dve.wait_ge(tr_ps[0], 1)
            v.tensor_copy(k.src_idx[:, :], k.psum[0][:, 0:T])
            v.tensor_copy(k.dst_idx[:, :], k.psum[1][:, 0:T])
            v.tensor_copy(k.last_idx[:, :], k.psum[2][:, 0:T])
            link(v.tensor_copy(k.dst_col[:, :], k.psum[3][:, 0:T]))

            dve.wait_ge(w_in[0], n_w * 16)
            for c in range(KC):
                v.tensor_copy(lnb_cols[:, c, :], lnb[:, c:c + 1].broadcast_to([P, P]))
            link(v.tensor_copy(betaw[:, :], b1row[:, :]))
            dve.wait_ge(beta_ps[0], 1)
            link(v.tensor_copy(betaw[:, :], k.psum[4][:, :]))
            v.tensor_tensor(k.bias1[:, :], betaw[:, :], b1row[:, :], ALU.add)
            for c in range(KC):
                link(v.tensor_scalar(k.w1[:, c, :], k.w1[:, c, :], lnw[:, c:c + 1], None, ALU.mult))
            for of, to in ((k.w1, k.w1_p), (k.w2, k.w2_p), (k.mw1, k.mw1_p), (k.mw2, k.mw2_p)):
                link(v.tensor_copy(to[0][:, :, :], of[:, :, :]))
                link(v.tensor_tensor(to[1][:, :, :], of[:, :, :], to[0][:, :, :].bitcast(F32), ALU.subtract))
            for j in range(2):
                for c in range(KC + 1):
                    of = betaw[:, :] if c == KC else k.w1[:, c, :]
                    to = k.a1_const[:, j * H:(j + 1) * H] if c == KC else k.a1[:, c, j * H:(j + 1) * H]
                    link(v.tensor_tensor(prod[:, :], of, att[:, j, :], ALU.mult))
                    link(v.tensor_reduce(to, prod[:, :].rearrange("p (h c) -> p h c", h=H), AX_X, ALU.add))
            link(v.tensor_tensor(prod[:, 0:D], k.att2[:, 0, :], k.att2[:, 1, :], ALU.add))
            link(v.tensor_tensor(prod[:, 0:D], prod[:, 0:D], b2row[:, :], ALU.mult))
            link(v.tensor_reduce(prod[:, D:D + 1], prod[:, 0:D], AX_X, ALU.add))
            link(v.tensor_scalar(k.att2_const[:, :], prod[:, D:D + 1], -1.0, None, ALU.mult))
            link(v.tensor_copy(bias[:, 0:HC], k.bias1[0:1, :]))
            link(v.tensor_copy(parts[0][:, :], bias[:, :]))
            link(v.tensor_tensor(rest[:, :], bias[:, :], parts[0][:, :], ALU.subtract))
            link(v.tensor_copy(parts[1][:, :], rest[:, :]))
            link(v.tensor_tensor(rest[:, :], rest[:, :], parts[1][:, :], ALU.subtract))
            v.tensor_copy(parts[2][:, :], rest[:, :]).then_inc(col_set[0], 1)

        @block.tensor
        def _(pe):
            pe.wait_ge(ident_set[0], 2)
            pe.wait_ge(dv[0], 5)
            for j in range(3):
                nc.tensor.transpose(k.psum[j][:, 0:T], idx_f[:, j, :], k.ident[0:T, 0:T])
            nc.tensor.transpose(k.psum[3][:, 0:T], rows_f[:, 1, :], k.ident[0:T, 0:T]).then_inc(tr_ps[0], 1)
            pe.wait_ge(dv[0], 7)
            for c in range(KC):
                last = nc.tensor.matmul(k.psum[4][:, :], lnb_cols[:, c, :], k.w1[:, c, :],
                                        start=(c == 0), stop=(c == KC - 1))
            last.then_inc(beta_ps[0], 1)


def norm_stats(dve, k, sems, item, data, stats, mv):
    rows = data.shape[1]
    for r in range(rows):
        last = dve.bn_stats(stats[:, r, :], data[:, r, :])
    last.then_inc(sems[0].at(item), 1)
    dve.wait_ge(sems[0].at(item), sems[0].count(item))
    apart(dve, k)
    for r in range(rows):
        last = dve.bn_aggr(mv[:, r, :], stats[:, r, :])
    last.then_inc(sems[1].at(item), 1)


def norm_rstd(pool, k, sems, item, mv, ve, rstd):
    p, rows = ve.shape
    pool.wait_ge(sems[0].at(item), sems[0].count(item))
    pool.tensor_tensor(ve, mv[:, :, 1], k.eps[0:p, 0:rows], ALU.add)\
        .then_inc(sems[1].at(item), 1)
    pool.wait_ge(sems[1].at(item), sems[1].count(item))
    pool.tensor_tensor(rstd, ve, k.half[0:p, 0:rows], ALU.pow)\
        .then_inc(sems[2].at(item), 1)


def norm_shift(dve, sems, item, mv, rstd, shift):
    dve.wait_ge(sems[0].at(item), sems[0].count(item))
    dve.scalar_tensor_tensor(shift, mv[:, :, 0], -1.0, rstd, ALU.mult, ALU.mult)\
        .then_inc(sems[1].at(item), 1)


def norm_on_act(act, shift_set, item, data, rstd, shift, to):
    act.wait_ge(shift_set.at(item), shift_set.count(item))
    for r in range(data.shape[1]):
        last = act.activation(to[:, r, :], data[:, r, :], ACT.Identity, bias=shift[:, r:r + 1],
                              scale=rstd[:, r:r + 1])
    return last


def norm_apply(dve, rstd_done, item, data, mv, rstd, to):
    dve.wait_ge(rstd_done.at(item), rstd_done.count(item))
    for r in range(data.shape[1]):
        last = dve.tensor_scalar(to[:, r, :], data[:, r, :], mv[:, r, 0:1], rstd[:, r:r + 1],
                                 ALU.subtract, ALU.mult)
    return last


def gat1_scores(nc, k, x):
    H, D, KC, T = k.H, k.D, k.KC, k.T
    PER = 4
    ctx, sb, sem = phase(nc, "gat1_scores")
    with ctx:
        idx_set, rows_in = sem("idx_set"), sem("rows_in", PER)
        st_done, mv_done, ve_done, rs_done = sem("st_done"), sem("mv_done"), sem("ve_done"), sem("rs_done")
        normed, turned, ht_set, ht_out, own_out = (
            sem("normed"), sem("turned"), sem("ht_set"), sem("ht_out", PER), sem("own_out", PER))
        prods, terms_set = sem("prods"), sem("terms_set")

        def ring(name, shape, dt=F32):
            return [sb(f"{name}{s}", shape, dt) for s in range(PER)]

        idx = [ring(f"idx_{n}", [P, 1], I32) for n in ("src", "dst")]
        rows, xn = ring("rows", [P, 2, D]), ring("xn", [P, 2, D])
        ht = ring("ht", [P, 2, KC, P])
        stats, mv, ve, rstd = ring("stats", [P, 2, 6]), ring("mv", [P, 2, 2]), ring("ve", [P, 2]), ring("rstd", [P, 2])
        turn_ps = k.psum[0:2]
        prod_ps = k.psum[2:4]
        block = ctx.enter_context(nc.Block())

        @block.gpsimd
        def _(pool):
            def gather(item):
                s = item.slot(PER)
                if item.follows(PER):
                    pool.wait_ge(rows_in.at(item - PER), rows_in.count(item - PER, 32))
                    pool.wait_ge(normed.at(item - PER), normed.count(item - PER))
                    pool.wait_ge(own_out.at(item - PER), own_out.count(item - PER, 16))
                pool.tensor_copy(idx[0][s][:, :], k.src_idx[:, bass.ds(item.index(), 1)])
                pool.tensor_copy(idx[1][s][:, :], k.dst_idx[:, bass.ds(item.index(), 1)])\
                    .then_inc(idx_set.at(item), 1)
                pool.wait_ge(idx_set.at(item), idx_set.count(item))
                apart(pool, k)
                for j in range(2):
                    pool.indirect_dma_start(
                        out=rows[s][:, j, :], out_offset=None, in_=x[:, :],
                        in_offset=bass.IndirectOffsetOnAxis(idx[j][s][:, :], 0),
                        bounds_check=k.N - 1, oob_is_err=True)\
                        .then_inc(rows_in.at(item), 16)

            def norm(item):
                s = item.slot(PER)
                norm_rstd(pool, k, (mv_done, ve_done, rs_done), item, mv[s], ve[s][:, :], rstd[s][:, :])

            each_item_lagged(pool, T, PER, (0, gather), (2, norm))

        @block.vector
        def _(dve):
            def statistics(item):
                s = item.slot(PER)
                dve.wait_ge(rows_in.at(item), rows_in.count(item, 32))
                norm_stats(dve, k, (st_done, mv_done), item, rows[s], stats[s], mv[s])

            def normalise(item):
                s = item.slot(PER)
                if item.follows(PER):
                    dve.wait_ge(turned.at(item - PER), turned.count(item - PER))
                norm_apply(dve, rs_done, item, rows[s], mv[s], rstd[s], xn[s])\
                    .then_inc(normed.at(item), 1)

            def terms(item):
                dve.wait_ge(prods.at(item), prods.count(item))
                to = k.terms1[:, bass.ds(item.index(), 1), :, :].rearrange("p t j h -> p (t j) h")
                const = k.a1_const[:, :].unsqueeze(1).broadcast_to([P, 2, 2 * H])
                dve.tensor_tensor(to, prod_ps[item.slot(2)][:, 0:4 * H].rearrange("p (j h) -> p j h", j=2),
                                  const, ALU.add)\
                    .then_inc(terms_set.at(item), 1)

            each_item_lagged(dve, T, PER, (0, statistics), (1, normalise), (3, terms))

        @block.tensor
        def _(pe):
            def turn(item):
                s, b = item.slot(PER), item.slot(2)
                pe.wait_ge(normed.at(item), normed.count(item))
                if item.follows(2):
                    pe.wait_ge(ht_set.at(item - 2), ht_set.count(item - 2))
                for j in range(2):
                    for c in range(KC):
                        last = pe.transpose(turn_ps[b][:, (j * KC + c) * P:(j * KC + c + 1) * P],
                                            xn[s][:, j, c * P:(c + 1) * P], k.ident[:, :])
                last.then_inc(turned.at(item), 1)

            def products(item):
                s, b = item.slot(PER), item.slot(2)
                pe.wait_ge(ht_set.at(item), ht_set.count(item))
                if item.follows(2):
                    pe.wait_ge(terms_set.at(item - 2), terms_set.count(item - 2))
                for j in range(2):
                    for c in range(KC):
                        last = pe.matmul(prod_ps[b][:, j * 2 * H:(j + 1) * 2 * H], ht[s][:, j, c, :],
                                         k.a1[:, c, :], start=(c == 0), stop=(c == KC - 1))
                last.then_inc(prods.at(item), 1)

            each_item_lagged(pe, T, PER, (0, turn), (1, products))

        @block.scalar
        def _(act):
            def copy_turned(item):
                s, b = item.slot(PER), item.slot(2)
                act.wait_ge(turned.at(item), turned.count(item))
                if item.follows(PER):
                    act.wait_ge(ht_out.at(item - PER), ht_out.count(item - PER, 16))
                    act.wait_ge(prods.at(item - PER), prods.count(item - PER))
                act.activation(ht[s][:, :, :, :].rearrange("p j c e -> p (j c e)"), turn_ps[b][:, :], ACT.Copy)\
                    .then_inc(ht_set.at(item), 1)

            each_item_lagged(act, T, PER, (0, copy_turned))

        @block.sync
        def _(sp):
            def store_own(item):
                sp.wait_ge(rows_in.at(item), rows_in.count(item, 32))
                sp.dma_start(k.x_own_dram[bass.ds(item.index(), 1), :, :].rearrange("t p d -> (t p) d"),
                             rows[item.slot(PER)][:, 1, :])\
                    .then_inc(own_out.at(item), 16)

            def store_turned(item):
                s = item.slot(PER)
                sp.wait_ge(ht_set.at(item), ht_set.count(item))
                sp.dma_start(k.ht_dram[bass.ds(item.index(), 1), :, :].rearrange("t p n -> (t p) n"),
                             ht[s][:, :, :, :].rearrange("p j c e -> p (j c e)"))\
                    .then_inc(ht_out.at(item), 16)

            each_item_lagged(sp, T, PER, (2, store_turned), (0, store_own))
            for back in range(PER):
                end = Item(None, T - 1 - back, PER)
                sp.wait_ge(ht_out.at(end), ht_out.count(end, 16))
                sp.wait_ge(own_out.at(end), own_out.count(end, 16))


class Link:

    def __init__(self, dve, sem):
        self.dve, self.sem, self.n = dve, sem, 0

    def __call__(self, ins):
        self.n += 1
        ins.then_inc(self.sem[0], 1)
        self.dve.wait_ge(self.sem[0], self.n)


class Segments:

    def __init__(self, k, lines, sb, sem, ps_tile, ps_back):
        T = k.T
        self.k, self.lines, self.ps_tile, self.ps_back = k, lines, ps_tile, ps_back
        self.ends_set, self.ends_turned = sem("ends_set"), sem("ends_turned")
        self.carry_set, self.carry_turned = sem("carry_set"), sem("carry_turned")
        self.ends = sb("ends", [T, 2, lines])
        self.cut_t = sb("cut_t", [lines, T])
        self.carry_t = sb("carry_t", [lines, T + 1])
        self.low = sb("low", [T, 1])
        self.carry = sb("carry", [T, lines])
        self.scans = 0

    def scan(self, dve, link, cut, values, into, ops, start, back):
        T, lines = self.k.T, self.lines
        self.scans += 1

        def way(ap):
            return ap[:, ::-1] if back else ap

        for h in range(lines):
            last = dve.tensor_tensor_scan(way(into[:, h, :]), way(cut), way(values[:, h, :]), start, *ops)
        dve.tensor_reduce(self.low[:, :], cut, AX_X, ALU.min)
        link(dve.memset(self.carry_t[:, :], start))
        dve.tensor_copy(self.ends[:, 0, :], into[:, :, 0 if back else P - 1])
        dve.tensor_copy(self.ends[:, 1, :], self.low[:, 0:1].broadcast_to([T, lines])).then_inc(self.ends_set[0], 1)
        dve.wait_ge(self.ends_turned[0], self.scans)
        link(dve.tensor_copy(self.cut_t[:, :], self.ps_tile[0:lines, P:P + T]))
        to = self.carry_t[:, 0:T] if back else self.carry_t[:, 1:T + 1]
        dve.tensor_tensor_scan(way(to), way(self.cut_t[:, :]), way(self.ps_tile[0:lines, 0:T]), start, *ops)\
            .then_inc(self.carry_set[0], 1)
        dve.wait_ge(self.carry_turned[0], self.scans)
        link(dve.tensor_copy(self.carry[:, :], self.ps_back[0:T, 0:lines]))
        for h in range(lines):
            last = dve.tensor_tensor_scan(way(into[:, h, :]), way(cut), way(values[:, h, :]),
                                          self.carry[:, h:h + 1], *ops)
        link(last)

    def turn(self, pe, scans, backs):
        k, T, lines = self.k, self.k.T, self.lines
        for n in range(scans):
            pe.wait_ge(self.ends_set[0], n + 1)
            pe.transpose(self.ps_tile[0:lines, 0:T], self.ends[:, 0, :], k.ident[0:T, 0:T])
            pe.transpose(self.ps_tile[0:lines, P:P + T], self.ends[:, 1, :], k.ident[0:T, 0:T])\
                .then_inc(self.ends_turned[0], 1)
            pe.wait_ge(self.carry_set[0], n + 1)
            of = self.carry_t[:, 1:T + 1] if backs[n] else self.carry_t[:, 0:T]
            pe.transpose(self.ps_back[0:T, 0:lines], of, k.ident[0:lines, 0:lines])\
                .then_inc(self.carry_turned[0], 1)


def gat1_softmax(nc, k):
    H, T = k.H, k.T
    HB = 4
    ctx, sb, sem = phase(nc, "gat1_softmax")
    with ctx:
        link_sem, raw_set, raw_turned = sem("link"), sem("raw_set"), sem("raw_turned")
        maxima_turned, shifted, exps_set = sem("maxima_turned"), sem("shifted"), sem("exps_set")
        raw = sb("raw", [P, 2, H, T])
        scores, run_max, maxima = (sb(n, [T, H, P]) for n in ("scores", "run_max", "maxima"))
        top = sb("top", [P, H, T])
        seg = Segments(k, H, sb, sem, k.psum[2], k.psum[3])
        block = ctx.enter_context(nc.Block())

        @block.vector
        def _(dve):
            link = Link(dve, link_sem)
            for j in range(2):
                last = dve.tensor_tensor(raw[:, j, :, :], k.terms1[:, :, j, 0:H].rearrange("p t h -> p h t"),
                                         k.terms1[:, :, 1, H:2 * H].rearrange("p t h -> p h t"), ALU.add)
            link(last)
            flat = raw[:, :, :, :].rearrange("p j h t -> p (j h t)")
            dve.scalar_tensor_tensor(flat, flat, NEG_SLOPE, flat, ALU.mult, ALU.max).then_inc(raw_set[0], 1)
            dve.wait_ge(raw_turned[0], 1)
            for b in range(H // HB):
                last = dve.tensor_copy(scores[:, HB * b:HB * (b + 1), :].rearrange("t h e -> t (h e)"),
                                       k.psum[b][0:T, :])
            link(last)
            seg.scan(dve, link, k.cut_first[:, :], scores, run_max, (ALU.add, ALU.max), LOW, False)
            seg.scan(dve, link, k.cut_last[:, :], run_max, maxima, (ALU.add, ALU.max), LOW, True)
            dve.wait_ge(maxima_turned[0], 1)
            for b in range(H // HB):
                of = k.psum[4 + b][:, :].rearrange("p (h e) -> p h e", h=HB)[:, :, 0:T]
                last = dve.tensor_tensor(top[:, HB * b:HB * (b + 1), :], of, raw[:, 1, HB * b:HB * (b + 1), :], ALU.max)
            link(last)
            for j in range(2):
                last = dve.tensor_tensor(raw[:, j, :, :], raw[:, j, :, :], top[:, :, :], ALU.subtract)
            last.then_inc(shifted[0], 1)

        @block.tensor
        def _(pe):
            pe.wait_ge(raw_set[0], 1)
            for h in range(H):
                last = pe.transpose(k.psum[h // HB][0:T, h % HB * P:(h % HB + 1) * P], raw[:, 0, h, :], k.ident[:, :])
            last.then_inc(raw_turned[0], 1)
            seg.turn(pe, 2, (False, True))
            pe.wait_ge(link_sem[0], 2 + 2 * 4)
            for h in range(H):
                last = pe.transpose(k.psum[4 + h // HB][:, h % HB * P:h % HB * P + T], maxima[:, h, :], k.ident[0:T, 0:T])
            last.then_inc(maxima_turned[0], 1)

        @block.scalar
        def _(act):
            act.wait_ge(shifted[0], 1)
            for to, j in ((k.p1, 0), (k.ps1, 1)):
                act.activation(to[:, :, :].rearrange("p t h -> p h t"), raw[:, j, :, :], ACT.Exp).then_inc(exps_set[0], 1)
            act.wait_ge(exps_set[0], 2)


def same_and_carry(dve, item, k, dst_row, same, carry):
    at = bass.ds(item.index(), 1)
    dve.tensor_scalar(same, dst_row, k.dst_col[:, at], None, ALU.is_equal)
    return dve.tensor_scalar(carry, dst_row, k.prev_col[:, at], None, ALU.is_equal)


def gat1_messages(nc, k):
    H, C, HC, D, KC, MC, T = k.H, k.C, k.HC, k.D, k.KC, k.MC, k.T
    PER = 4
    ctx, sb, sem = phase(nc, "gat1_messages")
    with ctx:
        ht_in, same_set, ht_hi_set, ht_lo_set = sem("ht_in", PER), sem("same_set"), sem("ht_hi_set"), sem("ht_lo_set")
        h_ps, msg_set, msg_hi_set, msg_lo_set, own_set = (
            sem("h_ps"), sem("msg_set"), sem("msg_hi_set"), sem("msg_lo_set"), sem("own_set"))
        sum_ps, sum_set, inv_set, zero_set, den_set = (
            sem("sum_ps"), sem("sum_set"), sem("inv_set"), sem("zero_set"), sem("den_set"))
        whole_set, scaled, y_set, exp_set, neg_set, elu_set = (
            sem("whole_set"), sem("scaled"), sem("y_set"), sem("exp_set"), sem("neg_set"), sem("elu_set"))
        turned, et_hi_set, et_lo_set, fix_ps, fix_set, fix_out = (
            sem("turned"), sem("et_hi_set"), sem("et_lo_set"), sem("fix_ps"), sem("fix_set"), sem("fix_out", PER))

        def ring(name, shape, dt=F32):
            return [sb(f"{name}{s}", shape, dt) for s in range(PER)]

        ht = ring("ht", [P, 2, KC, P])
        ht_hi, ht_lo = (ring(n, [P, 2, KC, P], F32R) for n in ("ht_hi", "ht_lo"))
        dst_row = ring("dst_row", [P, P])
        same, carry = (ring(n, [P, P], F32R) for n in ("same", "carry"))
        msg, sums = ring("msg", [P, HC + H]), ring("sums", [P, HC + H])
        msg_hi, msg_lo = (ring(n, [P, HC], F32R) for n in ("msg_hi", "msg_lo"))
        inv, y, neg = ring("inv", [P, H]), ring("y", [P, HC]), ring("neg", [P, HC])
        et_hi, et_lo = (ring(n, [P, MC, P], F32R) for n in ("et_hi", "et_lo"))
        fix = ring("fix", [P, D])
        src_ps, dst_ps, psum_ps, turn_ps = k.psum[0:4]
        msum_ps, w2_ps = k.psum[4:6], k.psum[6:8]
        block = ctx.enter_context(nc.Block())

        def heads(ap):
            return ap.rearrange("p (h c) -> p h c", h=H)

        def per_head(ap):
            return ap.unsqueeze(2).broadcast_to([P, H, C])

        @block.sync
        def _(sp):
            def load(item):
                s = item.slot(PER)
                if item.follows(PER):
                    sp.wait_ge(ht_hi_set.at(item - PER), ht_hi_set.count(item - PER))
                    sp.wait_ge(ht_lo_set.at(item - PER), ht_lo_set.count(item - PER))
                    sp.wait_ge(same_set.at(item - PER), same_set.count(item - PER))
                t = bass.ds(item.index(), 1)
                sp.dma_start(ht[s][:, :, :, :].rearrange("p j c e -> p (j c e)"),
                             k.ht_dram[t, :, :].rearrange("t p n -> (t p) n"))\
                    .then_inc(ht_in.at(item), 16)
                sp.dma_start(dst_row[s][:, :], k.dst_dram[t, :].broadcast_to([P, P]))\
                    .then_inc(ht_in.at(item), 16)

            def store(item):
                sp.wait_ge(fix_set.at(item), fix_set.count(item))
                sp.dma_start(k.fix_dram[bass.ds(item.index(), 1), :, :].rearrange("t p d -> (t p) d"),
                             fix[item.slot(PER)][:, :])\
                    .then_inc(fix_out.at(item), 16)

            each_item_lagged(sp, T, PER, (0, load), (7, store))
            for back in range(PER):
                sp.wait_ge(fix_out.at(Item(None, T - 1 - back, PER)), fix_out.count(Item(None, T - 1 - back, PER), 16))

        @block.tensor
        def _(pe):
            def turn(item):
                s = item.slot(PER)
                pe.wait_ge(elu_set.at(item), elu_set.count(item))
                if item.follows(1):
                    pe.wait_ge(et_hi_set.at(item - 1), et_hi_set.count(item - 1))
                    pe.wait_ge(et_lo_set.at(item - 1), et_lo_set.count(item - 1))
                for m in range(MC):
                    last = pe.transpose(turn_ps[:, m * P:(m + 1) * P], y[s][:, m * P:(m + 1) * P], k.ident[:, :])
                last.then_inc(turned.at(item), 1)

            def hidden(item):
                s = item.slot(PER)
                pe.wait_ge(ht_hi_set.at(item), ht_hi_set.count(item))
                pe.wait_ge(ht_lo_set.at(item), ht_lo_set.count(item))
                if item.follows(1):
                    pe.wait_ge(own_set.at(item - 1), own_set.count(item - 1))
                for j, ps in enumerate((src_ps, dst_ps)):
                    for c in range(KC):
                        pe.matmul(ps[:, :], ht_hi[s][:, j, c, :], k.w1_p[0][:, c, :], start=(c == 0), stop=False)
                        pe.matmul(ps[:, :], ht_hi[s][:, j, c, :], k.w1_p[1][:, c, :], start=False, stop=False)
                        last = pe.matmul(ps[:, :], ht_lo[s][:, j, c, :], k.w1_p[0][:, c, :], start=False,
                                         stop=(c == KC - 1))
                last.then_inc(h_ps.at(item), 1)

            def sum_up(item):
                s = item.slot(PER)
                before = sums[(s + PER - 1) % PER]
                to = msum_ps[item.slot(2)][:, :]
                pe.wait_ge(msg_hi_set.at(item), msg_hi_set.count(item))
                pe.wait_ge(msg_lo_set.at(item), msg_lo_set.count(item))
                if item.follows(2):
                    pe.wait_ge(sum_set.at(item - 2), sum_set.count(item - 2))
                pe.matmul(to, same[s][:, :], msg_hi[s][:, :], start=True, stop=False)
                pe.matmul(to, same[s][:, :], msg_lo[s][:, :], start=False, stop=False)
                if not item.follows(1):
                    pe.wait_ge(zero_set[0], 1)
                if item.follows(1):
                    pe.wait_ge(sum_set.at(item - 1), sum_set.count(item - 1))
                pe.matmul(to, carry[s][:, :].bitcast(F32), before[:, 0:HC], start=False, stop=True)
                pe.matmul(psum_ps[:, 0:H], same[s][:, :].bitcast(F32), msg[s][:, HC:HC + H], start=True, stop=False)
                pe.matmul(psum_ps[:, 0:H], carry[s][:, :].bitcast(F32), before[:, HC:HC + H], start=False, stop=True)\
                    .then_inc(sum_ps.at(item), 1)

            def second(item):
                s = item.slot(PER)
                to = w2_ps[item.slot(2)][:, 0:D]
                pe.wait_ge(et_hi_set.at(item), et_hi_set.count(item))
                pe.wait_ge(et_lo_set.at(item), et_lo_set.count(item))
                if item.follows(2):
                    pe.wait_ge(fix_set.at(item - 2), fix_set.count(item - 2))
                pe.matmul(to, k.ones3[:, 0:P], k.bias_parts[:, HC:HC + D], start=True, stop=False)
                for m in range(MC):
                    pe.matmul(to, et_hi[s][:, m, :], k.w2_p[0][:, m, :], start=False, stop=False)
                    pe.matmul(to, et_hi[s][:, m, :], k.w2_p[1][:, m, :], start=False, stop=False)
                    last = pe.matmul(to, et_lo[s][:, m, :], k.w2_p[0][:, m, :], start=False, stop=(m == MC - 1))
                last.then_inc(fix_ps.at(item), 1)

            each_item_lagged(pe, T, PER, (3, turn), (0, hidden), (3, second), (1, sum_up))

        @block.vector
        def _(dve):
            dve.memset(sums[PER - 1][:, :], 0.0)\
                .then_inc(zero_set.at(Item(None, 0, 1)), 1)

            def divide(item):
                s = item.slot(PER)
                ps_t = k.ps1[:, bass.ds(item.index(), 1), :].rearrange("p t h -> p (t h)")
                dve.wait_ge(sum_set.at(item), sum_set.count(item))
                dve.tensor_tensor(inv[s][:, :], sums[s][:, HC:HC + H], ps_t, ALU.add)\
                    .then_inc(den_set.at(item), 1)
                dve.tensor_tensor(y[s][:, :], y[s][:, :], sums[s][:, 0:HC], ALU.add)\
                    .then_inc(whole_set.at(item), 1)
                dve.wait_ge(den_set.at(item), den_set.count(item))
                dve.reciprocal(inv[s][:, :], inv[s][:, :])\
                    .then_inc(inv_set.at(item), 1)
                dve.wait_ge(whole_set.at(item), whole_set.count(item))
                dve.wait_ge(inv_set.at(item), inv_set.count(item))
                dve.tensor_tensor(heads(y[s][:, :]), heads(y[s][:, :]), per_head(inv[s][:, :]), ALU.mult)\
                    .then_inc(scaled.at(item), 1)
                dve.wait_ge(scaled.at(item), scaled.count(item))
                dve.tensor_tensor(y[s][:, :], y[s][:, :], k.bias1[:, :], ALU.add)\
                    .then_inc(y_set.at(item), 1)

            def lo_of_elu(item):
                s = item.slot(PER)
                dve.wait_ge(et_hi_set.at(item), et_hi_set.count(item))
                if item.follows(PER):
                    dve.wait_ge(fix_ps.at(item - PER), fix_ps.count(item - PER))
                dve.tensor_tensor(et_lo[s][:, :, :].rearrange("p m e -> p (m e)"), turn_ps[:, :],
                                  et_hi[s][:, :, :].rearrange("p m e -> p (m e)").bitcast(F32), ALU.subtract)\
                    .then_inc(et_lo_set.at(item), 1)

            def messages(item):
                s = item.slot(PER)
                t = bass.ds(item.index(), 1)
                p_t = k.p1[:, t, :].rearrange("p t h -> p (t h)")
                ps_t = k.ps1[:, t, :].rearrange("p t h -> p (t h)")
                dve.wait_ge(ht_in.at(item), ht_in.count(item, 32))
                if item.follows(PER):
                    dve.wait_ge(sum_ps.at(item - PER), sum_ps.count(item - PER))
                same_and_carry(dve, item, k, dst_row[s][:, :], same[s][:, :], carry[s][:, :])\
                    .then_inc(same_set.at(item), 1)
                dve.tensor_copy(msg[s][:, HC:HC + H], p_t)
                dve.wait_ge(h_ps.at(item), h_ps.count(item))
                dve.tensor_tensor(heads(msg[s][:, 0:HC]), heads(src_ps[:, :]), per_head(p_t), ALU.mult)\
                    .then_inc(msg_set.at(item), 1)
                if item.follows(PER):
                    dve.wait_ge(turned.at(item - PER), turned.count(item - PER))
                dve.tensor_tensor(heads(y[s][:, :]), heads(dst_ps[:, :]), per_head(ps_t), ALU.mult)\
                    .then_inc(own_set.at(item), 1)

            def elu(item):
                s = item.slot(PER)
                dve.wait_ge(neg_set.at(item), neg_set.count(item))
                dve.scalar_tensor_tensor(y[s][:, :], neg[s][:, :], -1.0, y[s][:, :], ALU.mult, ALU.max)\
                    .then_inc(elu_set.at(item), 1)

            each_item_lagged(dve, T, PER, (2, divide), (3, lo_of_elu), (0, messages), (2, elu))

        @block.gpsimd
        def _(pool):
            def lo_of_rows(item):
                s = item.slot(PER)
                pool.wait_ge(ht_hi_set.at(item), ht_hi_set.count(item))
                if item.follows(PER):
                    pool.wait_ge(h_ps.at(item - PER), h_ps.count(item - PER))
                pool.tensor_tensor(ht_lo[s][:, :, :, :], ht[s][:, :, :, :], ht_hi[s][:, :, :, :].bitcast(F32),
                                   ALU.subtract).then_inc(ht_lo_set.at(item), 1)

            def lo_of_messages(item):
                s = item.slot(PER)
                pool.wait_ge(msg_hi_set.at(item), msg_hi_set.count(item))
                if item.follows(PER):
                    pool.wait_ge(sum_ps.at(item - PER), sum_ps.count(item - PER))
                pool.tensor_tensor(msg_lo[s][:, :], msg[s][:, 0:HC], msg_hi[s][:, :].bitcast(F32), ALU.subtract)\
                    .then_inc(msg_lo_set.at(item), 1)

            each_item_lagged(pool, T, PER, (0, lo_of_rows), (1, lo_of_messages))

        @block.scalar
        def _(act):
            def hi_of_rows(item):
                s = item.slot(PER)
                act.wait_ge(ht_in.at(item), ht_in.count(item, 32))
                if item.follows(PER):
                    act.wait_ge(h_ps.at(item - PER), h_ps.count(item - PER))
                act.activation(ht_hi[s][:, :, :, :], ht[s][:, :, :, :], ACT.Copy)\
                    .then_inc(ht_hi_set.at(item), 1)

            def copy_sums(item):
                s = item.slot(PER)
                act.wait_ge(sum_ps.at(item), sum_ps.count(item))
                if item.follows(PER):
                    act.wait_ge(whole_set.at(item - PER), whole_set.count(item - PER))
                act.activation(sums[s][:, 0:HC], msum_ps[item.slot(2)][:, :], ACT.Copy)
                act.activation(sums[s][:, HC:HC + H], psum_ps[:, 0:H], ACT.Copy)\
                    .then_inc(sum_set.at(item), 1)

            def hi_of_elu(item):
                s = item.slot(PER)
                act.wait_ge(turned.at(item), turned.count(item))
                if item.follows(PER):
                    act.wait_ge(fix_ps.at(item - PER), fix_ps.count(item - PER))
                act.activation(et_hi[s][:, :, :].rearrange("p m e -> p (m e)"), turn_ps[:, :], ACT.Copy)\
                    .then_inc(et_hi_set.at(item), 1)

            def negative(item):
                s = item.slot(PER)
                act.wait_ge(y_set.at(item), y_set.count(item))
                if item.follows(PER):
                    act.wait_ge(elu_set.at(item - PER), elu_set.count(item - PER))
                act.activation(neg[s][:, :], y[s][:, :], ACT.Exp)\
                    .then_inc(exp_set.at(item), 1)
                act.wait_ge(exp_set.at(item), exp_set.count(item))
                act.activation(neg[s][:, :], neg[s][:, :], ACT.Relu, bias=1.0, scale=-1.0)\
                    .then_inc(neg_set.at(item), 1)

            def hi_of_messages(item):
                s = item.slot(PER)
                act.wait_ge(msg_set.at(item), msg_set.count(item))
                if item.follows(PER):
                    act.wait_ge(sum_ps.at(item - PER), sum_ps.count(item - PER))
                act.activation(msg_hi[s][:, :], msg[s][:, 0:HC], ACT.Copy)\
                    .then_inc(msg_hi_set.at(item), 1)

            def copy_fix(item):
                s = item.slot(PER)
                act.wait_ge(fix_ps.at(item), fix_ps.count(item))
                if item.follows(PER):
                    act.wait_ge(fix_out.at(item - PER), fix_out.count(item - PER, 16))
                act.activation(fix[s][:, :], w2_ps[item.slot(2)][:, 0:D], ACT.Copy)\
                    .then_inc(fix_set.at(item), 1)

            each_item_lagged(act, T, PER, (3, copy_sums), (4, hi_of_elu), (0, hi_of_rows), (3, negative),
                             (1, hi_of_messages), (4, copy_fix))


def dense(nc, k, x, out):
    N, D, HC, KC, MC = k.N, k.D, k.HC, k.KC, k.MC
    PER = 3
    R = 2
    G = R * P
    full = N // G
    rest = (N - full * G) // R
    groups = full + 1
    MH = MC // 2
    assert rest * R == N - full * G and 0 < rest < P and full % PER == 0
    ctx, sb, sem = phase(nc, "dense")
    with ctx:
        x_in = sem("x_in", PER)
        st = {n: tuple(sem(f"{n}_{m}") for m in ("st", "mv", "ve", "rstd", "shift")) for n in "xyvs"}
        xn_set, xn_turned, xt_hi_set, xt_set = sem("xn_set"), sem("xn_turned"), sem("xt_hi_set"), sem("xt_set")
        h_ps, exp_set, neg_set, elu_set, elu_hi_set, elu_lo_set = (
            [sem(f"{n}{j}") for j in range(2)]
            for n in ("h_ps", "exp_set", "neg_set", "elu_set", "elu_hi_set", "elu_lo_set"))
        h2_ps, h2_set, y_set, h2_out = sem("h2_ps"), sem("h2_set"), sem("y_set"), sem("h2_out", PER)
        x1_set, x1_out, x1_turned, zt_hi_set, zt_set, x1b_set = (
            sem("x1_set"), sem("x1_out", PER), sem("x1_turned"), sem("zt_hi_set"), sem("zt_set"), sem("x1b_set"))
        hid_ps, hid_hi_set, hid_set, mlp_ps, v_set, a_set, s_set, o_set, o_out = (
            sem("hid_ps"), sem("hid_hi_set"), sem("hid_set"), sem("mlp_ps"), sem("v_set"), sem("a_set"),
            sem("s_set"), sem("o_set"), sem("o_out", PER))

        def ring(name, shape, dt=F32):
            return [sb(f"{name}{s}", shape, dt) for s in range(PER)]

        xs, xn, y, x1b, v, h2 = (ring(n, [P, R, D]) for n in ("x", "xn", "y", "x1b", "v", "h2"))
        xt_hi, xt_lo, zt_hi, zt_lo, hid_hi, hid_lo = (
            ring(n, [P, KC, R, P], F32R) for n in ("xt_hi", "xt_lo", "zt_hi", "zt_lo", "hid_hi", "hid_lo"))
        elu = ring("elu", [P, MC, R, P])
        elu_hi, elu_lo = (ring(n, [P, MC, R, P], F32R) for n in ("elu_hi", "elu_lo"))
        stats = {n: ring(f"{n}_stats", [P, R, 6]) for n in "xyvs"}
        mv = {n: ring(f"{n}_mv", [P, R, 2]) for n in "xyvs"}
        ve, rstd, shift = ({n: ring(f"{n}_{m}", [P, R]) for n in "xyvs"} for m in ("ve", "rstd", "shift"))
        xt_ps, zt_ps, h2_bank, hid_bank, mlp_bank = k.psum[0], k.psum[1], k.psum[4], k.psum[5], k.psum[6]
        h_bank = k.psum[2:4]
        block = ctx.enter_context(nc.Block())

        def in_group(i, c, stage):
            g = c - stage
            if i is None and not 0 <= g < groups:
                return None, 0
            return Item(i, g, PER), rest if i is None and g == full else P

        def steps(engine, step):
            run(engine, groups + 2, PER, 2 * PER, (full - 1) // PER * PER, step)

        def rows(a, item, p):
            return a[bass.ds(item.index() * G, R * p), :].rearrange("(p r) d -> p r d", r=R)

        def flat(a, p):
            return a[0:p, :, :].rearrange("p r d -> p (r d)")

        def turned(bank, chunks):
            return bank[:, :].rearrange("q (m r p) -> q m r p", m=chunks, r=R)

        @block.sync
        def _(sp):
            def load(item, p):
                if item.follows(PER):
                    sp.wait_ge(y_set.at(item - PER), y_set.count(item - PER))
                sp.dma_start(xs[item.slot(PER)][0:p, :, :], rows(x, item, p)).then_inc(x_in.at(item), 16)

            def step(i, c):
                if i is None and c == 0:
                    load(Item(None, 0, PER), P)
                    load(Item(None, 1, PER), P)
                item, p = in_group(i, c, -2)
                if item is not None:
                    load(item, p)
                item, p = in_group(i, c, 1)
                if item is not None:
                    sp.wait_ge(x1_set.at(item), x1_set.count(item))
                    sp.dma_start(rows(k.x1_dram, item, p), y[item.slot(PER)][0:p, :, :]).then_inc(x1_out.at(item), 16)
                item, p = in_group(i, c, 0)
                if item is not None:
                    sp.wait_ge(h2_set.at(item), h2_set.count(item))
                    sp.dma_start(rows(k.h2_dram, item, p), h2[item.slot(PER)][0:p, :, :]).then_inc(h2_out.at(item), 16)
                item, p = in_group(i, c, 2)
                if item is not None:
                    sp.wait_ge(o_set.at(item), o_set.count(item))
                    sp.dma_start(rows(out, item, p), v[item.slot(PER)][0:p, :, :]).then_inc(o_out.at(item), 16)

            steps(sp, step)
            for back in range(PER):
                last = Item(None, groups - 1 - back, PER)
                sp.wait_ge(h2_out.at(last), h2_out.count(last, 16))
                sp.wait_ge(x1_out.at(last), x1_out.count(last, 16))
                sp.wait_ge(o_out.at(last), o_out.count(last, 16))

        @block.tensor
        def _(pe):
            def turn(of, ps, p):
                for r in range(R):
                    for c in range(KC):
                        at = (c * R + r) * P
                        last = pe.transpose(ps[:, at:at + p], of[0:p, r, c * P:(c + 1) * P], k.ident[0:p, 0:p])
                return last

            def turn_x(item, p):
                pe.wait_ge(xn_set.at(item), xn_set.count(item))
                if item.follows(1):
                    pe.wait_ge(xt_set.at(item - 1), xt_set.count(item - 1))
                turn(xn[item.slot(PER)], xt_ps, p).then_inc(xn_turned.at(item), 1)

            def turn_x1(item, p):
                pe.wait_ge(x1_set.at(item), x1_set.count(item))
                if item.follows(1):
                    pe.wait_ge(zt_set.at(item - 1), zt_set.count(item - 1))
                turn(y[item.slot(PER)], zt_ps, p).then_inc(x1_turned.at(item), 1)

            def channels(bank, chunks, at, bias_at, w, hi, lo):
                for m in range(chunks):
                    to = bank[:, m * G:(m + 1) * G]
                    ch = slice(at + m * P, at + (m + 1) * P)
                    pe.matmul(to, k.bias_parts[:, bias_at + m * P:bias_at + (m + 1) * P], k.ones3[:, :],
                              start=True, stop=False)
                    for c in range(KC):
                        x_hi, x_lo = (t[:, c, :, :].rearrange("q r p -> q (r p)") for t in (hi, lo))
                        pe.matmul(to, w[0][:, c, ch], x_hi, start=False, stop=False)
                        pe.matmul(to, w[0][:, c, ch], x_lo, start=False, stop=False)
                        last = pe.matmul(to, w[1][:, c, ch], x_hi, start=False, stop=(c == KC - 1))
                return last

            def gat1_half(item, j):
                s = item.slot(PER)
                pe.wait_ge(xt_set.at(item), xt_set.count(item))
                if item.follows(1):
                    pe.wait_ge(elu_set[j].at(item - 1), elu_set[j].count(item - 1))
                channels(h_bank[j], MH, j * MH * P, j * MH * P, k.w1_p, xt_hi[s], xt_lo[s])\
                    .then_inc(h_ps[j].at(item), 1)

            def mlp_hidden(item):
                s = item.slot(PER)
                pe.wait_ge(zt_set.at(item), zt_set.count(item))
                if item.follows(1):
                    pe.wait_ge(hid_set.at(item - 1), hid_set.count(item - 1))
                channels(hid_bank, KC, 0, HC + D, k.mw1_p, zt_hi[s], zt_lo[s]).then_inc(hid_ps.at(item), 1)

            def nodes(bank, chunks, hi, lo, w, ends):
                for r in range(R):
                    to = bank[:, r * D:(r + 1) * D]
                    for m in chunks:
                        pe.matmul(to, hi[:, m, r, :], w[0][:, m, :], start=False, stop=False, skip_group_check=True)
                        pe.matmul(to, hi[:, m, r, :], w[1][:, m, :], start=False, stop=False, skip_group_check=True)
                        last = pe.matmul(to, lo[:, m, r, :], w[0][:, m, :], start=False,
                                         stop=(ends and m == chunks[-1]), skip_group_check=True)
                return last

            def bias_rows(bank, at):
                for r in range(R):
                    pe.matmul(bank[:, r * D:(r + 1) * D], k.ones3[:, 0:P], k.bias_parts[:, at:at + D],
                              start=(r == 0), stop=False, skip_group_check=True)

            def gat2_half(item, j):
                s = item.slot(PER)
                if j == 0:
                    if item.follows(1):
                        pe.wait_ge(y_set.at(item - 1), y_set.count(item - 1))
                    bias_rows(h2_bank, HC)
                pe.wait_ge(elu_lo_set[j].at(item), elu_lo_set[j].count(item))
                last = nodes(h2_bank, range(j * MH, (j + 1) * MH), elu_hi[s], elu_lo[s], k.w2_p, j == 1)
                if j == 1:
                    last.then_inc(h2_ps.at(item), 1)

            def mlp_out(item):
                s = item.slot(PER)
                pe.wait_ge(hid_set.at(item), hid_set.count(item))
                if item.follows(1):
                    pe.wait_ge(v_set.at(item - 1), v_set.count(item - 1))
                bias_rows(mlp_bank, HC + 2 * D)
                nodes(mlp_bank, range(KC), hid_hi[s], hid_lo[s], k.mw2_p, True).then_inc(mlp_ps.at(item), 1)

            def step(i, c):
                if i is None and c == 0:
                    turn_x(Item(None, 0, PER), P)
                now, p = in_group(i, c, 0)
                was, q = in_group(i, c, 1)
                old, _ = in_group(i, c, 2)
                soon, o = in_group(i, c, -1)
                if now is not None:
                    gat1_half(now, 0)
                if old is not None:
                    mlp_out(old)
                if now is not None:
                    gat1_half(now, 1)
                if was is not None:
                    turn_x1(was, q)
                if soon is not None:
                    turn_x(soon, o)
                if now is not None:
                    gat2_half(now, 0)
                if was is not None:
                    mlp_hidden(was)
                if now is not None:
                    gat2_half(now, 1)

            steps(pe, step)

        @block.scalar
        def _(act):
            def norm_x(item, p):
                s = item.slot(PER)
                if item.follows(PER):
                    act.wait_ge(xn_turned.at(item - PER), xn_turned.count(item - PER))
                norm_on_act(act, st["x"][4], item, xs[s][0:p, :, :], rstd["x"][s][0:p], shift["x"][s][0:p],
                            xn[s][0:p, :, :]).then_inc(xn_set.at(item), 1)

            def copy_x(item, p):
                act.wait_ge(xn_turned.at(item), xn_turned.count(item))
                if item.follows(PER):
                    act.wait_ge(h_ps[1].at(item - PER), h_ps[1].count(item - PER))
                act.activation(xt_hi[item.slot(PER)][:, :, :, 0:p], turned(xt_ps, KC)[:, :, :, 0:p], ACT.Copy)\
                    .then_inc(xt_hi_set.at(item), 1)

            def half(t, item, j, p):
                return t[item.slot(PER)][:, j * MH:(j + 1) * MH, :, 0:p]

            def exp_half(item, p, j):
                act.wait_ge(h_ps[j].at(item), h_ps[j].count(item))
                if item.follows(PER):
                    act.wait_ge(elu_lo_set[j].at(item - PER), elu_lo_set[j].count(item - PER))
                act.activation(half(elu, item, j, p), turned(h_bank[j], MH)[:, :, :, 0:p], ACT.Exp)\
                    .then_inc(exp_set[j].at(item), 1)
                act.wait_ge(exp_set[j].at(item), exp_set[j].count(item))
                act.activation(half(elu, item, j, p), half(elu, item, j, p), ACT.Relu, bias=1.0, scale=-1.0)\
                    .then_inc(neg_set[j].at(item), 1)

            def elu_hi_half(item, p, j):
                act.wait_ge(elu_set[j].at(item), elu_set[j].count(item))
                if item.follows(PER):
                    act.wait_ge(h2_ps.at(item - PER), h2_ps.count(item - PER))
                act.activation(half(elu_hi, item, j, p), half(elu, item, j, p), ACT.Copy)\
                    .then_inc(elu_hi_set[j].at(item), 1)

            def step(i, c):
                if i is None and c == 0:
                    norm_x(Item(None, 0, PER), P)
                    copy_x(Item(None, 0, PER), P)
                now, p = in_group(i, c, 0)
                was, q = in_group(i, c, 1)
                old, u = in_group(i, c, 2)
                soon, o = in_group(i, c, -1)
                if now is not None:
                    exp_half(now, p, 0)
                if was is not None:
                    s = was.slot(PER)
                    norm_on_act(act, st["y"][4], was, y[s][0:q, :, :], rstd["y"][s][0:q], shift["y"][s][0:q],
                                y[s][0:q, :, :]).then_inc(x1_set.at(was), 1)
                if soon is not None:
                    norm_x(soon, o)
                if now is not None:
                    elu_hi_half(now, p, 0)
                    exp_half(now, p, 1)
                if was is not None:
                    act.wait_ge(x1_turned.at(was), x1_turned.count(was))
                    if was.follows(PER):
                        act.wait_ge(hid_ps.at(was - PER), hid_ps.count(was - PER))
                    act.activation(zt_hi[s][:, :, :, 0:q], turned(zt_ps, KC)[:, :, :, 0:q], ACT.Copy)\
                        .then_inc(zt_hi_set.at(was), 1)
                if now is not None:
                    elu_hi_half(now, p, 1)
                if soon is not None:
                    copy_x(soon, o)
                if was is not None:
                    act.wait_ge(hid_ps.at(was), hid_ps.count(was))
                    if was.follows(PER):
                        act.wait_ge(mlp_ps.at(was - PER), mlp_ps.count(was - PER))
                    act.activation(hid_hi[s][:, :, :, 0:q], turned(hid_bank, KC)[:, :, :, 0:q], ACT.Relu)\
                        .then_inc(hid_hi_set.at(was), 1)
                if old is not None:
                    s = old.slot(PER)
                    norm_on_act(act, st["s"][4], old, v[s][0:u, :, :], rstd["s"][s][0:u], shift["s"][s][0:u],
                                v[s][0:u, :, :]).then_inc(o_set.at(old), 1)
                if now is not None:
                    act.wait_ge(h2_ps.at(now), h2_ps.count(now))
                    if now.follows(PER):
                        act.wait_ge(h2_out.at(now - PER), h2_out.count(now - PER, 16))
                    act.activation(flat(h2[now.slot(PER)], p), h2_bank[0:p, :], ACT.Copy).then_inc(h2_set.at(now), 1)

            steps(act, step)

        @block.gpsimd
        def _(pool):
            def rstd_of(n, item, p):
                if item is not None:
                    s = item.slot(PER)
                    norm_rstd(pool, k, st[n][1:4], item, mv[n][s][0:p], ve[n][s][0:p, :], rstd[n][s][0:p, :])

            def elu_lo_half(item, p, j):
                if item is not None:
                    s = item.slot(PER)
                    pool.wait_ge(elu_hi_set[j].at(item), elu_hi_set[j].count(item))
                    if item.follows(PER):
                        pool.wait_ge(h2_ps.at(item - PER), h2_ps.count(item - PER))
                    m = slice(j * MH, (j + 1) * MH)
                    pool.tensor_tensor(elu_lo[s][:, m, :, 0:p], elu[s][:, m, :, 0:p],
                                       elu_hi[s][:, m, :, 0:p].bitcast(F32), ALU.subtract)\
                        .then_inc(elu_lo_set[j].at(item), 1)

            def step(i, c):
                if i is None and c == 0:
                    rstd_of("x", Item(None, 0, PER), P)
                now, p = in_group(i, c, 0)
                was, q = in_group(i, c, 1)
                old, o = in_group(i, c, 2)
                rstd_of("y", was, q)
                rstd_of("x", *in_group(i, c, -1))
                elu_lo_half(now, p, 0)
                rstd_of("v", old, o)
                if was is not None:
                    pool.wait_ge(x1_set.at(was), x1_set.count(was))
                    if was.follows(PER):
                        pool.wait_ge(s_set.at(was - PER), s_set.count(was - PER))
                    s = was.slot(PER)
                    beta = k.beta[0:q, :].unsqueeze(1).broadcast_to([q, R, D])
                    pool.tensor_tensor(x1b[s][0:q, :, :], y[s][0:q, :, :], beta, ALU.add).then_inc(x1b_set.at(was), 1)
                elu_lo_half(now, p, 1)
                rstd_of("s", old, o)

            steps(pool, step)

        @block.vector
        def _(dve):
            def stats_of(n, item, p, data):
                s = item.slot(PER)
                norm_stats(dve, k, st[n][0:2], item, data[s][0:p, :, :], stats[n][s][0:p], mv[n][s][0:p])

            def shift_of(n, item, p):
                s = item.slot(PER)
                norm_shift(dve, st[n][3:5], item, mv[n][s][0:p], rstd[n][s][0:p, :], shift[n][s][0:p, :])

            def elu_half(item, p, j):
                dve.wait_ge(neg_set[j].at(item), neg_set[j].count(item))
                half = elu[item.slot(PER)][:, j * MH:(j + 1) * MH, :, 0:p]
                bank = turned(h_bank[j], MH)[:, :, :, 0:p]
                if p == P:
                    half, bank = half.rearrange("q m r p -> q (m r p)"), h_bank[j][:, :]
                    dve.scalar_tensor_tensor(half, half, -1.0, bank, ALU.mult, ALU.max).then_inc(elu_set[j].at(item), 1)
                    return
                for m in range(MH):
                    last = dve.scalar_tensor_tensor(half[:, m], half[:, m], -1.0, bank[:, m], ALU.mult, ALU.max)
                last.then_inc(elu_set[j].at(item), 1)

            def lo_of(item, p, hi_set, lo_set, used, ps, hi, lo):
                s = item.slot(PER)
                dve.wait_ge(hi_set.at(item), hi_set.count(item))
                if item.follows(PER):
                    dve.wait_ge(used.at(item - PER), used.count(item - PER))
                dve.tensor_tensor(lo[s][:, :, :, 0:p], turned(ps, KC)[:, :, :, 0:p], hi[s][:, :, :, 0:p].bitcast(F32),
                                  ALU.subtract).then_inc(lo_set.at(item), 1)

            def lo_of_x(item, p):
                lo_of(item, p, xt_hi_set, xt_set, h_ps[1], xt_ps, xt_hi, xt_lo)

            def step(i, c):
                if i is None and c == 0:
                    first = Item(None, 0, PER)
                    dve.wait_ge(x_in.at(first), x_in.count(first, 16))
                    stats_of("x", first, P, xs)
                    shift_of("x", first, P)
                    lo_of_x(first, P)
                now, p = in_group(i, c, 0)
                was, q = in_group(i, c, 1)
                old, o = in_group(i, c, 2)
                soon, u = in_group(i, c, -1)
                if was is not None:
                    s = was.slot(PER)
                    dve.wait_ge(h2_set.at(was), h2_set.count(was))
                    if was.follows(PER):
                        dve.wait_ge(x1_out.at(was - PER), x1_out.count(was - PER, 16))
                        dve.wait_ge(x1_turned.at(was - PER), x1_turned.count(was - PER))
                        dve.wait_ge(x1b_set.at(was - PER), x1b_set.count(was - PER))
                    dve.tensor_tensor(flat(y[s], q), h2_bank[0:q, :], flat(xs[s], q), ALU.add).then_inc(y_set.at(was), 1)
                    dve.wait_ge(y_set.at(was), y_set.count(was))
                    stats_of("y", was, q, y)
                if soon is not None:
                    dve.wait_ge(x_in.at(soon), x_in.count(soon, 16))
                    stats_of("x", soon, u, xs)
                if was is not None:
                    shift_of("y", was, q)
                if now is not None:
                    elu_half(now, p, 0)
                if soon is not None:
                    shift_of("x", soon, u)
                if old is not None:
                    s = old.slot(PER)
                    dve.wait_ge(mlp_ps.at(old), mlp_ps.count(old))
                    if old.follows(PER):
                        dve.wait_ge(o_out.at(old - PER), o_out.count(old - PER, 16))
                    dve.scalar_tensor_tensor(flat(v[s], o), mlp_bank[0:o, :], 0.0, flat(y[s], o), ALU.max, ALU.add)\
                        .then_inc(v_set.at(old), 1)
                    dve.wait_ge(v_set.at(old), v_set.count(old))
                    stats_of("v", old, o, v)
                if now is not None:
                    elu_half(now, p, 1)
                if was is not None:
                    lo_of(was, q, zt_hi_set, zt_set, hid_ps, zt_ps, zt_hi, zt_lo)
                if old is not None:
                    s = old.slot(PER)
                    dve.wait_ge(st["v"][1].at(old), st["v"][1].count(old))
                    for r in range(R):
                        last = dve.scalar_tensor_tensor(v[s][0:o, r, :], v[s][0:o, r, :], mv["v"][s][0:o, r, 0:1],
                                                        k.gamma[0:o, :], ALU.subtract, ALU.mult)
                    last.then_inc(a_set.at(old), 1)
                if soon is not None:
                    lo_of_x(soon, u)
                if old is not None:
                    s = old.slot(PER)
                    dve.wait_ge(a_set.at(old), a_set.count(old))
                    dve.wait_ge(st["v"][3].at(old), st["v"][3].count(old))
                    dve.wait_ge(x1b_set.at(old), x1b_set.count(old))
                    for r in range(R):
                        last = dve.scalar_tensor_tensor(v[s][0:o, r, :], v[s][0:o, r, :], rstd["v"][s][0:o, r:r + 1],
                                                        x1b[s][0:o, r, :], ALU.mult, ALU.add)
                    last.then_inc(s_set.at(old), 1)
                    dve.wait_ge(s_set.at(old), s_set.count(old))
                    stats_of("s", old, o, v)
                if was is not None:
                    s = was.slot(PER)
                    dve.wait_ge(hid_hi_set.at(was), hid_hi_set.count(was))
                    if was.follows(PER):
                        dve.wait_ge(mlp_ps.at(was - PER), mlp_ps.count(was - PER))
                    for m in range(KC):
                        last = dve.scalar_tensor_tensor(hid_lo[s][:, m, :, 0:q], turned(hid_bank, KC)[:, m, :, 0:q], 0.0,
                                                        hid_hi[s][:, m, :, 0:q].bitcast(F32), ALU.max, ALU.subtract)
                    last.then_inc(hid_set.at(was), 1)
                if old is not None:
                    shift_of("s", old, o)

            steps(dve, step)


def gat2_replace(nc, k):
    D, T = k.D, k.T
    PER = 2
    ctx, sb, sem = phase(nc, "gat2_replace")
    with ctx:
        fix_in, idx_set, fix_out = sem("fix_in", 2), sem("idx_set"), sem("fix_out", 2)
        prod_set, term_set = sem("prod_set"), sem("term_set")
        fix = [sb(f"fix{s}", [P, D]) for s in range(2)]
        idx = [sb(f"idx{s}", [P, 1], I32) for s in range(2)]
        prod = [sb(f"prod{s}", [P, 2, D]) for s in range(2)]
        block = ctx.enter_context(nc.Block())

        @block.sync
        def _(sp):
            def body(item):
                s = item.slot(2)
                if item.follows(2):
                    sp.wait_ge(fix_out.at(item - 2), fix_out.count(item - 2, 16))
                if item.follows(2):
                    sp.wait_ge(prod_set.at(item - 2), prod_set.count(item - 2))
                sp.dma_start(fix[s][:, :], k.fix_dram[bass.ds(item.index(), 1), :, :].rearrange("t p d -> (t p) d"))\
                    .then_inc(fix_in.at(item), 16)

            each_item(sp, T, PER, body)

        @block.gpsimd
        def _(pool):
            def body(item):
                s = item.slot(2)
                if item.follows(2):
                    pool.wait_ge(fix_out.at(item - 2), fix_out.count(item - 2, 16))
                pool.tensor_copy(idx[s][:, :], k.last_idx[:, bass.ds(item.index(), 1)])\
                    .then_inc(idx_set.at(item), 1)
                pool.wait_ge(idx_set.at(item), idx_set.count(item))
                pool.wait_ge(fix_in.at(item), fix_in.count(item, 16))
                apart(pool, k)
                pool.indirect_dma_start(out=k.h2_dram[:, :], out_offset=bass.IndirectOffsetOnAxis(idx[s][:, :], 0),
                                             in_=fix[s][:, :], in_offset=None, bounds_check=k.N - 1,
                                             oob_is_err=False)\
                    .then_inc(fix_out.at(item), 16)

            each_item(pool, T, PER, body)
            for back in range(2):
                pool.wait_ge(fix_out.at(Item(None, T - 1 - back, PER)), fix_out.count(Item(None, T - 1 - back, PER), 16))

        @block.vector
        def _(dve):
            def body(item):
                s = item.slot(2)
                dve.wait_ge(fix_in.at(item), fix_in.count(item, 16))
                row = fix[s][:, :].unsqueeze(1).broadcast_to([P, 2, D])
                dve.tensor_tensor(prod[s][:, :, :], row, k.att2[:, :, :], ALU.mult)\
                    .then_inc(prod_set.at(item), 1)
                dve.wait_ge(prod_set.at(item), prod_set.count(item))
                dve.tensor_reduce(k.terms2[:, 1:3, bass.ds(item.index(), 1)], prod[s][:, :, :], AX_X, ALU.add)\
                    .then_inc(term_set.at(item), 1)

            each_item(dve, T, PER, body)


def gat2_scores(nc, k):
    D, T = k.D, k.T
    PER = 4
    ctx, sb, sem = phase(nc, "gat2_scores")
    with ctx:
        rows_in, rows_out = sem("rows_in", PER), sem("rows_out", PER)
        idx_set, prod_set, term_set = sem("idx_set"), sem("prod_set"), sem("term_set")
        rows = [sb(f"rows{s}", [P, D]) for s in range(PER)]
        idx = [sb(f"idx{s}", [P, 1], I32) for s in range(PER)]
        prod = [sb(f"prod{s}", [P, D]) for s in range(PER)]
        block = ctx.enter_context(nc.Block())

        @block.gpsimd
        def _(pool):
            def gather(item):
                s = item.slot(PER)
                if item.follows(PER):
                    pool.wait_ge(rows_in.at(item - PER), rows_in.count(item - PER, 16))
                    pool.wait_ge(prod_set.at(item - PER), prod_set.count(item - PER))
                    pool.wait_ge(rows_out.at(item - PER), rows_out.count(item - PER, 16))
                pool.tensor_copy(idx[s][:, :], k.src_idx[:, bass.ds(item.index(), 1)])\
                    .then_inc(idx_set.at(item), 1)
                pool.wait_ge(idx_set.at(item), idx_set.count(item))
                apart(pool, k)
                pool.indirect_dma_start(out=rows[s][:, :], out_offset=None, in_=k.h2_dram[:, :],
                                        in_offset=bass.IndirectOffsetOnAxis(idx[s][:, :], 0),
                                        bounds_check=k.N - 1, oob_is_err=True)\
                    .then_inc(rows_in.at(item), 16)

            each_item_lagged(pool, T, PER, (0, gather))

        @block.sync
        def _(sp):
            def store(item):
                sp.wait_ge(rows_in.at(item), rows_in.count(item, 16))
                sp.dma_start(k.h2_src_dram[bass.ds(item.index(), 1), :, :].rearrange("t p d -> (t p) d"),
                             rows[item.slot(PER)][:, :])\
                    .then_inc(rows_out.at(item), 16)

            each_item_lagged(sp, T, PER, (0, store))
            for back in range(PER):
                sp.wait_ge(rows_out.at(Item(None, T - 1 - back, PER)), rows_out.count(Item(None, T - 1 - back, PER), 16))

        @block.vector
        def _(dve):
            def multiply(item):
                s = item.slot(PER)
                dve.wait_ge(rows_in.at(item), rows_in.count(item, 16))
                dve.tensor_tensor(prod[s][:, :], rows[s][:, :], k.att2[:, 0, :], ALU.mult)\
                    .then_inc(prod_set.at(item), 1)

            def add_up(item):
                dve.wait_ge(prod_set.at(item), prod_set.count(item))
                dve.tensor_reduce(k.terms2[:, 0, bass.ds(item.index(), 1)], prod[item.slot(PER)][:, :], AX_X, ALU.add)\
                    .then_inc(term_set.at(item), 1)

            each_item_lagged(dve, T, PER, (0, multiply), (1, add_up))


def gat2_softmax(nc, k):
    T = k.T
    ctx, sb, sem = phase(nc, "gat2_softmax")
    with ctx:
        link_sem, rows_turned, shifted, exps_set, exps_turned, tables_set = (
            sem("link"), sem("rows_turned"), sem("shifted"), sem("exps_set"), sem("exps_turned"), sem("tables_set"))
        const = k.att2_const
        rows = sb("rows", [T, 3, P])
        spread = sb("spread", [T, 2, P])
        score = sb("score", [T, 2, P])
        run_max, maxima = sb("run_max", [T, 1, P]), sb("maxima", [T, 1, P])

        def names(tag):
            return (lambda n, shape, dt=F32: sb(f"{tag}_{n}", shape, dt)), (lambda n, ring=1: sem(f"{tag}_{n}", ring))

        seg_sum = Segments(k, 2, *names("spread"), k.psum[1], k.psum[2])
        seg_max = Segments(k, 1, *names("max"), k.psum[3], k.psum[4])
        block = ctx.enter_context(nc.Block())

        @block.vector
        def _(dve):
            link = Link(dve, link_sem)
            dve.wait_ge(rows_turned[0], 1)
            link(dve.tensor_copy(rows[:, :, :].rearrange("t n e -> t (n e)"), k.psum[0][0:T, 0:3 * P]))
            for j in range(2):
                last = dve.tensor_tensor(rows[:, 1 + j, :], rows[:, 1 + j, :], k.is_last[:, :], ALU.mult)
            link(last)
            seg_sum.scan(dve, link, k.not_last[:, :], rows[:, 1:3, :], spread, (ALU.mult, ALU.add), 0.0, True)
            dve.tensor_tensor(score[:, 0, :], rows[:, 0, :], spread[:, 1, :], ALU.add)
            link(dve.tensor_tensor(score[:, 1, :], spread[:, 0, :], spread[:, 1, :], ALU.add))
            flat = score[:, :, :].rearrange("t j e -> t (j e)")
            link(dve.tensor_scalar(flat, flat, const[0:T, :], None, ALU.add))
            link(dve.scalar_tensor_tensor(flat, flat, NEG_SLOPE, flat, ALU.mult, ALU.max))
            seg_max.scan(dve, link, k.cut_first[:, :], score[:, 0:1, :], run_max, (ALU.add, ALU.max), LOW, False)
            seg_max.scan(dve, link, k.cut_last[:, :], run_max, maxima, (ALU.add, ALU.max), LOW, True)
            link(dve.tensor_tensor(maxima[:, 0, :], maxima[:, 0, :], score[:, 1, :], ALU.max))
            for j in range(2):
                last = dve.tensor_tensor(score[:, j, :], score[:, j, :], maxima[:, 0, :], ALU.subtract)
            last.then_inc(shifted[0], 1)
            dve.wait_ge(exps_turned[0], 1)
            dve.tensor_copy(k.p2[:, :], k.psum[5][:, 0:T])
            dve.tensor_copy(k.ps2[:, :], k.psum[5][:, P:P + T]).then_inc(tables_set[0], 1)

        @block.scalar
        def _(act):
            act.wait_ge(shifted[0], 1)
            flat = score[:, :, :].rearrange("t j e -> t (j e)")
            act.activation(flat, flat, ACT.Exp).then_inc(exps_set[0], 1)

        @block.tensor
        def _(pe):
            for j in range(3):
                last = pe.transpose(k.psum[0][0:T, j * P:(j + 1) * P], k.terms2[:, j, :], k.ident[:, :])
            last.then_inc(rows_turned[0], 1)
            seg_sum.turn(pe, 1, (True,))
            seg_max.turn(pe, 2, (False, True))
            pe.wait_ge(exps_set[0], 1)
            for j in range(2):
                last = pe.transpose(k.psum[5][:, j * P:j * P + T], score[:, j, :], k.ident[0:T, 0:T])
            last.then_inc(exps_turned[0], 1)


def gat2_messages(nc, k):
    D, T = k.D, k.T
    PER = 4
    ctx, sb, sem = phase(nc, "gat2_messages")
    with ctx:
        last_idx_set, rows_in, same_set, msg_set = sem("last_idx_set"), sem("rows_in", PER), sem("same_set"), sem("msg_set")
        sum_ps, sum_set, zero_set = sem("sum_ps"), sem("sum_set"), sem("zero_set")
        den_set, inv_set, num_set, y_set = sem("den_set"), sem("inv_set"), sem("num_set"), sem("y_set")
        st = [sem(n) for n in ("st_done", "mv_done", "ve_done", "rs_done", "shift_done")]
        x1_set, x1_out, copy_out = sem("x1_set"), sem("x1_out", PER), sem("copy_out", PER)

        def ring(name, shape, dt=F32):
            return [sb(f"{name}{s}", shape, dt) for s in range(PER)]

        last_idx = ring("last_idx", [P, 1], I32)
        h2_src, x_own, fix = (ring(n, [P, D]) for n in ("h2_src", "x_own", "fix"))
        dst_row, same, carry = (ring(n, [P, P]) for n in ("dst_row", "same", "carry"))
        msg, sums = (ring(n, [P, D + 1]) for n in ("msg", "sums"))
        y = ring("y", [P, 1, D])
        stats, mv = ring("stats", [P, 1, 6]), ring("mv", [P, 1, 2])
        inv, ve, rstd, shift = (ring(n, [P, 1]) for n in ("inv", "ve", "rstd", "shift"))
        sum_bank = k.psum[0:2]
        block = ctx.enter_context(nc.Block())

        @block.sync
        def _(sp):
            def load(item):
                s = item.slot(PER)
                t = bass.ds(item.index(), 1)
                if item.follows(PER):
                    sp.wait_ge(msg_set.at(item - PER), msg_set.count(item - PER))
                    sp.wait_ge(y_set.at(item - PER), y_set.count(item - PER))
                    sp.wait_ge(same_set.at(item - PER), same_set.count(item - PER))
                for to, of in ((h2_src, k.h2_src_dram), (x_own, k.x_own_dram), (fix, k.fix_dram)):
                    sp.dma_start(to[s][:, :], of[t, :, :].rearrange("t p d -> (t p) d"))\
                        .then_inc(rows_in.at(item), 16)
                sp.dma_start(dst_row[s][:, :], k.dst_dram[t, :].broadcast_to([P, P]))\
                    .then_inc(rows_in.at(item), 16)

            def store(item):
                sp.wait_ge(x1_set.at(item), x1_set.count(item))
                sp.dma_start(k.fix1_dram[bass.ds(item.index(), 1), :, :].rearrange("t p d -> (t p) d"),
                             y[item.slot(PER)][:, 0, :])\
                    .then_inc(copy_out.at(item), 16)

            each_item_lagged(sp, T, PER, (0, load), (4, store))
            for back in range(PER):
                sp.wait_ge(copy_out.at(Item(None, T - 1 - back, PER)), copy_out.count(Item(None, T - 1 - back, PER), 16))

        @block.gpsimd
        def _(pool):
            def norm(item):
                s = item.slot(PER)
                norm_rstd(pool, k, st[1:4], item, mv[s], ve[s][:, :], rstd[s][:, :])

            def scatter(item):
                s = item.slot(PER)
                if item.follows(PER):
                    pool.wait_ge(x1_out.at(item - PER), x1_out.count(item - PER, 16))
                pool.tensor_copy(last_idx[s][:, :], k.last_idx[:, bass.ds(item.index(), 1)])\
                    .then_inc(last_idx_set.at(item), 1)
                pool.wait_ge(last_idx_set.at(item), last_idx_set.count(item))
                pool.wait_ge(x1_set.at(item), x1_set.count(item))
                apart(pool, k)
                pool.indirect_dma_start(out=k.x1_dram[:, :], out_offset=bass.IndirectOffsetOnAxis(last_idx[s][:, :], 0),
                                        in_=y[s][:, 0, :], in_offset=None, bounds_check=k.N - 1,
                                        oob_is_err=False)\
                    .then_inc(x1_out.at(item), 16)

            each_item_lagged(pool, T, PER, (0, norm), (2, scatter))
            for back in range(PER):
                pool.wait_ge(x1_out.at(Item(None, T - 1 - back, PER)), x1_out.count(Item(None, T - 1 - back, PER), 16))

        @block.tensor
        def _(pe):
            def sum_up(item):
                s, b = item.slot(PER), item.slot(2)
                pe.wait_ge(msg_set.at(item), msg_set.count(item))
                if not item.follows(1):
                    pe.wait_ge(zero_set[0], 1)
                if item.follows(1):
                    pe.wait_ge(sum_set.at(item - 1), sum_set.count(item - 1))
                pe.matmul(sum_bank[b][:, 0:D + 1], same[s][:, :], msg[s][:, :], start=True, stop=False)
                pe.matmul(sum_bank[b][:, 0:D + 1], carry[s][:, :], sums[(s + PER - 1) % PER][:, :], start=False, stop=True)\
                    .then_inc(sum_ps.at(item), 1)

            each_item_lagged(pe, T, PER, (0, sum_up))

        @block.scalar
        def _(act):
            def copy_sums(item):
                s, b = item.slot(PER), item.slot(2)
                act.wait_ge(sum_ps.at(item), sum_ps.count(item))
                if item.follows(PER):
                    act.wait_ge(num_set.at(item - PER), num_set.count(item - PER))
                act.activation(sums[s][:, :], sum_bank[b][:, 0:D + 1], ACT.Copy)\
                    .then_inc(sum_set.at(item), 1)

            def norm_out(item):
                s = item.slot(PER)
                norm_on_act(act, st[4], item, y[s], rstd[s], shift[s], y[s]).then_inc(x1_set.at(item), 1)

            each_item_lagged(act, T, PER, (0, copy_sums), (2, norm_out))

        @block.vector
        def _(dve):
            dve.memset(sums[PER - 1][:, :], 0.0)\
                .then_inc(zero_set.at(Item(None, 0, 1)), 1)

            def messages(item):
                s = item.slot(PER)
                t = bass.ds(item.index(), 1)
                dve.wait_ge(rows_in.at(item), rows_in.count(item, 64))
                if item.follows(PER):
                    dve.wait_ge(sum_ps.at(item - PER), sum_ps.count(item - PER))
                same_and_carry(dve, item, k, dst_row[s][:, :], same[s][:, :], carry[s][:, :])\
                    .then_inc(same_set.at(item), 1)
                dve.tensor_copy(msg[s][:, D:D + 1], k.p2[:, t])
                dve.tensor_scalar(msg[s][:, 0:D], h2_src[s][:, :], k.p2[:, t], None, ALU.mult)\
                    .then_inc(msg_set.at(item), 1)

            def divide(item):
                s = item.slot(PER)
                ps_t = k.ps2[:, bass.ds(item.index(), 1)]
                dve.wait_ge(sum_set.at(item), sum_set.count(item))
                if item.follows(PER):
                    dve.wait_ge(x1_out.at(item - PER), x1_out.count(item - PER, 16))
                    dve.wait_ge(copy_out.at(item - PER), copy_out.count(item - PER, 16))
                dve.tensor_tensor(inv[s][:, :], sums[s][:, D:D + 1], ps_t, ALU.add)\
                    .then_inc(den_set.at(item), 1)
                dve.scalar_tensor_tensor(y[s][:, 0, :], fix[s][:, :], ps_t, sums[s][:, 0:D], ALU.mult, ALU.add)\
                    .then_inc(num_set.at(item), 1)
                dve.wait_ge(den_set.at(item), den_set.count(item))
                dve.reciprocal(inv[s][:, :], inv[s][:, :])\
                    .then_inc(inv_set.at(item), 1)
                dve.wait_ge(num_set.at(item), num_set.count(item))
                dve.wait_ge(inv_set.at(item), inv_set.count(item))
                dve.scalar_tensor_tensor(y[s][:, 0, :], y[s][:, 0, :], inv[s][:, 0:1], x_own[s][:, :],
                                         ALU.mult, ALU.add)\
                    .then_inc(y_set.at(item), 1)

            def statistics(item):
                s = item.slot(PER)
                dve.wait_ge(y_set.at(item), y_set.count(item))
                norm_stats(dve, k, (st[0], st[1]), item, y[s], stats[s], mv[s])

            def shift_of(item):
                s = item.slot(PER)
                norm_shift(dve, st[3:5], item, mv[s], rstd[s][:, :], shift[s][:, :])

            each_item_lagged(dve, T, PER, (0, messages), (1, divide), (1, statistics), (2, shift_of))


def gine(nc, k, edge_attr, out):
    D, KC, HC, T, E, LAST = k.D, k.KC, k.HC, k.T, k.E, k.LAST
    PER = 6
    ctx, sb, sem = phase(nc, "gine")
    with ctx:
        src_idx_set, last_idx_set = sem("src_idx_set"), sem("last_idx_set")
        src_in, own_in, same_set = sem("src_in", PER), sem("own_in", PER), sem("same_set")
        edge_set, msg_set, sum_ps, sum_set, zero_set = (
            sem("edge_set"), sem("msg_set"), sem("sum_ps"), sem("sum_set"), sem("zero_set"))
        z_set, z_turned, zt_set, hid_ps, hid_set, mlp_ps = (
            sem("z_set"), sem("z_turned"), sem("zt_set"), sem("hid_ps"), sem("hid_set"), sem("mlp_ps"))
        v_set, a_set, b_set, s_set, o_set, o_out = (
            sem("v_set"), sem("a_set"), sem("b_set"), sem("s_set"), sem("o_set"), sem("o_out", PER))
        st_v = [sem(f"v_{n}") for n in ("st", "mv", "ve", "rstd")]
        st_s = [sem(f"s_{n}") for n in ("st", "mv", "ve", "rstd", "shift")]

        def ring(name, shape, dt=F32):
            return [sb(f"{name}{s}", shape, dt) for s in range(PER)]

        src_idx, last_idx = ring("src_idx", [P, 1], I32), ring("last_idx", [P, 1], I32)
        x1_src, attr, x1_own, x1b, sums, z = (
            ring(n, [P, D]) for n in ("x1_src", "attr", "x1_own", "x1b", "sums", "z"))
        dst_row, same, carry = (ring(n, [P, P]) for n in ("dst_row", "same", "carry"))
        zt, hid = ring("zt", [P, KC, P]), ring("hid", [P, KC, P])
        v = ring("v", [P, 1, D])
        v_stats, s_stats = ring("v_stats", [P, 1, 6]), ring("s_stats", [P, 1, 6])
        v_mv, s_mv = ring("v_mv", [P, 1, 2]), ring("s_mv", [P, 1, 2])
        v_ve, v_rstd, s_ve, s_rstd, s_shift = (
            ring(n, [P, 1]) for n in ("v_ve", "v_rstd", "s_ve", "s_rstd", "s_shift"))
        sum_bank, turn_bank, hid_bank, mlp_bank = k.psum[0:2], k.psum[2:4], k.psum[4:6], k.psum[6:8]
        block = ctx.enter_context(nc.Block())

        @block.sync
        def _(sp):
            def load(item):
                s = item.slot(PER)
                t = bass.ds(item.index(), 1)
                if item.follows(PER):
                    sp.wait_ge(same_set.at(item - PER), same_set.count(item - PER))
                    sp.wait_ge(edge_set.at(item - PER), edge_set.count(item - PER))
                    sp.wait_ge(b_set.at(item - PER), b_set.count(item - PER))
                    sp.wait_ge(v_set.at(item - PER), v_set.count(item - PER))
                n = LAST if item.i is None and item.c == T - 1 else P
                sp.dma_start(attr[s][0:n, :], edge_attr[bass.ds(item.index() * P, n), :])\
                    .then_inc(own_in.at(item), 16)
                sp.dma_start(x1_own[s][:, :], k.fix1_dram[t, :, :].rearrange("t p d -> (t p) d"))\
                    .then_inc(own_in.at(item), 16)
                sp.dma_start(dst_row[s][:, :], k.dst_dram[t, :].broadcast_to([P, P]))\
                    .then_inc(own_in.at(item), 16)

            each_item_lagged(sp, T, PER, (0, load))

        @block.gpsimd
        def _(pool):
            def gather(item):
                s = item.slot(PER)
                if item.follows(PER):
                    pool.wait_ge(src_in.at(item - PER), src_in.count(item - PER, 16))
                    pool.wait_ge(sum_ps.at(item - PER), sum_ps.count(item - PER))
                pool.tensor_copy(src_idx[s][:, :], k.src_idx[:, bass.ds(item.index(), 1)])\
                    .then_inc(src_idx_set.at(item), 1)
                pool.wait_ge(src_idx_set.at(item), src_idx_set.count(item))
                apart(pool, k)
                pool.indirect_dma_start(out=x1_src[s][:, :], out_offset=None, in_=k.x1_dram[:, :],
                                        in_offset=bass.IndirectOffsetOnAxis(src_idx[s][:, :], 0),
                                        bounds_check=k.N - 1, oob_is_err=True)\
                    .then_inc(src_in.at(item), 16)

            def v_norm(item):
                s = item.slot(PER)
                norm_rstd(pool, k, st_v[1:4], item, v_mv[s], v_ve[s][:, :], v_rstd[s][:, :])

            def s_norm(item):
                s = item.slot(PER)
                norm_rstd(pool, k, st_s[1:4], item, s_mv[s], s_ve[s][:, :], s_rstd[s][:, :])

            def scatter(item):
                s = item.slot(PER)
                if item.follows(PER):
                    pool.wait_ge(o_out.at(item - PER), o_out.count(item - PER, 16))
                pool.tensor_copy(last_idx[s][:, :], k.last_idx[:, bass.ds(item.index(), 1)])\
                    .then_inc(last_idx_set.at(item), 1)
                pool.wait_ge(last_idx_set.at(item), last_idx_set.count(item))
                pool.wait_ge(o_set.at(item), o_set.count(item))
                apart(pool, k)
                pool.indirect_dma_start(out=out[:, :], out_offset=bass.IndirectOffsetOnAxis(last_idx[s][:, :], 0),
                                        in_=v[s][:, 0, :], in_offset=None, bounds_check=k.N - 1,
                                        oob_is_err=False)\
                    .then_inc(o_out.at(item), 16)

            each_item_lagged(pool, T, PER, (0, gather), (6, s_norm), (7, scatter), (5, v_norm))
            for back in range(PER):
                pool.wait_ge(o_out.at(Item(None, T - 1 - back, PER)), o_out.count(Item(None, T - 1 - back, PER), 16))

        @block.tensor
        def _(pe):
            def turn(item):
                s, b = item.slot(PER), item.slot(2)
                pe.wait_ge(z_set.at(item), z_set.count(item))
                if item.follows(2):
                    pe.wait_ge(zt_set.at(item - 2), zt_set.count(item - 2))
                for c in range(KC):
                    last = pe.transpose(turn_bank[b][:, c * P:(c + 1) * P], z[s][:, c * P:(c + 1) * P], k.ident[:, :])
                last.then_inc(z_turned.at(item), 1)

            def sum_up(item):
                s, b = item.slot(PER), item.slot(2)
                pe.wait_ge(msg_set.at(item), msg_set.count(item))
                if not item.follows(1):
                    pe.wait_ge(zero_set[0], 1)
                if item.follows(1):
                    pe.wait_ge(sum_set.at(item - 1), sum_set.count(item - 1))
                pe.matmul(sum_bank[b][:, 0:D], same[s][:, :], x1_src[s][:, :], start=True, stop=False)
                pe.matmul(sum_bank[b][:, 0:D], carry[s][:, :], sums[(s + PER - 1) % PER][:, :], start=False, stop=True)\
                    .then_inc(sum_ps.at(item), 1)

            def mlp_out(item):
                s, b = item.slot(PER), item.slot(2)
                pe.wait_ge(hid_set.at(item), hid_set.count(item))
                if item.follows(2):
                    pe.wait_ge(v_set.at(item - 2), v_set.count(item - 2))
                pe.matmul(mlp_bank[b][:, 0:D], k.ones3[:, 0:P], k.bias_parts[:, HC + 2 * D:HC + 3 * D],
                          start=True, stop=False)
                for c in range(KC):
                    last = pe.matmul(mlp_bank[b][:, 0:D], hid[s][:, c, :], k.mw2[:, c, :], start=False, stop=(c == KC - 1))
                last.then_inc(mlp_ps.at(item), 1)

            def mlp_hidden(item):
                s, b = item.slot(PER), item.slot(2)
                pe.wait_ge(zt_set.at(item), zt_set.count(item))
                if item.follows(2):
                    pe.wait_ge(hid_set.at(item - 2), hid_set.count(item - 2))
                for m in range(KC):
                    to, at = hid_bank[b][:, m * P:(m + 1) * P], HC + D + m * P
                    pe.matmul(to, k.bias_parts[:, at:at + P], k.ones3[:, 0:P], start=True, stop=False)
                    for c in range(KC):
                        last = pe.matmul(to, k.mw1[:, c, m * P:(m + 1) * P], zt[s][:, c, :], start=False, stop=(c == KC - 1))
                last.then_inc(hid_ps.at(item), 1)

            each_item_lagged(pe, T, PER, (1, turn), (0, sum_up), (2, mlp_out), (1, mlp_hidden))

        @block.scalar
        def _(act):
            def copy_turned(item):
                s, b = item.slot(PER), item.slot(2)
                act.wait_ge(z_turned.at(item), z_turned.count(item))
                if item.follows(PER):
                    act.wait_ge(hid_ps.at(item - PER), hid_ps.count(item - PER))
                act.activation(zt[s][:, :, :].rearrange("p c e -> p (c e)"), turn_bank[b][:, 0:D], ACT.Copy)\
                    .then_inc(zt_set.at(item), 1)

            def norm_out(item):
                s = item.slot(PER)
                norm_on_act(act, st_s[4], item, v[s], s_rstd[s], s_shift[s], v[s]).then_inc(o_set.at(item), 1)

            def copy_sums(item):
                s, b = item.slot(PER), item.slot(2)
                act.wait_ge(sum_ps.at(item), sum_ps.count(item))
                if item.follows(PER):
                    act.wait_ge(z_set.at(item - PER), z_set.count(item - PER))
                act.activation(sums[s][:, :], sum_bank[b][:, 0:D], ACT.Copy)\
                    .then_inc(sum_set.at(item), 1)

            def messages(item):
                s = item.slot(PER)
                act.wait_ge(edge_set.at(item), edge_set.count(item))
                act.activation(x1_src[s][:, :], x1_src[s][:, :], ACT.Relu)\
                    .then_inc(msg_set.at(item), 1)

            def hidden(item):
                s, b = item.slot(PER), item.slot(2)
                act.wait_ge(hid_ps.at(item), hid_ps.count(item))
                if item.follows(PER):
                    act.wait_ge(mlp_ps.at(item - PER), mlp_ps.count(item - PER))
                act.activation(hid[s][:, :, :].rearrange("p c e -> p (c e)"), hid_bank[b][:, 0:D], ACT.Relu)\
                    .then_inc(hid_set.at(item), 1)

            each_item_lagged(act, T, PER, (2, copy_turned), (5, norm_out), (1, copy_sums), (0, messages), (2, hidden))

        @block.vector
        def _(dve):
            dve.memset(sums[PER - 1][:, :], 0.0)\
                .then_inc(zero_set.at(Item(None, 0, 1)), 1)

            def front(item):
                s = item.slot(PER)
                dve.wait_ge(own_in.at(item), own_in.count(item, 48))
                if item.follows(PER):
                    dve.wait_ge(sum_ps.at(item - PER), sum_ps.count(item - PER))
                same_and_carry(dve, item, k, dst_row[s][:, :], same[s][:, :], carry[s][:, :])\
                    .then_inc(same_set.at(item), 1)
                dve.wait_ge(src_in.at(item), src_in.count(item, 16))
                dve.tensor_tensor(x1_src[s][:, :], x1_src[s][:, :], attr[s][:, :], ALU.add)\
                    .then_inc(edge_set.at(item), 1)

            def sum_own(item):
                s = item.slot(PER)
                dve.wait_ge(sum_set.at(item), sum_set.count(item))
                if item.follows(PER):
                    dve.wait_ge(z_turned.at(item - PER), z_turned.count(item - PER))
                dve.tensor_tensor(z[s][:, :], sums[s][:, :], x1_own[s][:, :], ALU.add)\
                    .then_inc(z_set.at(item), 1)

            def make_v(item):
                s, b = item.slot(PER), item.slot(2)
                dve.wait_ge(mlp_ps.at(item), mlp_ps.count(item))
                if item.follows(PER):
                    dve.wait_ge(o_out.at(item - PER), o_out.count(item - PER, 16))
                dve.scalar_tensor_tensor(v[s][:, 0, :], mlp_bank[b][:, 0:D], 0.0, x1_own[s][:, :], ALU.max, ALU.add)\
                    .then_inc(v_set.at(item), 1)
                dve.wait_ge(v_set.at(item), v_set.count(item))
                norm_stats(dve, k, (st_v[0], st_v[1]), item, v[s], v_stats[s], v_mv[s])
                dve.tensor_tensor(x1b[s][:, :], x1_own[s][:, :], k.beta[:, :], ALU.add)\
                    .then_inc(b_set.at(item), 1)
                dve.wait_ge(st_v[1].at(item), st_v[1].count(item))
                dve.scalar_tensor_tensor(v[s][:, 0, :], v[s][:, 0, :], v_mv[s][:, 0, 0:1], k.gamma[:, :],
                                         ALU.subtract, ALU.mult)\
                    .then_inc(a_set.at(item), 1)

            def make_s(item):
                s = item.slot(PER)
                dve.wait_ge(a_set.at(item), a_set.count(item))
                dve.wait_ge(b_set.at(item), b_set.count(item))
                dve.wait_ge(st_v[3].at(item), st_v[3].count(item))
                dve.scalar_tensor_tensor(v[s][:, 0, :], v[s][:, 0, :], v_rstd[s][:, 0:1], x1b[s][:, :],
                                         ALU.mult, ALU.add)\
                    .then_inc(s_set.at(item), 1)
                dve.wait_ge(s_set.at(item), s_set.count(item))
                norm_stats(dve, k, (st_s[0], st_s[1]), item, v[s], s_stats[s], s_mv[s])

            def shift(item):
                s = item.slot(PER)
                norm_shift(dve, st_s[3:5], item, s_mv[s], s_rstd[s][:, :], s_shift[s][:, :])

            each_item_lagged(dve, T, PER, (0, front), (4, make_s), (1, sum_own), (3, make_v), (4, shift))


_INS = ["x", "src", "dst", "edge_attr_256", "L0_gnn_ln_w", "L0_gnn_ln_b", "L0_gnn_W1", "L0_gnn_att_src1",
        "L0_gnn_att_dst1", "L0_gnn_b1", "L0_gnn_W2", "L0_gnn_att_src2", "L0_gnn_att_dst2", "L0_gnn_b2",
        "L1_gnn_W1", "L1_gnn_b1", "L1_gnn_W2", "L1_gnn_b2", "L1_gnn_gamma", "L1_gnn_beta"]


def kernel(**inputs):
    import numpy as _np
    import concourse.bacc as _bacc
    from concourse import mybir as _mybir
    from concourse.bass_utils import run_bass_kernel_spmd as _run

    nc = _bacc.Bacc("TRN2", target_bir_lowering=False, num_devices=1)
    arrays, args = {}, []
    for name in _INS:
        a = _np.ascontiguousarray(inputs[name])
        arrays[f"in_{name}"] = a
        args.append(nc.dram_tensor(f"in_{name}", a.shape, _mybir.dt.from_np(a.dtype), kind="ExternalInput").ap())
    args.append(nc.dram_tensor("out_0", arrays["in_x"].shape, _mybir.dt.float32, kind="ExternalOutput").ap())
    build(nc, *args)
    r = _run(nc, [arrays], core_ids=[0])
    return r.results[0]["out_0"]
```

```python
from contextlib import ExitStack

import numpy as np

import concourse.bass as bass
from concourse import mybir

ALU = mybir.AluOpType
ACT = mybir.ActivationFunctionType
F32 = mybir.dt.float32
F32R = mybir.dt.float32r
BF16 = mybir.dt.bfloat16
I32 = mybir.dt.int32
AX_X = mybir.AxisListType.X

P = 128
LN_EPS = 1e-5
NEG_SLOPE = 0.2
NO_NODE = 1 << 20
LOW = -1.0e30


class Item:

    def __init__(self, i, c, per):
        self.i, self.c, self.per = i, c, per

    def index(self, more=0):
        k = self.c + more
        if self.i is None:
            return k
        return self.i * self.per + k if k else self.i * self.per

    def slot(self, ring):
        return self.c % ring

    def uses(self, ring):
        k = self.c // ring + 1
        if self.i is None:
            return k
        base = self.i if self.per == ring else self.i * (self.per // ring)
        return base + k if k else base

    def follows(self, k):
        return self.i is not None or self.c >= k

    def __sub__(self, k):
        return Item(self.i, self.c - k, self.per)


class Ring(list):

    def at(self, item):
        return self[item.slot(len(self))]

    def count(self, item, inc=1):
        n = item.uses(len(self))
        return n if inc == 1 else n * inc


def apart(engine, k):
    engine.sem_inc(k.waits_passed[0], 1)


def run(engine, steps, per, first, last, step):
    for c in range(min(first, steps)):
        step(None, c)
    if last > first:
        with engine.Fori(first // per, last // per) as i:
            for c in range(per):
                step(i, c)
    for c in range(max(last, first), steps):
        step(None, c)


def each_item(engine, items, per, *stages):
    behind = max(lag for lag, _ in stages)

    def step(i, c):
        for lag, stage in stages:
            if i is not None or 0 <= c - lag < items:
                stage(Item(i, c - lag, per))

    run(engine, items + behind, per, (behind + 2 * per - 1) // per * per, (items - 1) // per * per, step)


class Shared:
    pass


def build(nc, x, src, dst, edge_attr, ln_w, ln_b, g_w1, att_src1, att_dst1, g_b1, g_w2, att_src2,
          att_dst2, g_b2, m_w1, m_b1, m_w2, m_b2, gamma, beta, out):
    N, D = x.shape
    (E,) = src.shape
    H, C = att_src1.shape
    HC = H * C
    KC = D // P
    MC = HC // P
    T = (E + P - 1) // P
    LAST = E - (T - 1) * P
    assert D == 256 and HC == 512 and LAST < P and T <= P

    ctx = ExitStack()
    k = Shared()
    k.N, k.D, k.E, k.H, k.C, k.HC, k.KC, k.MC, k.T, k.LAST = N, D, E, H, C, HC, KC, MC, T, LAST
    with ctx:
        def sb(name, shape, dt=F32):
            return ctx.enter_context(nc.sbuf_tensor(name, shape, dt))

        k.psum = [ctx.enter_context(nc.psum_tensor(f"bank{b}", [P, 512], F32)) for b in range(8)]
        k.ht_dram = nc.dram_tensor("ht_dram", [T, P, 2 * D], F32).ap()
        k.dst_dram = nc.dram_tensor("dst_dram", [T, P], F32).ap()
        k.x_own_dram = nc.dram_tensor("x_own_dram", [T, P, D], F32).ap()
        k.h2_src_dram = nc.dram_tensor("h2_src_dram", [T, P, D], F32).ap()
        k.fix_dram = nc.dram_tensor("fix_dram", [T, P, D], F32).ap()
        k.fix1_dram = nc.dram_tensor("fix1_dram", [T, P, D], F32).ap()
        k.h2_dram = nc.dram_tensor("h2_dram", [N, D], F32).ap()
        k.x1_dram = nc.dram_tensor("x1_dram", [N, D], F32).ap()
        k.ident = sb("ident", [P, P])
        k.half = sb("minus_half", [P, 2])
        k.eps = sb("eps", [P, 2])
        k.waits_passed = [ctx.enter_context(nc.semaphore("waits_passed"))]
        k.w1 = sb("w1", [P, KC, HC])
        k.w2 = sb("w2", [P, MC, D])
        k.mw1 = sb("mw1", [P, KC, D])
        k.mw2 = sb("mw2", [P, KC, D])
        k.w1_p, k.w2_p, k.mw1_p, k.mw2_p = (
            [sb(f"{n}_part{j}", [P, ch, w], F32R) for j in range(2)]
            for n, ch, w in (("w1", KC, HC), ("w2", MC, D), ("mw1", KC, D), ("mw2", KC, D)))
        k.a1 = sb("a1", [P, KC, 2 * H])
        k.a1_const = sb("a1_const", [P, 2 * H])
        k.bias1 = sb("bias1", [P, HC])
        k.bias_parts = sb("bias_parts", [3, HC + 3 * D], BF16)
        k.ones3 = sb("ones3", [3, 2 * P], BF16)
        k.gamma = sb("gamma", [P, D])
        k.beta = sb("beta", [P, D])
        k.att2 = sb("att2", [P, 2, D])
        k.att2_const = sb("att2_const", [P, 1])
        k.src_idx = sb("src_idx", [P, T], I32)
        k.dst_idx = sb("dst_idx", [P, T], I32)
        k.last_idx = sb("last_idx", [P, T], I32)
        k.dst_col = sb("dst_col", [P, T])
        k.prev_col = sb("prev_col", [P, T])
        k.cut_first = sb("cut_first", [T, P])
        k.cut_last = sb("cut_last", [T, P])
        k.is_last = sb("is_last", [T, P])
        k.not_last = sb("not_last", [T, P])
        k.p1 = sb("p1", [P, T, H])
        k.ps1 = sb("ps1", [P, T, H])
        k.p2 = sb("p2", [P, T])
        k.ps2 = sb("ps2", [P, T])
        k.terms2 = sb("terms2", [P, 3, T])
        prepare(nc, k, src, dst, ln_w, ln_b, g_w1, att_src1, att_dst1, g_b1, g_w2, att_src2,
                att_dst2, g_b2, m_w1, m_b1, m_w2, m_b2, gamma, beta)
        with ExitStack() as inner:
            k.terms1 = inner.enter_context(nc.sbuf_tensor("terms1", [P, T, 2, 2 * H], F32))
            gat1_scores(nc, k, x)
            gat1_softmax(nc, k)
        dense(nc, k, x, out)
        gat1_messages(nc, k)
        gat2_scores(nc, k)
        gat2_softmax(nc, k)
        gat2_messages(nc, k)
        gine(nc, k, edge_attr, out)


def phase(nc, tag):
    ctx = ExitStack()
    made = []

    def clear():
        nc.clear_and_free_semaphores(made)
        nc.all_engine_barrier()

    ctx.callback(clear)

    def sb(name, shape, dt=F32):
        return ctx.enter_context(nc.sbuf_tensor(f"{tag}_{name}", shape, dt))

    def sem(name, ring=1):
        new = Ring(nc.alloc_semaphore(f"{tag}_{name}_{j}") for j in range(ring))
        made.extend(new)
        return new

    return ctx, sb, sem


def prepare(nc, k, src, dst, ln_w, ln_b, g_w1, att_src1, att_dst1, g_b1, g_w2, att_src2, att_dst2,
            g_b2, m_w1, m_b1, m_w2, m_b2, gamma, beta):
    H, C, HC, D, KC, MC, T, E, LAST = k.H, k.C, k.HC, k.D, k.KC, k.MC, k.T, k.E, k.LAST
    NB = HC + 3 * D
    ctx, sb, sem = phase(nc, "prepare")
    with ctx:
        w_in, tab_in, tab_set = sem("w_in"), sem("tab_in"), sem("tab_set")
        ident_set, ones_set, prev_set = sem("ident_set"), sem("ones_set"), sem("prev_set")
        dv, beta_ps, tr_ps, col_set, parts_in, dst_out = (
            sem("dv_step"), sem("beta_ps"), sem("tr_ps"), sem("col_set"), sem("parts_in"), sem("dst_out"))
        prev_in = sem("prev_in")
        lnw = sb("lnw", [P, KC])
        lnb = sb("lnb", [P, KC])
        lnb_cols = sb("lnb_cols", [P, KC, P])
        att = sb("att", [P, 2, HC])
        prod = sb("prod", [P, HC])
        bias = sb("bias", [1, NB])
        b1row = sb("b1row", [P, HC])
        b2row = sb("b2row", [P, D])
        betaw = sb("betaw", [P, HC])
        rest = sb("rest", [1, NB])
        parts = [sb(f"part{j}", [1, NB], BF16) for j in range(3)]
        rows = sb("rows", [T, 4, P], I32)
        rows_f = sb("rows_f", [T, 4, P])
        idx_f = sb("idx_f", [T, 3, P])
        flag = sb("flag", [T, P])

        block = ctx.enter_context(nc.Block())

        def row(a):
            return a.rearrange("(a n) -> a n", a=1)

        n_w = 18

        @block.sync
        def _(sp):
            with nc.allow_non_contiguous_dma(reason="columns of gains, last rows"):
                loads = [
                    (k.w1[:, :, :], g_w1.rearrange("(c p) n -> p c n", p=P)),
                    (k.w2[:, :, :], g_w2.rearrange("(c p) n -> p c n", p=P)),
                    (k.mw1[:, :, :], m_w1.rearrange("(c p) n -> p c n", p=P)),
                    (k.mw2[:, :, :], m_w2.rearrange("(c p) n -> p c n", p=P)),
                    (lnw[:, :], ln_w.rearrange("(c p) -> p c", p=P)),
                    (lnb[:, :], ln_b.rearrange("(c p) -> p c", p=P)),
                    (att[:, 0, :], att_src1.rearrange("h c -> (h c)").partition_broadcast(P)),
                    (att[:, 1, :], att_dst1.rearrange("h c -> (h c)").partition_broadcast(P)),
                    (b1row[:, :], g_b1.partition_broadcast(P)),
                    (b2row[:, :], g_b2.partition_broadcast(P)),
                    (k.gamma[:, :], gamma.partition_broadcast(P)),
                    (k.beta[:, :], beta.partition_broadcast(P)),
                    (k.att2[:, 0, :], att_src2.rearrange("a c -> (a c)").partition_broadcast(P)),
                    (k.att2[:, 1, :], att_dst2.rearrange("a c -> (a c)").partition_broadcast(P)),
                    (bias[:, HC:HC + D], row(g_b2)),
                    (bias[:, HC + D:HC + 2 * D], row(m_b1)),
                    (bias[:, HC + 2 * D:NB], row(m_b2)),
                ]
                assert len(loads) == n_w - 1
                for to, of in loads:
                    sp.dma_start(to, of).then_inc(w_in[0], 16)
                sp.dma_start(bias[:, 0:HC], row(g_b1)).then_inc(w_in[0], 16)
                sp.wait_ge(tab_set[0], 1)
                full = (T - 1) * P
                tables = [
                    (rows[0:T - 1, 0, :], src[0:full].rearrange("(t e) -> t e", e=P)),
                    (rows[T - 1:T, 0, 0:LAST], row(src[full:E])),
                    (rows[0:T - 1, 1, :], dst[0:full].rearrange("(t e) -> t e", e=P)),
                    (rows[T - 1:T, 1, 0:LAST], row(dst[full:E])),
                    (rows[0:T - 1, 2, :], dst[1:full + 1].rearrange("(t e) -> t e", e=P)),
                    (rows[T - 1:T, 2, 0:LAST - 1], row(dst[full + 1:E])),
                    (rows[0:1, 3, 1:P], row(dst[0:P - 1])),
                    (rows[1:T - 1, 3, :], dst[P - 1:full - 1].rearrange("(t e) -> t e", e=P)),
                    (rows[T - 1:T, 3, 0:LAST + 1], row(dst[full - 1:E])),
                ]
                for to, of in tables:
                    sp.dma_start(to, of).then_inc(tab_in[0], 16)
                sp.wait_ge(dv[0], 1)
                sp.dma_start(k.dst_dram[:, :], rows_f[:, 1, :]).then_inc(dst_out[0], 16)
                sp.wait_ge(dst_out[0], 16)
                sp.wait_ge(prev_set[0], 1)
                sp.dma_start(k.prev_col[P - 1:P, 1:T], k.dst_dram[0:T - 1, P - 1:P].rearrange("t a -> a t"))\
                    .then_inc(prev_in[0], 16)
                sp.wait_ge(prev_in[0], 16)
                sp.wait_ge(col_set[0], 1)
                for j in range(3):
                    sp.dma_start(k.bias_parts[j:j + 1, :], parts[j][:, :]).then_inc(parts_in[0], 16)
                sp.wait_ge(parts_in[0], 48)

        @block.gpsimd
        def _(pool):
            nc.gpsimd.memset(rows[:, 0, :], 0)
            nc.gpsimd.memset(rows[:, 1:3, :], NO_NODE)
            nc.gpsimd.memset(rows[:, 3, :], NO_NODE).then_inc(tab_set[0], 1)
            nc.gpsimd.memset(k.ident[:, :], 0.0).then_inc(ident_set[0], 1)
            pool.wait_ge(ident_set[0], 1)
            nc.gpsimd.affine_select(out=k.ident[:, :], in_=k.ident[:, :], compare_op=ALU.not_equal,
                                    fill=1.0, base=0, pattern=[[-1, P]], channel_multiplier=1)\
                .then_inc(ident_set[0], 1)
            nc.gpsimd.memset(k.half[:, :], -0.5)
            nc.gpsimd.memset(k.eps[:, :], LN_EPS)
            nc.gpsimd.memset(k.ones3[:, :], 1.0).then_inc(ones_set[0], 1)
            nc.gpsimd.memset(k.prev_col[:, :], -1.0).then_inc(prev_set[0], 1)

        @block.vector
        def _(dve):
            v = nc.vector
            n = [0]

            def link(ins):
                n[0] += 1
                ins.then_inc(dv[0], 1)
                dve.wait_ge(dv[0], n[0])

            dve.wait_ge(tab_in[0], 9 * 16)
            link(v.tensor_copy(rows_f[:, :, :], rows[:, :, :]))
            link(v.memset(rows_f[0:1, 3, 0:1], -1.0))
            nodes, after, prev = rows_f[:, 1, :], rows_f[:, 2, :], rows_f[:, 3, :]
            v.tensor_tensor(flag[:, :], nodes, prev, ALU.not_equal)
            v.tensor_tensor(k.is_last[:, :], nodes, after, ALU.not_equal)
            link(v.tensor_tensor(k.not_last[:, :], nodes, after, ALU.is_equal))
            v.tensor_scalar(k.cut_first[:, :], flag[:, :], LOW, None, ALU.mult)
            v.tensor_scalar(k.cut_last[:, :], k.is_last[:, :], LOW, None, ALU.mult)
            v.tensor_copy(idx_f[:, 0, :], rows_f[:, 0, :])
            v.tensor_scalar(idx_f[:, 1, :], nodes, float(k.N), None, ALU.is_lt)
            link(v.tensor_scalar(idx_f[:, 2, :], k.not_last[:, :], float(NO_NODE), None, ALU.mult))
            v.tensor_tensor(idx_f[:, 1, :], idx_f[:, 1, :], nodes, ALU.mult)
            link(v.tensor_tensor(idx_f[:, 2, :], idx_f[:, 2, :], nodes, ALU.add))
            dve.wait_ge(tr_ps[0], 1)
            v.tensor_copy(k.src_idx[:, :], k.psum[0][:, 0:T])
            v.tensor_copy(k.dst_idx[:, :], k.psum[1][:, 0:T])
            v.tensor_copy(k.last_idx[:, :], k.psum[2][:, 0:T])
            link(v.tensor_copy(k.dst_col[:, :], k.psum[3][:, 0:T]))

            dve.wait_ge(w_in[0], n_w * 16)
            for c in range(KC):
                v.tensor_copy(lnb_cols[:, c, :], lnb[:, c:c + 1].broadcast_to([P, P]))
            link(v.tensor_copy(betaw[:, :], b1row[:, :]))
            dve.wait_ge(beta_ps[0], 1)
            link(v.tensor_copy(betaw[:, :], k.psum[4][:, :]))
            v.tensor_tensor(k.bias1[:, :], betaw[:, :], b1row[:, :], ALU.add)
            for c in range(KC):
                link(v.tensor_scalar(k.w1[:, c, :], k.w1[:, c, :], lnw[:, c:c + 1], None, ALU.mult))
            for of, to, sign in ((k.w1, k.w1_p, -1.0), (k.w2, k.w2_p, -1.0), (k.mw1, k.mw1_p, 1.0), (k.mw2, k.mw2_p, 1.0)):
                link(v.tensor_scalar(to[0][:, :, :], of[:, :, :], sign, None, ALU.mult))
                link(v.scalar_tensor_tensor(to[1][:, :, :], of[:, :, :], sign, to[0][:, :, :].bitcast(F32),
                                            ALU.mult, ALU.subtract))
            for j in range(2):
                for c in range(KC + 1):
                    of = betaw[:, :] if c == KC else k.w1[:, c, :]
                    to = k.a1_const[:, j * H:(j + 1) * H] if c == KC else k.a1[:, c, j * H:(j + 1) * H]
                    link(v.tensor_tensor(prod[:, :], of, att[:, j, :], ALU.mult))
                    link(v.tensor_reduce(to, prod[:, :].rearrange("p (h c) -> p h c", h=H), AX_X, ALU.add))
            link(v.tensor_tensor(prod[:, 0:D], k.att2[:, 0, :], k.att2[:, 1, :], ALU.add))
            link(v.tensor_tensor(prod[:, 0:D], prod[:, 0:D], b2row[:, :], ALU.mult))
            link(v.tensor_reduce(prod[:, D:D + 1], prod[:, 0:D], AX_X, ALU.add))
            link(v.tensor_scalar(k.att2_const[:, :], prod[:, D:D + 1], -1.0, None, ALU.mult))
            link(v.tensor_copy(bias[:, 0:HC], k.bias1[0:1, :]))
            link(v.tensor_copy(parts[0][:, :], bias[:, :]))
            link(v.tensor_tensor(rest[:, :], bias[:, :], parts[0][:, :], ALU.subtract))
            link(v.tensor_copy(parts[1][:, :], rest[:, :]))
            link(v.tensor_tensor(rest[:, :], rest[:, :], parts[1][:, :], ALU.subtract))
            v.tensor_copy(parts[2][:, :], rest[:, :]).then_inc(col_set[0], 1)

        @block.tensor
        def _(pe):
            pe.wait_ge(ident_set[0], 2)
            pe.wait_ge(dv[0], 5)
            for j in range(3):
                nc.tensor.transpose(k.psum[j][:, 0:T], idx_f[:, j, :], k.ident[0:T, 0:T])
            nc.tensor.transpose(k.psum[3][:, 0:T], rows_f[:, 1, :], k.ident[0:T, 0:T]).then_inc(tr_ps[0], 1)
            pe.wait_ge(dv[0], 7)
            for c in range(KC):
                last = nc.tensor.matmul(k.psum[4][:, :], lnb_cols[:, c, :], k.w1[:, c, :],
                                        start=(c == 0), stop=(c == KC - 1))
            last.then_inc(beta_ps[0], 1)


def norm_sums(dve, sums_done, item, data, stats):
    for r in range(data.shape[1]):
        last = dve.bn_stats(stats[:, r, :], data[:, r, :])
    last.then_inc(sums_done.at(item), 1)


def norm_mean(dve, k, sems, item, stats, mv):
    dve.wait_ge(sems[0].at(item), sems[0].count(item))
    apart(dve, k)
    for r in range(mv.shape[1]):
        last = dve.bn_aggr(mv[:, r, :], stats[:, r, :])
    last.then_inc(sems[1].at(item), 1)


def norm_stats(dve, k, sems, item, data, stats, mv):
    norm_sums(dve, sems[0], item, data, stats)
    norm_mean(dve, k, sems, item, stats, mv)


def norm_rstd(pool, k, sems, item, mv, ve, rstd):
    p, rows = ve.shape
    pool.wait_ge(sems[0].at(item), sems[0].count(item))
    pool.tensor_tensor(ve, mv[:, :, 1], k.eps[0:p, 0:rows], ALU.add)\
        .then_inc(sems[1].at(item), 1)
    pool.wait_ge(sems[1].at(item), sems[1].count(item))
    pool.tensor_tensor(rstd, ve, k.half[0:p, 0:rows], ALU.pow)\
        .then_inc(sems[2].at(item), 1)


def norm_shift(dve, sems, item, mv, rstd, shift):
    dve.wait_ge(sems[0].at(item), sems[0].count(item))
    dve.scalar_tensor_tensor(shift, mv[:, :, 0], -1.0, rstd, ALU.mult, ALU.mult)\
        .then_inc(sems[1].at(item), 1)


def norm_on_act(act, shift_set, item, data, rstd, shift, to):
    act.wait_ge(shift_set.at(item), shift_set.count(item))
    for r in range(data.shape[1]):
        last = act.activation(to[:, r, :], data[:, r, :], ACT.Identity, bias=shift[:, r:r + 1],
                              scale=rstd[:, r:r + 1])
    return last


def norm_apply(dve, rstd_done, item, data, mv, rstd, to):
    dve.wait_ge(rstd_done.at(item), rstd_done.count(item))
    for r in range(data.shape[1]):
        last = dve.tensor_scalar(to[:, r, :], data[:, r, :], mv[:, r, 0:1], rstd[:, r:r + 1],
                                 ALU.subtract, ALU.mult)
    return last


def gat1_scores(nc, k, x):
    H, D, KC, T = k.H, k.D, k.KC, k.T
    PER = 4
    ctx, sb, sem = phase(nc, "gat1_scores")
    with ctx:
        idx_set, rows_in = sem("idx_set"), sem("rows_in", PER)
        st_done, mv_done, ve_done, rs_done = sem("st_done"), sem("mv_done"), sem("ve_done"), sem("rs_done")
        normed, turned, ht_set, ht_out, own_out = (
            sem("normed"), sem("turned"), sem("ht_set"), sem("ht_out", PER), sem("own_out", PER))
        prods, terms_set = sem("prods"), sem("terms_set")

        def ring(name, shape, dt=F32):
            return [sb(f"{name}{s}", shape, dt) for s in range(PER)]

        idx = [ring(f"idx_{n}", [P, 1], I32) for n in ("src", "dst")]
        rows, xn = ring("rows", [P, 2, D]), ring("xn", [P, 2, D])
        ht = ring("ht", [P, 2, KC, P])
        stats, mv, ve, rstd = ring("stats", [P, 2, 6]), ring("mv", [P, 2, 2]), ring("ve", [P, 2]), ring("rstd", [P, 2])
        turn_ps = k.psum[0:2]
        prod_ps = k.psum[2:4]
        block = ctx.enter_context(nc.Block())

        @block.gpsimd
        def _(pool):
            def gather(item):
                s = item.slot(PER)
                if item.follows(PER):
                    pool.wait_ge(rows_in.at(item - PER), rows_in.count(item - PER, 32))
                    pool.wait_ge(normed.at(item - PER), normed.count(item - PER))
                    pool.wait_ge(own_out.at(item - PER), own_out.count(item - PER, 16))
                pool.tensor_copy(idx[0][s][:, :], k.src_idx[:, bass.ds(item.index(), 1)])
                pool.tensor_copy(idx[1][s][:, :], k.dst_idx[:, bass.ds(item.index(), 1)])\
                    .then_inc(idx_set.at(item), 1)
                pool.wait_ge(idx_set.at(item), idx_set.count(item))
                apart(pool, k)
                for j in range(2):
                    pool.indirect_dma_start(
                        out=rows[s][:, j, :], out_offset=None, in_=x[:, :],
                        in_offset=bass.IndirectOffsetOnAxis(idx[j][s][:, :], 0),
                        bounds_check=k.N - 1, oob_is_err=True)\
                        .then_inc(rows_in.at(item), 16)

            def norm(item):
                s = item.slot(PER)
                norm_rstd(pool, k, (mv_done, ve_done, rs_done), item, mv[s], ve[s][:, :], rstd[s][:, :])

            each_item(pool, T, PER, (0, gather), (2, norm))

        @block.vector
        def _(dve):
            def statistics(item):
                s = item.slot(PER)
                dve.wait_ge(rows_in.at(item), rows_in.count(item, 32))
                norm_stats(dve, k, (st_done, mv_done), item, rows[s], stats[s], mv[s])

            def normalise(item):
                s = item.slot(PER)
                if item.follows(PER):
                    dve.wait_ge(turned.at(item - PER), turned.count(item - PER))
                norm_apply(dve, rs_done, item, rows[s], mv[s], rstd[s], xn[s])\
                    .then_inc(normed.at(item), 1)

            def terms(item):
                dve.wait_ge(prods.at(item), prods.count(item))
                to = k.terms1[:, bass.ds(item.index(), 1), :, :].rearrange("p t j h -> p (t j) h")
                const = k.a1_const[:, :].unsqueeze(1).broadcast_to([P, 2, 2 * H])
                dve.tensor_tensor(to, prod_ps[item.slot(2)][:, 0:4 * H].rearrange("p (j h) -> p j h", j=2),
                                  const, ALU.add)\
                    .then_inc(terms_set.at(item), 1)

            each_item(dve, T, PER, (0, statistics), (1, normalise), (3, terms))

        @block.tensor
        def _(pe):
            def turn(item):
                s, b = item.slot(PER), item.slot(2)
                pe.wait_ge(normed.at(item), normed.count(item))
                if item.follows(2):
                    pe.wait_ge(ht_set.at(item - 2), ht_set.count(item - 2))
                for j in range(2):
                    for c in range(KC):
                        last = pe.transpose(turn_ps[b][:, (j * KC + c) * P:(j * KC + c + 1) * P],
                                            xn[s][:, j, c * P:(c + 1) * P], k.ident[:, :])
                last.then_inc(turned.at(item), 1)

            def products(item):
                s, b = item.slot(PER), item.slot(2)
                pe.wait_ge(ht_set.at(item), ht_set.count(item))
                if item.follows(2):
                    pe.wait_ge(terms_set.at(item - 2), terms_set.count(item - 2))
                for j in range(2):
                    for c in range(KC):
                        last = pe.matmul(prod_ps[b][:, j * 2 * H:(j + 1) * 2 * H], ht[s][:, j, c, :],
                                         k.a1[:, c, :], start=(c == 0), stop=(c == KC - 1))
                last.then_inc(prods.at(item), 1)

            each_item(pe, T, PER, (0, turn), (1, products))

        @block.scalar
        def _(act):
            def copy_turned(item):
                s, b = item.slot(PER), item.slot(2)
                act.wait_ge(turned.at(item), turned.count(item))
                if item.follows(PER):
                    act.wait_ge(ht_out.at(item - PER), ht_out.count(item - PER, 16))
                    act.wait_ge(prods.at(item - PER), prods.count(item - PER))
                act.activation(ht[s][:, :, :, :].rearrange("p j c e -> p (j c e)"), turn_ps[b][:, :], ACT.Copy)\
                    .then_inc(ht_set.at(item), 1)

            each_item(act, T, PER, (0, copy_turned))

        @block.sync
        def _(sp):
            def store_own(item):
                sp.wait_ge(rows_in.at(item), rows_in.count(item, 32))
                sp.dma_start(k.x_own_dram[bass.ds(item.index(), 1), :, :].rearrange("t p d -> (t p) d"),
                             rows[item.slot(PER)][:, 1, :])\
                    .then_inc(own_out.at(item), 16)

            def store_turned(item):
                s = item.slot(PER)
                sp.wait_ge(ht_set.at(item), ht_set.count(item))
                sp.dma_start(k.ht_dram[bass.ds(item.index(), 1), :, :].rearrange("t p n -> (t p) n"),
                             ht[s][:, :, :, :].rearrange("p j c e -> p (j c e)"))\
                    .then_inc(ht_out.at(item), 16)

            each_item(sp, T, PER, (2, store_turned), (0, store_own))
            for back in range(PER):
                end = Item(None, T - 1 - back, PER)
                sp.wait_ge(ht_out.at(end), ht_out.count(end, 16))
                sp.wait_ge(own_out.at(end), own_out.count(end, 16))


class Link:

    def __init__(self, dve, sem):
        self.dve, self.sem, self.n = dve, sem, 0

    def __call__(self, ins):
        self.n += 1
        ins.then_inc(self.sem[0], 1)
        self.dve.wait_ge(self.sem[0], self.n)


class Segments:

    def __init__(self, k, lines, sb, sem, ps_tile, ps_back):
        T = k.T
        self.k, self.lines, self.ps_tile, self.ps_back = k, lines, ps_tile, ps_back
        self.ends_set, self.ends_turned = sem("ends_set"), sem("ends_turned")
        self.carry_set, self.carry_turned = sem("carry_set"), sem("carry_turned")
        self.ends = sb("ends", [T, 2, lines])
        self.cut_t = sb("cut_t", [lines, T])
        self.carry_t = sb("carry_t", [lines, T + 1])
        self.low = sb("low", [T, 1])
        self.carry = sb("carry", [T, lines])
        self.scans = 0

    def scan(self, dve, link, cut, values, into, ops, start, back):
        T, lines = self.k.T, self.lines
        self.scans += 1

        def way(ap):
            return ap[:, ::-1] if back else ap

        for h in range(lines):
            last = dve.tensor_tensor_scan(way(into[:, h, :]), way(cut), way(values[:, h, :]), start, *ops)
        dve.tensor_reduce(self.low[:, :], cut, AX_X, ALU.min)
        link(dve.memset(self.carry_t[:, :], start))
        dve.tensor_copy(self.ends[:, 0, :], into[:, :, 0 if back else P - 1])
        dve.tensor_copy(self.ends[:, 1, :], self.low[:, 0:1].broadcast_to([T, lines])).then_inc(self.ends_set[0], 1)
        dve.wait_ge(self.ends_turned[0], self.scans)
        link(dve.tensor_copy(self.cut_t[:, :], self.ps_tile[0:lines, P:P + T]))
        to = self.carry_t[:, 0:T] if back else self.carry_t[:, 1:T + 1]
        dve.tensor_tensor_scan(way(to), way(self.cut_t[:, :]), way(self.ps_tile[0:lines, 0:T]), start, *ops)\
            .then_inc(self.carry_set[0], 1)
        dve.wait_ge(self.carry_turned[0], self.scans)
        link(dve.tensor_copy(self.carry[:, :], self.ps_back[0:T, 0:lines]))
        for h in range(lines):
            last = dve.tensor_tensor_scan(way(into[:, h, :]), way(cut), way(values[:, h, :]),
                                          self.carry[:, h:h + 1], *ops)
        link(last)

    def turn(self, pe, scans, backs):
        k, T, lines = self.k, self.k.T, self.lines
        for n in range(scans):
            pe.wait_ge(self.ends_set[0], n + 1)
            pe.transpose(self.ps_tile[0:lines, 0:T], self.ends[:, 0, :], k.ident[0:T, 0:T])
            pe.transpose(self.ps_tile[0:lines, P:P + T], self.ends[:, 1, :], k.ident[0:T, 0:T])\
                .then_inc(self.ends_turned[0], 1)
            pe.wait_ge(self.carry_set[0], n + 1)
            of = self.carry_t[:, 1:T + 1] if backs[n] else self.carry_t[:, 0:T]
            pe.transpose(self.ps_back[0:T, 0:lines], of, k.ident[0:lines, 0:lines])\
                .then_inc(self.carry_turned[0], 1)


def gat1_softmax(nc, k):
    H, T = k.H, k.T
    HB = 4
    ctx, sb, sem = phase(nc, "gat1_softmax")
    with ctx:
        link_sem, raw_set, raw_turned = sem("link"), sem("raw_set"), sem("raw_turned")
        maxima_turned, shifted, exps_set = sem("maxima_turned"), sem("shifted"), sem("exps_set")
        raw = sb("raw", [P, 2, H, T])
        scores, run_max, maxima = (sb(n, [T, H, P]) for n in ("scores", "run_max", "maxima"))
        top = sb("top", [P, H, T])
        seg = Segments(k, H, sb, sem, k.psum[2], k.psum[3])
        block = ctx.enter_context(nc.Block())

        @block.vector
        def _(dve):
            link = Link(dve, link_sem)
            for j in range(2):
                last = dve.tensor_tensor(raw[:, j, :, :], k.terms1[:, :, j, 0:H].rearrange("p t h -> p h t"),
                                         k.terms1[:, :, 1, H:2 * H].rearrange("p t h -> p h t"), ALU.add)
            link(last)
            flat = raw[:, :, :, :].rearrange("p j h t -> p (j h t)")
            dve.scalar_tensor_tensor(flat, flat, NEG_SLOPE, flat, ALU.mult, ALU.max).then_inc(raw_set[0], 1)
            dve.wait_ge(raw_turned[0], 1)
            for b in range(H // HB):
                last = dve.tensor_copy(scores[:, HB * b:HB * (b + 1), :].rearrange("t h e -> t (h e)"),
                                       k.psum[b][0:T, :])
            link(last)
            seg.scan(dve, link, k.cut_first[:, :], scores, run_max, (ALU.add, ALU.max), LOW, False)
            seg.scan(dve, link, k.cut_last[:, :], run_max, maxima, (ALU.add, ALU.max), LOW, True)
            dve.wait_ge(maxima_turned[0], 1)
            for b in range(H // HB):
                of = k.psum[4 + b][:, :].rearrange("p (h e) -> p h e", h=HB)[:, :, 0:T]
                last = dve.tensor_tensor(top[:, HB * b:HB * (b + 1), :], of, raw[:, 1, HB * b:HB * (b + 1), :], ALU.max)
            link(last)
            for j in range(2):
                last = dve.tensor_tensor(raw[:, j, :, :], raw[:, j, :, :], top[:, :, :], ALU.subtract)
            last.then_inc(shifted[0], 1)

        @block.tensor
        def _(pe):
            pe.wait_ge(raw_set[0], 1)
            for h in range(H):
                last = pe.transpose(k.psum[h // HB][0:T, h % HB * P:(h % HB + 1) * P], raw[:, 0, h, :], k.ident[:, :])
            last.then_inc(raw_turned[0], 1)
            seg.turn(pe, 2, (False, True))
            pe.wait_ge(link_sem[0], 2 + 2 * 4)
            for h in range(H):
                last = pe.transpose(k.psum[4 + h // HB][:, h % HB * P:h % HB * P + T], maxima[:, h, :], k.ident[0:T, 0:T])
            last.then_inc(maxima_turned[0], 1)

        @block.scalar
        def _(act):
            act.wait_ge(shifted[0], 1)
            for to, j in ((k.p1, 0), (k.ps1, 1)):
                act.activation(to[:, :, :].rearrange("p t h -> p h t"), raw[:, j, :, :], ACT.Exp).then_inc(exps_set[0], 1)
            act.wait_ge(exps_set[0], 2)


def same_and_carry(dve, item, k, dst_row, same, carry):
    at = bass.ds(item.index(), 1)
    dve.tensor_scalar(same, dst_row, k.dst_col[:, at], None, ALU.is_equal)
    return dve.tensor_scalar(carry, dst_row, k.prev_col[:, at], None, ALU.is_equal)


def gat1_messages(nc, k):
    H, C, HC, D, KC, MC, T = k.H, k.C, k.HC, k.D, k.KC, k.MC, k.T
    PER = 4
    ctx, sb, sem = phase(nc, "gat1_messages")
    with ctx:
        ht_in, same_set, ht_hi_set, ht_lo_set = sem("ht_in", PER), sem("same_set"), sem("ht_hi_set"), sem("ht_lo_set")
        h_ps, msg_set, msg_hi_set, msg_lo_set, own_set = (
            sem("h_ps"), sem("msg_set"), sem("msg_hi_set"), sem("msg_lo_set"), sem("own_set"))
        sum_ps, sum_set, inv_set, zero_set, den_set = (
            sem("sum_ps"), sem("sum_set"), sem("inv_set"), sem("zero_set"), sem("den_set"))
        whole_set, scaled, y_set, exp_set, neg_set, elu_set = (
            sem("whole_set"), sem("scaled"), sem("y_set"), sem("exp_set"), sem("neg_set"), sem("elu_set"))
        turned, et_hi_set, et_lo_set, fix_ps, fix_set, fix_out = (
            sem("turned"), sem("et_hi_set"), sem("et_lo_set"), sem("fix_ps"), sem("fix_set"), sem("fix_out", PER))
        last_idx_set, rows_out = sem("last_idx_set"), sem("rows_out", PER)
        sum_hi_set, sum_lo_set = sem("sum_hi_set"), sem("sum_lo_set")

        def ring(name, shape, dt=F32):
            return [sb(f"{name}{s}", shape, dt) for s in range(PER)]

        last_idx = ring("last_idx", [P, 1], I32)
        ht = ring("ht", [P, 2, KC, P])
        ht_hi, ht_lo = (ring(n, [P, 2, KC, P], F32R) for n in ("ht_hi", "ht_lo"))
        dst_row = ring("dst_row", [P, P])
        same, carry = (ring(n, [P, P], F32R) for n in ("same", "carry"))
        msg, sums = ring("msg", [P, HC + H]), ring("sums", [P, HC + H])
        msg_hi, msg_lo, sums_hi, sums_lo = (ring(n, [P, HC], F32R) for n in ("msg_hi", "msg_lo", "sums_hi", "sums_lo"))
        inv, y, neg = ring("inv", [P, H]), ring("y", [P, HC]), ring("neg", [P, HC])
        et_hi, et_lo = (ring(n, [P, MC, P], F32R) for n in ("et_hi", "et_lo"))
        fix = ring("fix", [P, D])
        src_ps, dst_ps, psum_ps, turn_ps = k.psum[0:4]
        msum_ps, w2_ps = k.psum[4:6], k.psum[6:8]
        block = ctx.enter_context(nc.Block())

        def heads(ap):
            return ap.rearrange("p (h c) -> p h c", h=H)

        def per_head(ap):
            return ap.unsqueeze(2).broadcast_to([P, H, C])

        @block.sync
        def _(sp):
            def load(item):
                s = item.slot(PER)
                if item.follows(PER):
                    sp.wait_ge(ht_hi_set.at(item - PER), ht_hi_set.count(item - PER))
                    sp.wait_ge(ht_lo_set.at(item - PER), ht_lo_set.count(item - PER))
                    sp.wait_ge(same_set.at(item - PER), same_set.count(item - PER))
                t = bass.ds(item.index(), 1)
                sp.dma_start(ht[s][:, :, :, :].rearrange("p j c e -> p (j c e)"),
                             k.ht_dram[t, :, :].rearrange("t p n -> (t p) n"))\
                    .then_inc(ht_in.at(item), 16)
                sp.dma_start(dst_row[s][:, :], k.dst_dram[t, :].broadcast_to([P, P]))\
                    .then_inc(ht_in.at(item), 16)

            def store(item):
                sp.wait_ge(fix_set.at(item), fix_set.count(item))
                sp.dma_start(k.fix_dram[bass.ds(item.index(), 1), :, :].rearrange("t p d -> (t p) d"),
                             fix[item.slot(PER)][:, :])\
                    .then_inc(fix_out.at(item), 16)

            each_item(sp, T, PER, (0, load), (7, store))
            for back in range(PER):
                sp.wait_ge(fix_out.at(Item(None, T - 1 - back, PER)), fix_out.count(Item(None, T - 1 - back, PER), 16))

        @block.tensor
        def _(pe):
            def turn(item):
                s = item.slot(PER)
                pe.wait_ge(elu_set.at(item), elu_set.count(item))
                if item.follows(1):
                    pe.wait_ge(et_hi_set.at(item - 1), et_hi_set.count(item - 1))
                    pe.wait_ge(et_lo_set.at(item - 1), et_lo_set.count(item - 1))
                for m in range(MC):
                    last = pe.transpose(turn_ps[:, m * P:(m + 1) * P], y[s][:, m * P:(m + 1) * P], k.ident[:, :])
                last.then_inc(turned.at(item), 1)

            def hidden(item):
                s = item.slot(PER)
                pe.wait_ge(ht_hi_set.at(item), ht_hi_set.count(item))
                pe.wait_ge(ht_lo_set.at(item), ht_lo_set.count(item))
                if item.follows(1):
                    pe.wait_ge(own_set.at(item - 1), own_set.count(item - 1))
                for j, ps in enumerate((src_ps, dst_ps)):
                    for c in range(KC):
                        pe.matmul(ps[:, :], ht_hi[s][:, j, c, :], k.w1_p[0][:, c, :], start=(c == 0), stop=False)
                        pe.matmul(ps[:, :], ht_hi[s][:, j, c, :], k.w1_p[1][:, c, :], start=False, stop=False)
                        last = pe.matmul(ps[:, :], ht_lo[s][:, j, c, :], k.w1_p[0][:, c, :], start=False,
                                         stop=(c == KC - 1))
                last.then_inc(h_ps.at(item), 1)

            def sum_up(item):
                s = item.slot(PER)
                before = sums[(s + PER - 1) % PER]
                to = msum_ps[item.slot(2)][:, :]
                pe.wait_ge(msg_hi_set.at(item), msg_hi_set.count(item))
                pe.wait_ge(msg_lo_set.at(item), msg_lo_set.count(item))
                if item.follows(2):
                    pe.wait_ge(sum_hi_set.at(item - 2), sum_hi_set.count(item - 2))
                pe.matmul(to, same[s][:, :], msg_hi[s][:, :], start=True, stop=False)
                pe.matmul(to, same[s][:, :], msg_lo[s][:, :], start=False, stop=False)
                if not item.follows(1):
                    pe.wait_ge(zero_set[0], 2)
                if item.follows(1):
                    pe.wait_ge(sum_set.at(item - 1), sum_set.count(item - 1))
                    pe.wait_ge(sum_lo_set.at(item - 1), sum_lo_set.count(item - 1))
                pe.matmul(to, carry[s][:, :], sums_hi[(s + PER - 1) % PER][:, :], start=False, stop=False)
                pe.matmul(to, carry[s][:, :], sums_lo[(s + PER - 1) % PER][:, :], start=False, stop=True)
                pe.matmul(psum_ps[:, 0:H], same[s][:, :].bitcast(F32), msg[s][:, HC:HC + H], start=True, stop=False)
                pe.matmul(psum_ps[:, 0:H], carry[s][:, :].bitcast(F32), before[:, HC:HC + H], start=False, stop=True)\
                    .then_inc(sum_ps.at(item), 1)

            def second(item):
                s = item.slot(PER)
                to = w2_ps[item.slot(2)][:, 0:D]
                pe.wait_ge(et_hi_set.at(item), et_hi_set.count(item))
                pe.wait_ge(et_lo_set.at(item), et_lo_set.count(item))
                if item.follows(2):
                    pe.wait_ge(fix_set.at(item - 2), fix_set.count(item - 2))
                pe.matmul(to, k.ones3[:, 0:P], k.bias_parts[:, HC:HC + D], start=True, stop=False)
                for m in range(MC):
                    pe.matmul(to, et_hi[s][:, m, :], k.w2_p[0][:, m, :], start=False, stop=False)
                    pe.matmul(to, et_hi[s][:, m, :], k.w2_p[1][:, m, :], start=False, stop=False)
                    last = pe.matmul(to, et_lo[s][:, m, :], k.w2_p[0][:, m, :], start=False, stop=(m == MC - 1))
                last.then_inc(fix_ps.at(item), 1)

            each_item(pe, T, PER, (3, turn), (0, hidden), (3, second), (1, sum_up))

        @block.vector
        def _(dve):
            dve.memset(sums[PER - 1][:, :], 0.0)\
                .then_inc(zero_set[0], 1)
            dve.wait_ge(zero_set[0], 1)
            dve.tensor_copy(sums_hi[PER - 1][:, :], sums[PER - 1][:, 0:HC])
            dve.tensor_copy(sums_lo[PER - 1][:, :], sums[PER - 1][:, 0:HC])\
                .then_inc(zero_set[0], 1)

            def whole(item):
                s = item.slot(PER)
                ps_t = k.ps1[:, bass.ds(item.index(), 1), :].rearrange("p t h -> p (t h)")
                dve.wait_ge(sum_set.at(item), sum_set.count(item))
                dve.tensor_tensor(inv[s][:, :], sums[s][:, HC:HC + H], ps_t, ALU.add)\
                    .then_inc(den_set.at(item), 1)
                dve.tensor_tensor(y[s][:, :], y[s][:, :], sums[s][:, 0:HC], ALU.add)\
                    .then_inc(whole_set.at(item), 1)

            def divide(item):
                s = item.slot(PER)
                dve.wait_ge(den_set.at(item), den_set.count(item))
                dve.reciprocal(inv[s][:, :], inv[s][:, :])\
                    .then_inc(inv_set.at(item), 1)
                dve.wait_ge(whole_set.at(item), whole_set.count(item))
                dve.wait_ge(inv_set.at(item), inv_set.count(item))
                dve.tensor_tensor(heads(y[s][:, :]), heads(y[s][:, :]), per_head(inv[s][:, :]), ALU.mult)\
                    .then_inc(scaled.at(item), 1)
                dve.wait_ge(scaled.at(item), scaled.count(item))
                dve.tensor_tensor(y[s][:, :], y[s][:, :], k.bias1[:, :], ALU.subtract)\
                    .then_inc(y_set.at(item), 1)

            def lo_of_elu(item):
                s = item.slot(PER)
                dve.wait_ge(et_hi_set.at(item), et_hi_set.count(item))
                if item.follows(PER):
                    dve.wait_ge(fix_ps.at(item - PER), fix_ps.count(item - PER))
                dve.tensor_tensor(et_lo[s][:, :, :].rearrange("p m e -> p (m e)"), turn_ps[:, :],
                                  et_hi[s][:, :, :].rearrange("p m e -> p (m e)").bitcast(F32), ALU.subtract)\
                    .then_inc(et_lo_set.at(item), 1)

            def messages(item):
                s = item.slot(PER)
                t = bass.ds(item.index(), 1)
                p_t = k.p1[:, t, :].rearrange("p t h -> p (t h)")
                ps_t = k.ps1[:, t, :].rearrange("p t h -> p (t h)")
                dve.wait_ge(ht_in.at(item), ht_in.count(item, 32))
                if item.follows(PER):
                    dve.wait_ge(sum_ps.at(item - PER), sum_ps.count(item - PER))
                same_and_carry(dve, item, k, dst_row[s][:, :], same[s][:, :], carry[s][:, :])\
                    .then_inc(same_set.at(item), 1)
                dve.tensor_copy(msg[s][:, HC:HC + H], p_t)
                dve.wait_ge(h_ps.at(item), h_ps.count(item))
                dve.tensor_tensor(heads(msg[s][:, 0:HC]), heads(src_ps[:, :]), per_head(p_t), ALU.mult)\
                    .then_inc(msg_set.at(item), 1)
                if item.follows(PER):
                    dve.wait_ge(turned.at(item - PER), turned.count(item - PER))
                dve.tensor_tensor(heads(y[s][:, :]), heads(dst_ps[:, :]), per_head(ps_t), ALU.mult)\
                    .then_inc(own_set.at(item), 1)

            def elu(item):
                s = item.slot(PER)
                dve.wait_ge(neg_set.at(item), neg_set.count(item))
                dve.tensor_tensor(y[s][:, :], y[s][:, :], neg[s][:, :], ALU.min)\
                    .then_inc(elu_set.at(item), 1)

            each_item(dve, T, PER, (2, whole), (3, lo_of_elu), (2, divide), (0, messages), (2, elu))

        @block.gpsimd
        def _(pool):
            def lo_of_rows(item):
                s = item.slot(PER)
                pool.wait_ge(ht_hi_set.at(item), ht_hi_set.count(item))
                if item.follows(PER):
                    pool.wait_ge(h_ps.at(item - PER), h_ps.count(item - PER))
                pool.tensor_tensor(ht_lo[s][:, :, :, :], ht[s][:, :, :, :], ht_hi[s][:, :, :, :].bitcast(F32),
                                   ALU.subtract).then_inc(ht_lo_set.at(item), 1)

            def lo_of_sums(item):
                s = item.slot(PER)
                pool.wait_ge(sum_hi_set.at(item), sum_hi_set.count(item))
                if item.follows(PER):
                    pool.wait_ge(sum_ps.at(item - (PER - 1)), sum_ps.count(item - (PER - 1)))
                pool.tensor_tensor(sums_lo[s][:, :], sums[s][:, 0:HC], sums_hi[s][:, :].bitcast(F32), ALU.subtract)\
                    .then_inc(sum_lo_set.at(item), 1)

            def lo_of_messages(item):
                s = item.slot(PER)
                pool.wait_ge(msg_hi_set.at(item), msg_hi_set.count(item))
                if item.follows(PER):
                    pool.wait_ge(sum_ps.at(item - PER), sum_ps.count(item - PER))
                pool.tensor_tensor(msg_lo[s][:, :], msg[s][:, 0:HC], msg_hi[s][:, :].bitcast(F32), ALU.subtract)\
                    .then_inc(msg_lo_set.at(item), 1)

            def scatter(item):
                s = item.slot(PER)
                if item.follows(PER):
                    pool.wait_ge(rows_out.at(item - PER), rows_out.count(item - PER, 16))
                pool.tensor_copy(last_idx[s][:, :], k.last_idx[:, bass.ds(item.index(), 1)])\
                    .then_inc(last_idx_set.at(item), 1)
                pool.wait_ge(last_idx_set.at(item), last_idx_set.count(item))
                pool.wait_ge(fix_set.at(item), fix_set.count(item))
                apart(pool, k)
                pool.indirect_dma_start(out=k.h2_dram[:, :], out_offset=bass.IndirectOffsetOnAxis(last_idx[s][:, :], 0),
                                        in_=fix[s][:, :], in_offset=None, bounds_check=k.N - 1,
                                        oob_is_err=False)\
                    .then_inc(rows_out.at(item), 16)

            each_item(pool, T, PER, (3, lo_of_sums), (5, scatter), (0, lo_of_rows), (1, lo_of_messages))
            for back in range(PER):
                pool.wait_ge(rows_out.at(Item(None, T - 1 - back, PER)), rows_out.count(Item(None, T - 1 - back, PER), 16))

        @block.scalar
        def _(act):
            def hi_of_rows(item):
                s = item.slot(PER)
                act.wait_ge(ht_in.at(item), ht_in.count(item, 32))
                if item.follows(PER):
                    act.wait_ge(h_ps.at(item - PER), h_ps.count(item - PER))
                act.activation(ht_hi[s][:, :, :, :], ht[s][:, :, :, :], ACT.Copy)\
                    .then_inc(ht_hi_set.at(item), 1)

            def copy_sums(item):
                s = item.slot(PER)
                act.wait_ge(sum_ps.at(item), sum_ps.count(item))
                if item.follows(PER):
                    act.wait_ge(whole_set.at(item - PER), whole_set.count(item - PER))
                    act.wait_ge(sum_lo_set.at(item - PER), sum_lo_set.count(item - PER))
                act.activation(sums[s][:, 0:HC], msum_ps[item.slot(2)][:, :], ACT.Copy)
                act.activation(sums[s][:, HC:HC + H], psum_ps[:, 0:H], ACT.Copy)\
                    .then_inc(sum_set.at(item), 1)
                act.activation(sums_hi[s][:, :], msum_ps[item.slot(2)][:, :], ACT.Copy)\
                    .then_inc(sum_hi_set.at(item), 1)

            def hi_of_elu(item):
                s = item.slot(PER)
                act.wait_ge(turned.at(item), turned.count(item))
                if item.follows(PER):
                    act.wait_ge(fix_ps.at(item - PER), fix_ps.count(item - PER))
                act.activation(et_hi[s][:, :, :].rearrange("p m e -> p (m e)"), turn_ps[:, :], ACT.Copy)\
                    .then_inc(et_hi_set.at(item), 1)

            def negative(item):
                s = item.slot(PER)
                act.wait_ge(y_set.at(item), y_set.count(item))
                if item.follows(PER):
                    act.wait_ge(elu_set.at(item - PER), elu_set.count(item - PER))
                act.activation(neg[s][:, :], y[s][:, :], ACT.Exp, scale=-1.0)\
                    .then_inc(exp_set.at(item), 1)
                act.wait_ge(exp_set.at(item), exp_set.count(item))
                act.activation(neg[s][:, :], neg[s][:, :], ACT.Relu, bias=1.0, scale=-1.0)\
                    .then_inc(neg_set.at(item), 1)

            def hi_of_messages(item):
                s = item.slot(PER)
                act.wait_ge(msg_set.at(item), msg_set.count(item))
                if item.follows(PER):
                    act.wait_ge(sum_ps.at(item - PER), sum_ps.count(item - PER))
                act.activation(msg_hi[s][:, :], msg[s][:, 0:HC], ACT.Copy)\
                    .then_inc(msg_hi_set.at(item), 1)

            def copy_fix(item):
                s = item.slot(PER)
                act.wait_ge(fix_ps.at(item), fix_ps.count(item))
                if item.follows(PER):
                    act.wait_ge(fix_out.at(item - PER), fix_out.count(item - PER, 16))
                    act.wait_ge(rows_out.at(item - PER), rows_out.count(item - PER, 16))
                act.activation(fix[s][:, :], w2_ps[item.slot(2)][:, 0:D], ACT.Copy)\
                    .then_inc(fix_set.at(item), 1)

            each_item(act, T, PER, (3, copy_sums), (4, hi_of_elu), (0, hi_of_rows), (3, negative),
                             (1, hi_of_messages), (4, copy_fix))


def dense(nc, k, x, out):
    N, D, HC, KC, MC = k.N, k.D, k.HC, k.KC, k.MC
    PER = 6
    R = 2
    G = R * P
    full = N // G
    rest = (N - full * G) // R
    groups = full + 1
    MH = MC // 2
    assert rest * R == N - full * G and 0 < rest < P
    ctx, sb, sem = phase(nc, "dense")
    with ctx:
        x_in, bias_turned, bias_set = sem("x_in", PER), sem("bias_turned"), sem("bias_set")
        st = {n: tuple(sem(f"{n}_{m}") for m in ("st", "mv", "ve", "rstd", "shift")) for n in "xyvs"}
        xn_set, xn_turned, xt_hi_set, xt_set = sem("xn_set"), sem("xn_turned"), sem("xt_hi_set"), sem("xt_set")
        h_ps, exp_set, neg_set, elu_set, elu_hi_set, elu_lo_set = (
            [sem(f"{n}{j}") for j in range(2)]
            for n in ("h_ps", "exp_set", "neg_set", "elu_set", "elu_hi_set", "elu_lo_set"))
        h2_ps, h2_set, y_set, h2_out = sem("h2_ps"), sem("h2_set"), sem("y_set"), sem("h2_out", 3)
        x1_set, x1_out, x1_turned, zt_hi_set, zt_set, x1b_set = (
            sem("x1_set"), sem("x1_out", 3), sem("x1_turned"), sem("zt_hi_set"), sem("zt_set"), sem("x1b_set"))
        hid_ps, hid_hi_set, hid_set, mlp_ps, v_set, a_set, s_set, o_set, o_out = (
            sem("hid_ps"), sem("hid_hi_set"), sem("hid_set"), sem("mlp_ps"), sem("v_set"), sem("a_set"),
            sem("s_set"), sem("o_set"), sem("o_out", 3))

        def ring(name, slots, shape, dt=F32):
            return [sb(f"{name}{s}", shape, dt) for s in range(slots)]

        b1_col = sb("b1_col", [P, MC])
        xs = ring("x", 6, [P, R, D])
        y, v, h2 = (ring(n, 3, [P, R, D]) for n in ("y", "v", "h2"))
        xn, x1b = (ring(n, 2, [P, R, D]) for n in ("xn", "x1b"))
        xt_hi, xt_lo, zt_hi, zt_lo, hid_hi, hid_lo = (
            ring(n, 2, [P, KC, R, P], F32R) for n in ("xt_hi", "xt_lo", "zt_hi", "zt_lo", "hid_hi", "hid_lo"))
        elu = ring("elu", 2, [P, MC, R, P])
        elu_hi, elu_lo = (ring(n, 2, [P, MC, R, P], F32R) for n in ("elu_hi", "elu_lo"))
        stats = {n: ring(f"{n}_stats", 3, [P, R, 6]) for n in "xyvs"}
        mv = {n: ring(f"{n}_mv", 3, [P, R, 2]) for n in "xyvs"}
        ve, rstd, shift = ({n: ring(f"{n}_{m}", 3, [P, R]) for n in "xyvs"} for m in ("ve", "rstd", "shift"))
        xt_ps, zt_ps, h2_bank, hid_bank, mlp_bank = k.psum[0], k.psum[1], k.psum[4], k.psum[5], k.psum[6]
        h_bank = k.psum[2:4]
        block = ctx.enter_context(nc.Block())

        def each_group(engine, *stages):
            behind = max(lag for lag, _ in stages)

            def step(i, c):
                for lag, stage in stages:
                    if i is not None or 0 <= c - lag < groups:
                        stage(Item(i, c - lag, PER), rest if i is None and c - lag == full else P)

            run(engine, groups + behind, PER, (behind + 2 * PER - 1) // PER * PER, (full - 1) // PER * PER, step)

        def rows(a, item, p):
            return a[bass.ds(item.index() * G, R * p), :].rearrange("(p r) d -> p r d", r=R)

        def flat(a, p):
            return a[0:p, :, :].rearrange("p r d -> p (r d)")

        def turned(bank, chunks):
            return bank[:, :].rearrange("q (m r p) -> q m r p", m=chunks, r=R)

        @block.sync
        def _(sp):
            def load(item, p):
                if item.follows(6):
                    sp.wait_ge(y_set.at(item - 6), y_set.count(item - 6))
                sp.dma_start(xs[item.slot(6)][0:p, :, :], rows(x, item, p)).then_inc(x_in.at(item), 16)

            def store_h2(item, p):
                sp.wait_ge(h2_set.at(item), h2_set.count(item))
                sp.dma_start(rows(k.h2_dram, item, p), h2[item.slot(3)][0:p, :, :]).then_inc(h2_out.at(item), 16)

            def store_x1(item, p):
                sp.wait_ge(x1_set.at(item), x1_set.count(item))
                sp.dma_start(rows(k.x1_dram, item, p), y[item.slot(3)][0:p, :, :]).then_inc(x1_out.at(item), 16)

            def store_out(item, p):
                sp.wait_ge(o_set.at(item), o_set.count(item))
                sp.dma_start(rows(out, item, p), v[item.slot(3)][0:p, :, :]).then_inc(o_out.at(item), 16)

            each_group(sp, (0, load), (6, store_h2), (6, store_x1), (9, store_out))
            for back in range(3):
                last = Item(None, groups - 1 - back, PER)
                sp.wait_ge(h2_out.at(last), h2_out.count(last, 16))
                sp.wait_ge(x1_out.at(last), x1_out.count(last, 16))
                sp.wait_ge(o_out.at(last), o_out.count(last, 16))

        @block.tensor
        def _(pe):
            for m in range(MC):
                last = pe.transpose(k.psum[7][:, m * P:(m + 1) * P], k.bias1[:, m * P:(m + 1) * P], k.ident[:, :])
            last.then_inc(bias_turned[0], 1)

            def turn(of, ps, p):
                for r in range(R):
                    for c in range(KC):
                        at = (c * R + r) * P
                        last = pe.transpose(ps[:, at:at + p], of[0:p, r, c * P:(c + 1) * P], k.ident[0:p, 0:p])
                return last

            def turn_x(item, p):
                pe.wait_ge(xn_set.at(item), xn_set.count(item))
                if item.follows(1):
                    pe.wait_ge(xt_set.at(item - 1), xt_set.count(item - 1))
                turn(xn[item.slot(2)], xt_ps, p).then_inc(xn_turned.at(item), 1)

            def turn_x1(item, p):
                pe.wait_ge(x1_set.at(item), x1_set.count(item))
                if item.follows(1):
                    pe.wait_ge(zt_set.at(item - 1), zt_set.count(item - 1))
                turn(y[item.slot(3)], zt_ps, p).then_inc(x1_turned.at(item), 1)

            def channels(bank, chunks, at, bias_at, w, hi, lo):
                for m in range(chunks):
                    to = bank[:, m * G:(m + 1) * G]
                    ch = slice(at + m * P, at + (m + 1) * P)
                    if bias_at is not None:
                        pe.matmul(to, k.bias_parts[:, bias_at + m * P:bias_at + (m + 1) * P], k.ones3[:, :],
                                  start=True, stop=False)
                    for c in range(KC):
                        x_hi, x_lo = (t[:, c, :, :].rearrange("q r p -> q (r p)") for t in (hi, lo))
                        pe.matmul(to, w[0][:, c, ch], x_hi, start=(bias_at is None and c == 0), stop=False)
                        pe.matmul(to, w[0][:, c, ch], x_lo, start=False, stop=False)
                        last = pe.matmul(to, w[1][:, c, ch], x_hi, start=False, stop=(c == KC - 1))
                return last

            def gat1(item, p):
                s = item.slot(2)
                pe.wait_ge(xt_set.at(item), xt_set.count(item))
                for j in range(2):
                    if item.follows(1):
                        pe.wait_ge(elu_set[j].at(item - 1), elu_set[j].count(item - 1))
                    channels(h_bank[j], MH, j * MH * P, None, k.w1_p, xt_hi[s], xt_lo[s])\
                        .then_inc(h_ps[j].at(item), 1)

            def mlp_hidden(item, p):
                s = item.slot(2)
                pe.wait_ge(zt_set.at(item), zt_set.count(item))
                if item.follows(1):
                    pe.wait_ge(hid_set.at(item - 1), hid_set.count(item - 1))
                channels(hid_bank, KC, 0, HC + D, k.mw1_p, zt_hi[s], zt_lo[s]).then_inc(hid_ps.at(item), 1)

            def nodes(bank, bias_at, chunks, hi, lo, w):
                for r in range(R):
                    to = bank[:, r * D:(r + 1) * D]
                    pe.matmul(to, k.ones3[:, 0:P], k.bias_parts[:, bias_at:bias_at + D], start=True, stop=False)
                    for m in range(chunks):
                        pe.matmul(to, hi[:, m, r, :], w[0][:, m, :], start=False, stop=False)
                        pe.matmul(to, hi[:, m, r, :], w[1][:, m, :], start=False, stop=False)
                        last = pe.matmul(to, lo[:, m, r, :], w[0][:, m, :], start=False, stop=(m == chunks - 1))
                return last

            def gat2(item, p):
                s = item.slot(2)
                for j in range(2):
                    pe.wait_ge(elu_lo_set[j].at(item), elu_lo_set[j].count(item))
                if item.follows(1):
                    pe.wait_ge(h2_set.at(item - 1), h2_set.count(item - 1))
                nodes(h2_bank, HC, MC, elu_hi[s], elu_lo[s], k.w2_p).then_inc(h2_ps.at(item), 1)

            def mlp_out(item, p):
                s = item.slot(2)
                pe.wait_ge(hid_set.at(item), hid_set.count(item))
                if item.follows(1):
                    pe.wait_ge(v_set.at(item - 1), v_set.count(item - 1))
                nodes(mlp_bank, HC + 2 * D, KC, hid_hi[s], hid_lo[s], k.mw2_p).then_inc(mlp_ps.at(item), 1)

            each_group(pe, (5, turn_x1), (6, mlp_out), (1, turn_x), (2, gat1), (5, mlp_hidden), (3, gat2))

        @block.scalar
        def _(act):
            act.wait_ge(bias_set[0], 1)

            def copy_h2(item, p):
                act.wait_ge(h2_ps.at(item), h2_ps.count(item))
                if item.follows(3):
                    act.wait_ge(h2_out.at(item - 3), h2_out.count(item - 3, 16))
                    act.wait_ge(y_set.at(item - 3), y_set.count(item - 3))
                act.activation(flat(h2[item.slot(3)], p), h2_bank[0:p, :], ACT.Copy).then_inc(h2_set.at(item), 1)

            def hi_of_x(item, p):
                act.wait_ge(xn_turned.at(item), xn_turned.count(item))
                if item.follows(2):
                    act.wait_ge(h_ps[1].at(item - 2), h_ps[1].count(item - 2))
                act.activation(xt_hi[item.slot(2)][:, :, :, 0:p], turned(xt_ps, KC)[:, :, :, 0:p], ACT.Copy)\
                    .then_inc(xt_hi_set.at(item), 1)

            def hi_of_x1(item, p):
                act.wait_ge(x1_turned.at(item), x1_turned.count(item))
                if item.follows(2):
                    act.wait_ge(hid_ps.at(item - 2), hid_ps.count(item - 2))
                act.activation(zt_hi[item.slot(2)][:, :, :, 0:p], turned(zt_ps, KC)[:, :, :, 0:p], ACT.Copy)\
                    .then_inc(zt_hi_set.at(item), 1)

            def norm_s(item, p):
                s = item.slot(3)
                norm_on_act(act, st["s"][4], item, v[s][0:p, :, :], rstd["s"][s][0:p], shift["s"][s][0:p],
                            v[s][0:p, :, :]).then_inc(o_set.at(item), 1)

            def half(t, item, j, p):
                return t[item.slot(2)][:, j * MH:(j + 1) * MH, :, 0:p]

            def exp_half(j):
                def stage(item, p):
                    act.wait_ge(h_ps[j].at(item), h_ps[j].count(item))
                    if item.follows(2):
                        act.wait_ge(elu_lo_set[j].at(item - 2), elu_lo_set[j].count(item - 2))
                    for m in range(MH):
                        ch = j * MH + m
                        last = act.activation(elu[item.slot(2)][:, ch, :, 0:p], turned(h_bank[j], MH)[:, m, :, 0:p],
                                              ACT.Exp, bias=b1_col[:, ch:ch + 1], scale=-1.0)
                    last.then_inc(exp_set[j].at(item), 1)
                    act.wait_ge(exp_set[j].at(item), exp_set[j].count(item))
                    act.activation(half(elu, item, j, p), half(elu, item, j, p), ACT.Relu, bias=1.0, scale=-1.0)\
                        .then_inc(neg_set[j].at(item), 1)
                return stage

            def elu_hi_half(j):
                def stage(item, p):
                    act.wait_ge(elu_set[j].at(item), elu_set[j].count(item))
                    if item.follows(2):
                        act.wait_ge(h2_ps.at(item - 2), h2_ps.count(item - 2))
                    act.activation(half(elu_hi, item, j, p), half(elu, item, j, p), ACT.Copy)\
                        .then_inc(elu_hi_set[j].at(item), 1)
                return stage

            def norm_y(item, p):
                s = item.slot(3)
                norm_on_act(act, st["y"][4], item, y[s][0:p, :, :], rstd["y"][s][0:p], shift["y"][s][0:p],
                            y[s][0:p, :, :]).then_inc(x1_set.at(item), 1)

            def hi_of_hidden(item, p):
                act.wait_ge(hid_ps.at(item), hid_ps.count(item))
                if item.follows(2):
                    act.wait_ge(mlp_ps.at(item - 2), mlp_ps.count(item - 2))
                act.activation(hid_hi[item.slot(2)][:, :, :, 0:p], turned(hid_bank, KC)[:, :, :, 0:p], ACT.Relu)\
                    .then_inc(hid_hi_set.at(item), 1)

            def norm_x(item, p):
                s = item.slot(3)
                if item.follows(2):
                    act.wait_ge(xn_turned.at(item - 2), xn_turned.count(item - 2))
                norm_on_act(act, st["x"][4], item, xs[item.slot(6)][0:p, :, :], rstd["x"][s][0:p], shift["x"][s][0:p],
                            xn[item.slot(2)][0:p, :, :]).then_inc(xn_set.at(item), 1)

            each_group(act, (4, copy_h2), (1, norm_x), (5, hi_of_x1), (1, hi_of_x), (8, norm_s), (2, exp_half(0)),
                       (2, exp_half(1)), (4, norm_y), (2, elu_hi_half(0)), (5, hi_of_hidden), (2, elu_hi_half(1)))

        @block.gpsimd
        def _(pool):
            def rstd_of(n):
                def stage(item, p):
                    s = item.slot(3)
                    norm_rstd(pool, k, st[n][1:4], item, mv[n][s][0:p], ve[n][s][0:p, :], rstd[n][s][0:p, :])
                return stage

            def elu_lo_half(j):
                def stage(item, p):
                    s = item.slot(2)
                    pool.wait_ge(elu_hi_set[j].at(item), elu_hi_set[j].count(item))
                    if item.follows(2):
                        pool.wait_ge(h2_ps.at(item - 2), h2_ps.count(item - 2))
                    m = slice(j * MH, (j + 1) * MH)
                    pool.tensor_tensor(elu_lo[s][:, m, :, 0:p], elu[s][:, m, :, 0:p],
                                       elu_hi[s][:, m, :, 0:p].bitcast(F32), ALU.subtract)\
                        .then_inc(elu_lo_set[j].at(item), 1)
                return stage

            def add_y(item, p):
                s = item.slot(3)
                pool.wait_ge(h2_set.at(item), h2_set.count(item))
                if item.follows(3):
                    pool.wait_ge(x1_out.at(item - 3), x1_out.count(item - 3, 16))
                    pool.wait_ge(x1_turned.at(item - 3), x1_turned.count(item - 3))
                    pool.wait_ge(v_set.at(item - 3), v_set.count(item - 3))
                pool.tensor_tensor(flat(y[s], p), flat(h2[s], p), flat(xs[item.slot(6)], p), ALU.add)\
                    .then_inc(y_set.at(item), 1)

            def add_beta(item, p):
                pool.wait_ge(x1_set.at(item), x1_set.count(item))
                if item.follows(2):
                    pool.wait_ge(s_set.at(item - 2), s_set.count(item - 2))
                beta = k.beta[0:p, :].unsqueeze(1).broadcast_to([p, R, D])
                pool.tensor_tensor(x1b[item.slot(2)][0:p, :, :], y[item.slot(3)][0:p, :, :], beta, ALU.add)\
                    .then_inc(x1b_set.at(item), 1)

            each_group(pool, (4, add_y), (3, elu_lo_half(1)), (7, rstd_of("s")), (0, rstd_of("x")), (4, rstd_of("y")),
                       (6, rstd_of("v")), (5, add_beta), (2, elu_lo_half(0)))

        @block.vector
        def _(dve):
            dve.wait_ge(bias_turned[0], 1)
            dve.tensor_copy(b1_col[:, :], k.psum[7][:, :].rearrange("q (m p) -> q m p", m=MC)[:, :, 0])\
                .then_inc(bias_set[0], 1)
            dve.wait_ge(bias_set[0], 1)
            data = {"x": (xs, 6), "y": (y, 3), "v": (v, 3), "s": (v, 3)}

            def sums_of(n):
                def stage(item, p):
                    t, slots = data[n]
                    norm_sums(dve, st[n][0], item, t[item.slot(slots)][0:p, :, :], stats[n][item.slot(3)][0:p])
                return stage

            def mean_of(n):
                def stage(item, p):
                    s = item.slot(3)
                    norm_mean(dve, k, st[n][0:2], item, stats[n][s][0:p], mv[n][s][0:p])
                return stage

            def shift_of(n):
                def stage(item, p):
                    s = item.slot(3)
                    norm_shift(dve, st[n][3:5], item, mv[n][s][0:p], rstd[n][s][0:p, :], shift[n][s][0:p, :])
                return stage

            def elu_half(j):
                def stage(item, p):
                    dve.wait_ge(neg_set[j].at(item), neg_set[j].count(item))
                    for m in range(MH):
                        ch = j * MH + m
                        half = elu[item.slot(2)][:, ch, :, 0:p]
                        last = dve.scalar_tensor_tensor(half, turned(h_bank[j], MH)[:, m, :, 0:p], b1_col[:, ch:ch + 1],
                                                        half, ALU.subtract, ALU.min)
                    last.then_inc(elu_set[j].at(item), 1)
                return stage

            def lo_of(item, p, hi_set, lo_set, used, ps, hi, lo):
                s = item.slot(2)
                dve.wait_ge(hi_set.at(item), hi_set.count(item))
                if item.follows(2):
                    dve.wait_ge(used.at(item - 2), used.count(item - 2))
                dve.tensor_tensor(lo[s][:, :, :, 0:p], turned(ps, KC)[:, :, :, 0:p], hi[s][:, :, :, 0:p].bitcast(F32),
                                  ALU.subtract).then_inc(lo_set.at(item), 1)

            def lo_of_x(item, p):
                lo_of(item, p, xt_hi_set, xt_set, h_ps[1], xt_ps, xt_hi, xt_lo)

            def lo_of_x1(item, p):
                lo_of(item, p, zt_hi_set, zt_set, hid_ps, zt_ps, zt_hi, zt_lo)

            def x_sums(item, p):
                dve.wait_ge(x_in.at(item), x_in.count(item, 16))
                sums_of("x")(item, p)

            def y_sums(item, p):
                dve.wait_ge(y_set.at(item), y_set.count(item))
                sums_of("y")(item, p)

            def make_v(item, p):
                s = item.slot(3)
                dve.wait_ge(mlp_ps.at(item), mlp_ps.count(item))
                if item.follows(3):
                    dve.wait_ge(o_out.at(item - 3), o_out.count(item - 3, 16))
                dve.scalar_tensor_tensor(flat(v[s], p), mlp_bank[0:p, :], 0.0, flat(y[s], p), ALU.max, ALU.add)\
                    .then_inc(v_set.at(item), 1)

            def v_sums(item, p):
                dve.wait_ge(v_set.at(item), v_set.count(item))
                sums_of("v")(item, p)

            def gain(item, p):
                s = item.slot(3)
                dve.wait_ge(st["v"][1].at(item), st["v"][1].count(item))
                for r in range(R):
                    last = dve.scalar_tensor_tensor(v[s][0:p, r, :], v[s][0:p, r, :], mv["v"][s][0:p, r, 0:1],
                                                    k.gamma[0:p, :], ALU.subtract, ALU.mult)
                last.then_inc(a_set.at(item), 1)

            def make_s(item, p):
                s = item.slot(3)
                dve.wait_ge(a_set.at(item), a_set.count(item))
                dve.wait_ge(st["v"][3].at(item), st["v"][3].count(item))
                dve.wait_ge(x1b_set.at(item), x1b_set.count(item))
                for r in range(R):
                    last = dve.scalar_tensor_tensor(v[s][0:p, r, :], v[s][0:p, r, :], rstd["v"][s][0:p, r:r + 1],
                                                    x1b[item.slot(2)][0:p, r, :], ALU.mult, ALU.add)
                last.then_inc(s_set.at(item), 1)

            def lo_of_hidden(item, p):
                s = item.slot(2)
                dve.wait_ge(hid_hi_set.at(item), hid_hi_set.count(item))
                if item.follows(2):
                    dve.wait_ge(mlp_ps.at(item - 2), mlp_ps.count(item - 2))
                if p == P:
                    last = dve.scalar_tensor_tensor(hid_lo[s][:, :, :, :].rearrange("q m r p -> q (m r p)"), hid_bank[:, :],
                                                    0.0, hid_hi[s][:, :, :, :].rearrange("q m r p -> q (m r p)").bitcast(F32),
                                                    ALU.max, ALU.subtract)
                for m in range(KC if p < P else 0):
                    last = dve.scalar_tensor_tensor(hid_lo[s][:, m, :, 0:p], turned(hid_bank, KC)[:, m, :, 0:p], 0.0,
                                                    hid_hi[s][:, m, :, 0:p].bitcast(F32), ALU.max, ALU.subtract)
                last.then_inc(hid_set.at(item), 1)

            def s_sums(item, p):
                dve.wait_ge(s_set.at(item), s_set.count(item))
                sums_of("s")(item, p)

            each_group(dve, (0, x_sums), (7, mean_of("s")), (5, lo_of_x1), (4, y_sums), (0, mean_of("x")), (4, mean_of("y")),
                       (6, make_v), (1, lo_of_x), (6, v_sums), (2, elu_half(0)), (6, mean_of("v")),
                       (7, shift_of("s")), (0, shift_of("x")), (4, shift_of("y")), (6, gain), (2, elu_half(1)),
                       (6, make_s), (5, lo_of_hidden), (6, s_sums))


def gat2_scores(nc, k):
    D, T = k.D, k.T
    PER = 4
    ctx, sb, sem = phase(nc, "gat2_scores")
    with ctx:
        rows_in, rows_out = sem("rows_in", PER), sem("rows_out", PER)
        idx_set, prod_set, term_set = sem("idx_set"), sem("prod_set"), sem("term_set")
        fix_in, own_prod_set, own_term_set = sem("fix_in", PER), sem("own_prod_set"), sem("own_term_set")
        rows = [sb(f"rows{s}", [P, D]) for s in range(PER)]
        idx = [sb(f"idx{s}", [P, 1], I32) for s in range(PER)]
        prod = [sb(f"prod{s}", [P, D]) for s in range(PER)]
        fix = [sb(f"fix{s}", [P, D]) for s in range(PER)]
        own_prod = [sb(f"own_prod{s}", [P, 2, D]) for s in range(PER)]
        block = ctx.enter_context(nc.Block())

        @block.gpsimd
        def _(pool):
            def gather(item):
                s = item.slot(PER)
                if item.follows(PER):
                    pool.wait_ge(prod_set.at(item - PER), prod_set.count(item - PER))
                    pool.wait_ge(rows_out.at(item - PER), rows_out.count(item - PER, 16))
                pool.wait_ge(idx_set.at(item), idx_set.count(item))
                apart(pool, k)
                pool.indirect_dma_start(out=rows[s][:, :], out_offset=None, in_=k.h2_dram[:, :],
                                        in_offset=bass.IndirectOffsetOnAxis(idx[s][:, :], 0),
                                        bounds_check=k.N - 1, oob_is_err=True)\
                    .then_inc(rows_in.at(item), 16)

            def multiply(item):
                s = item.slot(PER)
                pool.wait_ge(rows_in.at(item), rows_in.count(item, 16))
                if item.follows(PER):
                    pool.wait_ge(term_set.at(item - PER), term_set.count(item - PER))
                pool.tensor_tensor(prod[s][:, :], rows[s][:, :], k.att2[:, 0, :], ALU.mult)\
                    .then_inc(prod_set.at(item), 1)

            each_item(pool, T, PER, (0, gather), (2, multiply))

        @block.sync
        def _(sp):
            def store(item):
                sp.wait_ge(rows_in.at(item), rows_in.count(item, 16))
                sp.dma_start(k.h2_src_dram[bass.ds(item.index(), 1), :, :].rearrange("t p d -> (t p) d"),
                             rows[item.slot(PER)][:, :])\
                    .then_inc(rows_out.at(item), 16)

            def load_fix(item):
                if item.follows(PER):
                    sp.wait_ge(own_prod_set.at(item - PER), own_prod_set.count(item - PER))
                sp.dma_start(fix[item.slot(PER)][:, :],
                             k.fix_dram[bass.ds(item.index(), 1), :, :].rearrange("t p d -> (t p) d"))\
                    .then_inc(fix_in.at(item), 16)

            each_item(sp, T, PER, (0, load_fix), (2, store))
            for back in range(PER):
                sp.wait_ge(rows_out.at(Item(None, T - 1 - back, PER)), rows_out.count(Item(None, T - 1 - back, PER), 16))

        @block.vector
        def _(dve):
            def index(item):
                if item.follows(PER):
                    dve.wait_ge(rows_in.at(item - PER), rows_in.count(item - PER, 16))
                dve.tensor_copy(idx[item.slot(PER)][:, :], k.src_idx[:, bass.ds(item.index(), 1)])\
                    .then_inc(idx_set.at(item), 1)

            def multiply_own(item):
                s = item.slot(PER)
                dve.wait_ge(fix_in.at(item), fix_in.count(item, 16))
                row = fix[s][:, :].unsqueeze(1).broadcast_to([P, 2, D])
                dve.tensor_tensor(own_prod[s][:, :, :], row, k.att2[:, :, :], ALU.mult)\
                    .then_inc(own_prod_set.at(item), 1)

            def add_up_own(item):
                dve.wait_ge(own_prod_set.at(item), own_prod_set.count(item))
                dve.tensor_reduce(k.terms2[:, 1:3, bass.ds(item.index(), 1)], own_prod[item.slot(PER)][:, :, :],
                                  AX_X, ALU.add)\
                    .then_inc(own_term_set.at(item), 1)

            def add_up(item):
                dve.wait_ge(prod_set.at(item), prod_set.count(item))
                dve.tensor_reduce(k.terms2[:, 0, bass.ds(item.index(), 1)], prod[item.slot(PER)][:, :], AX_X, ALU.add)\
                    .then_inc(term_set.at(item), 1)

            each_item(dve, T, PER, (0, index), (2, multiply_own), (3, add_up), (2, add_up_own))


def gat2_softmax(nc, k):
    T = k.T
    ctx, sb, sem = phase(nc, "gat2_softmax")
    with ctx:
        link_sem, rows_turned, shifted, exps_set, exps_turned, tables_set = (
            sem("link"), sem("rows_turned"), sem("shifted"), sem("exps_set"), sem("exps_turned"), sem("tables_set"))
        const = k.att2_const
        rows = sb("rows", [T, 3, P])
        spread = sb("spread", [T, 2, P])
        score = sb("score", [T, 2, P])
        run_max, maxima = sb("run_max", [T, 1, P]), sb("maxima", [T, 1, P])

        def names(tag):
            return (lambda n, shape, dt=F32: sb(f"{tag}_{n}", shape, dt)), (lambda n, ring=1: sem(f"{tag}_{n}", ring))

        seg_sum = Segments(k, 2, *names("spread"), k.psum[1], k.psum[2])
        seg_max = Segments(k, 1, *names("max"), k.psum[3], k.psum[4])
        block = ctx.enter_context(nc.Block())

        @block.vector
        def _(dve):
            link = Link(dve, link_sem)
            dve.wait_ge(rows_turned[0], 1)
            link(dve.tensor_copy(rows[:, :, :].rearrange("t n e -> t (n e)"), k.psum[0][0:T, 0:3 * P]))
            for j in range(2):
                last = dve.tensor_tensor(rows[:, 1 + j, :], rows[:, 1 + j, :], k.is_last[:, :], ALU.mult)
            link(last)
            seg_sum.scan(dve, link, k.not_last[:, :], rows[:, 1:3, :], spread, (ALU.mult, ALU.add), 0.0, True)
            dve.tensor_tensor(score[:, 0, :], rows[:, 0, :], spread[:, 1, :], ALU.add)
            link(dve.tensor_tensor(score[:, 1, :], spread[:, 0, :], spread[:, 1, :], ALU.add))
            flat = score[:, :, :].rearrange("t j e -> t (j e)")
            link(dve.tensor_scalar(flat, flat, const[0:T, :], None, ALU.add))
            link(dve.scalar_tensor_tensor(flat, flat, NEG_SLOPE, flat, ALU.mult, ALU.max))
            seg_max.scan(dve, link, k.cut_first[:, :], score[:, 0:1, :], run_max, (ALU.add, ALU.max), LOW, False)
            seg_max.scan(dve, link, k.cut_last[:, :], run_max, maxima, (ALU.add, ALU.max), LOW, True)
            link(dve.tensor_tensor(maxima[:, 0, :], maxima[:, 0, :], score[:, 1, :], ALU.max))
            for j in range(2):
                last = dve.tensor_tensor(score[:, j, :], score[:, j, :], maxima[:, 0, :], ALU.subtract)
            last.then_inc(shifted[0], 1)
            dve.wait_ge(exps_turned[0], 1)
            dve.tensor_copy(k.p2[:, :], k.psum[5][:, 0:T])
            dve.tensor_copy(k.ps2[:, :], k.psum[5][:, P:P + T]).then_inc(tables_set[0], 1)

        @block.scalar
        def _(act):
            act.wait_ge(shifted[0], 1)
            flat = score[:, :, :].rearrange("t j e -> t (j e)")
            act.activation(flat, flat, ACT.Exp).then_inc(exps_set[0], 1)

        @block.tensor
        def _(pe):
            for j in range(3):
                last = pe.transpose(k.psum[0][0:T, j * P:(j + 1) * P], k.terms2[:, j, :], k.ident[:, :])
            last.then_inc(rows_turned[0], 1)
            seg_sum.turn(pe, 1, (True,))
            seg_max.turn(pe, 2, (False, True))
            pe.wait_ge(exps_set[0], 1)
            for j in range(2):
                last = pe.transpose(k.psum[5][:, j * P:j * P + T], score[:, j, :], k.ident[0:T, 0:T])
            last.then_inc(exps_turned[0], 1)


def gat2_messages(nc, k):
    D, T = k.D, k.T
    PER = 6
    ctx, sb, sem = phase(nc, "gat2_messages")
    with ctx:
        last_idx_set, rows_in, same_set, msg_set = sem("last_idx_set"), sem("rows_in", PER), sem("same_set"), sem("msg_set")
        sum_ps, sum_set, zero_set = sem("sum_ps"), sem("sum_set"), sem("zero_set")
        den_set, inv_set, num_set, y_set = sem("den_set"), sem("inv_set"), sem("num_set"), sem("y_set")
        st = [sem(n) for n in ("st_done", "mv_done", "ve_done", "rs_done", "shift_done")]
        x1_set, x1_out, copy_out = sem("x1_set"), sem("x1_out", PER), sem("copy_out", PER)

        def ring(name, shape, dt=F32):
            return [sb(f"{name}{s}", shape, dt) for s in range(PER)]

        last_idx = ring("last_idx", [P, 1], I32)
        h2_src, x_own, fix = (ring(n, [P, D]) for n in ("h2_src", "x_own", "fix"))
        dst_row, same, carry = (ring(n, [P, P]) for n in ("dst_row", "same", "carry"))
        msg, sums = (ring(n, [P, D + 1]) for n in ("msg", "sums"))
        y = ring("y", [P, 1, D])
        stats, mv = ring("stats", [P, 1, 6]), ring("mv", [P, 1, 2])
        inv, ve, rstd, shift = (ring(n, [P, 1]) for n in ("inv", "ve", "rstd", "shift"))
        sum_bank = k.psum[0:2]
        block = ctx.enter_context(nc.Block())

        @block.sync
        def _(sp):
            def load(item):
                s = item.slot(PER)
                t = bass.ds(item.index(), 1)
                if item.follows(PER):
                    sp.wait_ge(msg_set.at(item - PER), msg_set.count(item - PER))
                    sp.wait_ge(y_set.at(item - PER), y_set.count(item - PER))
                    sp.wait_ge(same_set.at(item - PER), same_set.count(item - PER))
                for to, of in ((h2_src, k.h2_src_dram), (x_own, k.x_own_dram), (fix, k.fix_dram)):
                    sp.dma_start(to[s][:, :], of[t, :, :].rearrange("t p d -> (t p) d"))\
                        .then_inc(rows_in.at(item), 16)
                sp.dma_start(dst_row[s][:, :], k.dst_dram[t, :].broadcast_to([P, P]))\
                    .then_inc(rows_in.at(item), 16)

            def store(item):
                sp.wait_ge(x1_set.at(item), x1_set.count(item))
                sp.dma_start(k.fix1_dram[bass.ds(item.index(), 1), :, :].rearrange("t p d -> (t p) d"),
                             y[item.slot(PER)][:, 0, :])\
                    .then_inc(copy_out.at(item), 16)

            each_item(sp, T, PER, (0, load), (6, store))
            for back in range(PER):
                sp.wait_ge(copy_out.at(Item(None, T - 1 - back, PER)), copy_out.count(Item(None, T - 1 - back, PER), 16))

        @block.gpsimd
        def _(pool):
            def norm(item):
                s = item.slot(PER)
                norm_rstd(pool, k, st[1:4], item, mv[s], ve[s][:, :], rstd[s][:, :])

            def scatter(item):
                s = item.slot(PER)
                if item.follows(PER):
                    pool.wait_ge(x1_out.at(item - PER), x1_out.count(item - PER, 16))
                pool.tensor_copy(last_idx[s][:, :], k.last_idx[:, bass.ds(item.index(), 1)])\
                    .then_inc(last_idx_set.at(item), 1)
                pool.wait_ge(last_idx_set.at(item), last_idx_set.count(item))
                pool.wait_ge(x1_set.at(item), x1_set.count(item))
                apart(pool, k)
                pool.indirect_dma_start(out=k.x1_dram[:, :], out_offset=bass.IndirectOffsetOnAxis(last_idx[s][:, :], 0),
                                        in_=y[s][:, 0, :], in_offset=None, bounds_check=k.N - 1,
                                        oob_is_err=False)\
                    .then_inc(x1_out.at(item), 16)

            each_item(pool, T, PER, (0, norm), (1, scatter))
            for back in range(PER):
                pool.wait_ge(x1_out.at(Item(None, T - 1 - back, PER)), x1_out.count(Item(None, T - 1 - back, PER), 16))

        @block.tensor
        def _(pe):
            def sum_up(item):
                s, b = item.slot(PER), item.slot(2)
                pe.wait_ge(msg_set.at(item), msg_set.count(item))
                if item.follows(2):
                    pe.wait_ge(sum_set.at(item - 2), sum_set.count(item - 2))
                pe.matmul(sum_bank[b][:, 0:D + 1], same[s][:, :], msg[s][:, :], start=True, stop=False)
                if not item.follows(1):
                    pe.wait_ge(zero_set[0], 1)
                if item.follows(1):
                    pe.wait_ge(sum_set.at(item - 1), sum_set.count(item - 1))
                pe.matmul(sum_bank[b][:, 0:D + 1], carry[s][:, :], sums[(s + PER - 1) % PER][:, :], start=False, stop=True)\
                    .then_inc(sum_ps.at(item), 1)

            each_item(pe, T, PER, (0, sum_up))

        @block.scalar
        def _(act):
            def copy_sums(item):
                s, b = item.slot(PER), item.slot(2)
                act.wait_ge(sum_ps.at(item), sum_ps.count(item))
                if item.follows(PER):
                    act.wait_ge(num_set.at(item - PER), num_set.count(item - PER))
                act.activation(sums[s][:, :], sum_bank[b][:, 0:D + 1], ACT.Copy)\
                    .then_inc(sum_set.at(item), 1)

            def norm_out(item):
                s = item.slot(PER)
                norm_on_act(act, st[4], item, y[s], rstd[s], shift[s], y[s]).then_inc(x1_set.at(item), 1)

            each_item(act, T, PER, (0, copy_sums), (3, norm_out))

        @block.vector
        def _(dve):
            dve.memset(sums[PER - 1][:, :], 0.0)\
                .then_inc(zero_set.at(Item(None, 0, 1)), 1)

            def messages(item):
                s = item.slot(PER)
                t = bass.ds(item.index(), 1)
                dve.wait_ge(rows_in.at(item), rows_in.count(item, 64))
                if item.follows(PER):
                    dve.wait_ge(sum_ps.at(item - PER), sum_ps.count(item - PER))
                same_and_carry(dve, item, k, dst_row[s][:, :], same[s][:, :], carry[s][:, :])\
                    .then_inc(same_set.at(item), 1)
                dve.tensor_copy(msg[s][:, D:D + 1], k.p2[:, t])
                dve.tensor_scalar(msg[s][:, 0:D], h2_src[s][:, :], k.p2[:, t], None, ALU.mult)\
                    .then_inc(msg_set.at(item), 1)

            def whole(item):
                s = item.slot(PER)
                ps_t = k.ps2[:, bass.ds(item.index(), 1)]
                dve.wait_ge(sum_set.at(item), sum_set.count(item))
                if item.follows(PER):
                    dve.wait_ge(x1_out.at(item - PER), x1_out.count(item - PER, 16))
                    dve.wait_ge(copy_out.at(item - PER), copy_out.count(item - PER, 16))
                dve.tensor_tensor(inv[s][:, :], sums[s][:, D:D + 1], ps_t, ALU.add)\
                    .then_inc(den_set.at(item), 1)
                dve.scalar_tensor_tensor(y[s][:, 0, :], fix[s][:, :], ps_t, sums[s][:, 0:D], ALU.mult, ALU.add)\
                    .then_inc(num_set.at(item), 1)

            def invert(item):
                s = item.slot(PER)
                dve.wait_ge(den_set.at(item), den_set.count(item))
                dve.reciprocal(inv[s][:, :], inv[s][:, :])\
                    .then_inc(inv_set.at(item), 1)

            def residual(item):
                s = item.slot(PER)
                dve.wait_ge(num_set.at(item), num_set.count(item))
                dve.wait_ge(inv_set.at(item), inv_set.count(item))
                dve.scalar_tensor_tensor(y[s][:, 0, :], y[s][:, 0, :], inv[s][:, 0:1], x_own[s][:, :],
                                         ALU.mult, ALU.add)\
                    .then_inc(y_set.at(item), 1)

            def y_sums(item):
                dve.wait_ge(y_set.at(item), y_set.count(item))
                norm_sums(dve, st[0], item, y[item.slot(PER)], stats[item.slot(PER)])

            def y_mean(item):
                norm_mean(dve, k, st[0:2], item, stats[item.slot(PER)], mv[item.slot(PER)])

            def shift_of(item):
                s = item.slot(PER)
                norm_shift(dve, st[3:5], item, mv[s], rstd[s][:, :], shift[s][:, :])

            each_item(dve, T, PER, (0, messages), (1, whole), (2, y_sums), (1, invert), (2, y_mean), (1, residual),
                             (3, shift_of))


def gine(nc, k, edge_attr, out):
    D, KC, HC, T, E, LAST = k.D, k.KC, k.HC, k.T, k.E, k.LAST
    PER = 6
    ctx, sb, sem = phase(nc, "gine")
    with ctx:
        src_idx_set, last_idx_set = sem("src_idx_set"), sem("last_idx_set")
        src_in, own_in, same_set = sem("src_in", PER), sem("own_in", PER), sem("same_set")
        edge_set, msg_set, sum_ps, sum_set, zero_set = (
            sem("edge_set"), sem("msg_set"), sem("sum_ps"), sem("sum_set"), sem("zero_set"))
        z_set, z_turned, zt_set, hid_ps, hid_set, mlp_ps = (
            sem("z_set"), sem("z_turned"), sem("zt_set"), sem("hid_ps"), sem("hid_set"), sem("mlp_ps"))
        v_set, a_set, b_set, s_set, o_set, o_out = (
            sem("v_set"), sem("a_set"), sem("b_set"), sem("s_set"), sem("o_set"), sem("o_out", PER))
        st_v = [sem(f"v_{n}") for n in ("st", "mv", "ve", "rstd")]
        st_s = [sem(f"s_{n}") for n in ("st", "mv", "ve", "rstd", "shift")]

        def ring(name, shape, dt=F32):
            return [sb(f"{name}{s}", shape, dt) for s in range(PER)]

        src_idx, last_idx = ring("src_idx", [P, 1], I32), ring("last_idx", [P, 1], I32)
        x1_src, attr, x1_own, x1b, sums, z = (
            ring(n, [P, D]) for n in ("x1_src", "attr", "x1_own", "x1b", "sums", "z"))
        dst_row, same, carry = (ring(n, [P, P]) for n in ("dst_row", "same", "carry"))
        zt, hid = ring("zt", [P, KC, P]), ring("hid", [P, KC, P])
        v = ring("v", [P, 1, D])
        v_stats, s_stats = ring("v_stats", [P, 1, 6]), ring("s_stats", [P, 1, 6])
        v_mv, s_mv = ring("v_mv", [P, 1, 2]), ring("s_mv", [P, 1, 2])
        v_ve, v_rstd, s_ve, s_rstd, s_shift = (
            ring(n, [P, 1]) for n in ("v_ve", "v_rstd", "s_ve", "s_rstd", "s_shift"))
        sum_bank, turn_bank, hid_bank, mlp_bank = k.psum[0:2], k.psum[2:4], k.psum[4:6], k.psum[6:8]
        block = ctx.enter_context(nc.Block())

        @block.sync
        def _(sp):
            def load(item):
                s = item.slot(PER)
                t = bass.ds(item.index(), 1)
                if item.follows(PER):
                    sp.wait_ge(same_set.at(item - PER), same_set.count(item - PER))
                    sp.wait_ge(edge_set.at(item - PER), edge_set.count(item - PER))
                    sp.wait_ge(b_set.at(item - PER), b_set.count(item - PER))
                    sp.wait_ge(v_set.at(item - PER), v_set.count(item - PER))
                n = LAST if item.i is None and item.c == T - 1 else P
                sp.dma_start(attr[s][0:n, :], edge_attr[bass.ds(item.index() * P, n), :])\
                    .then_inc(own_in.at(item), 16)
                sp.dma_start(x1_own[s][:, :], k.fix1_dram[t, :, :].rearrange("t p d -> (t p) d"))\
                    .then_inc(own_in.at(item), 16)
                sp.dma_start(dst_row[s][:, :], k.dst_dram[t, :].broadcast_to([P, P]))\
                    .then_inc(own_in.at(item), 16)

            each_item(sp, T, PER, (0, load))

        @block.gpsimd
        def _(pool):
            def gather(item):
                s = item.slot(PER)
                if item.follows(PER):
                    pool.wait_ge(sum_ps.at(item - PER), sum_ps.count(item - PER))
                pool.wait_ge(src_idx_set.at(item), src_idx_set.count(item))
                apart(pool, k)
                pool.indirect_dma_start(out=x1_src[s][:, :], out_offset=None, in_=k.x1_dram[:, :],
                                        in_offset=bass.IndirectOffsetOnAxis(src_idx[s][:, :], 0),
                                        bounds_check=k.N - 1, oob_is_err=True)\
                    .then_inc(src_in.at(item), 16)

            def v_norm(item):
                s = item.slot(PER)
                norm_rstd(pool, k, st_v[1:4], item, v_mv[s], v_ve[s][:, :], v_rstd[s][:, :])

            def s_norm(item):
                s = item.slot(PER)
                norm_rstd(pool, k, st_s[1:4], item, s_mv[s], s_ve[s][:, :], s_rstd[s][:, :])

            def scatter(item):
                s = item.slot(PER)
                pool.wait_ge(last_idx_set.at(item), last_idx_set.count(item))
                pool.wait_ge(o_set.at(item), o_set.count(item))
                apart(pool, k)
                pool.indirect_dma_start(out=out[:, :], out_offset=bass.IndirectOffsetOnAxis(last_idx[s][:, :], 0),
                                        in_=v[s][:, 0, :], in_offset=None, bounds_check=k.N - 1,
                                        oob_is_err=False)\
                    .then_inc(o_out.at(item), 16)

            each_item(pool, T, PER, (6, s_norm), (5, v_norm), (0, gather), (7, scatter))
            for back in range(PER):
                pool.wait_ge(o_out.at(Item(None, T - 1 - back, PER)), o_out.count(Item(None, T - 1 - back, PER), 16))

        @block.tensor
        def _(pe):
            def turn(item):
                s, b = item.slot(PER), item.slot(2)
                pe.wait_ge(z_set.at(item), z_set.count(item))
                if item.follows(2):
                    pe.wait_ge(zt_set.at(item - 2), zt_set.count(item - 2))
                for c in range(KC):
                    last = pe.transpose(turn_bank[b][:, c * P:(c + 1) * P], z[s][:, c * P:(c + 1) * P], k.ident[:, :])
                last.then_inc(z_turned.at(item), 1)

            def sum_up(item):
                s, b = item.slot(PER), item.slot(2)
                pe.wait_ge(msg_set.at(item), msg_set.count(item))
                if item.follows(2):
                    pe.wait_ge(sum_set.at(item - 2), sum_set.count(item - 2))
                pe.matmul(sum_bank[b][:, 0:D], same[s][:, :], x1_src[s][:, :], start=True, stop=False)
                if not item.follows(1):
                    pe.wait_ge(zero_set[0], 1)
                if item.follows(1):
                    pe.wait_ge(sum_set.at(item - 1), sum_set.count(item - 1))
                pe.matmul(sum_bank[b][:, 0:D], carry[s][:, :], sums[(s + PER - 1) % PER][:, :], start=False, stop=True)\
                    .then_inc(sum_ps.at(item), 1)

            def mlp_out(item):
                s, b = item.slot(PER), item.slot(2)
                pe.wait_ge(hid_set.at(item), hid_set.count(item))
                if item.follows(2):
                    pe.wait_ge(v_set.at(item - 2), v_set.count(item - 2))
                pe.matmul(mlp_bank[b][:, 0:D], k.ones3[:, 0:P], k.bias_parts[:, HC + 2 * D:HC + 3 * D],
                          start=True, stop=False)
                for c in range(KC):
                    last = pe.matmul(mlp_bank[b][:, 0:D], hid[s][:, c, :], k.mw2[:, c, :], start=False, stop=(c == KC - 1))
                last.then_inc(mlp_ps.at(item), 1)

            def mlp_hidden(item):
                s, b = item.slot(PER), item.slot(2)
                pe.wait_ge(zt_set.at(item), zt_set.count(item))
                if item.follows(2):
                    pe.wait_ge(hid_set.at(item - 2), hid_set.count(item - 2))
                for m in range(KC):
                    to, at = hid_bank[b][:, m * P:(m + 1) * P], HC + D + m * P
                    pe.matmul(to, k.bias_parts[:, at:at + P], k.ones3[:, 0:P], start=True, stop=False)
                    for c in range(KC):
                        last = pe.matmul(to, k.mw1[:, c, m * P:(m + 1) * P], zt[s][:, c, :], start=False, stop=(c == KC - 1))
                last.then_inc(hid_ps.at(item), 1)

            each_item(pe, T, PER, (1, turn), (0, sum_up), (2, mlp_out), (1, mlp_hidden))

        @block.scalar
        def _(act):
            def copy_turned(item):
                s, b = item.slot(PER), item.slot(2)
                act.wait_ge(z_turned.at(item), z_turned.count(item))
                if item.follows(PER):
                    act.wait_ge(hid_ps.at(item - PER), hid_ps.count(item - PER))
                act.activation(zt[s][:, :, :].rearrange("p c e -> p (c e)"), turn_bank[b][:, 0:D], ACT.Copy)\
                    .then_inc(zt_set.at(item), 1)

            def norm_out(item):
                s = item.slot(PER)
                norm_on_act(act, st_s[4], item, v[s], s_rstd[s], s_shift[s], v[s]).then_inc(o_set.at(item), 1)

            def copy_sums(item):
                s, b = item.slot(PER), item.slot(2)
                act.wait_ge(sum_ps.at(item), sum_ps.count(item))
                if item.follows(PER):
                    act.wait_ge(z_set.at(item - PER), z_set.count(item - PER))
                act.activation(sums[s][:, :], sum_bank[b][:, 0:D], ACT.Copy)\
                    .then_inc(sum_set.at(item), 1)

            def messages(item):
                s = item.slot(PER)
                act.wait_ge(edge_set.at(item), edge_set.count(item))
                act.activation(x1_src[s][:, :], x1_src[s][:, :], ACT.Relu)\
                    .then_inc(msg_set.at(item), 1)

            def hidden(item):
                s, b = item.slot(PER), item.slot(2)
                act.wait_ge(hid_ps.at(item), hid_ps.count(item))
                if item.follows(PER):
                    act.wait_ge(mlp_ps.at(item - PER), mlp_ps.count(item - PER))
                act.activation(hid[s][:, :, :].rearrange("p c e -> p (c e)"), hid_bank[b][:, 0:D], ACT.Relu)\
                    .then_inc(hid_set.at(item), 1)

            each_item(act, T, PER, (2, copy_turned), (1, copy_sums), (0, messages), (2, hidden), (5, norm_out))

        @block.vector
        def _(dve):
            dve.memset(sums[PER - 1][:, :], 0.0)\
                .then_inc(zero_set.at(Item(None, 0, 1)), 1)

            def index_src(item):
                if item.follows(PER):
                    dve.wait_ge(src_in.at(item - PER), src_in.count(item - PER, 16))
                dve.tensor_copy(src_idx[item.slot(PER)][:, :], k.src_idx[:, bass.ds(item.index(), 1)])\
                    .then_inc(src_idx_set.at(item), 1)

            def index_last(item):
                if item.follows(PER):
                    dve.wait_ge(o_out.at(item - PER), o_out.count(item - PER, 16))
                dve.tensor_copy(last_idx[item.slot(PER)][:, :], k.last_idx[:, bass.ds(item.index(), 1)])\
                    .then_inc(last_idx_set.at(item), 1)

            def front(item):
                s = item.slot(PER)
                dve.wait_ge(own_in.at(item), own_in.count(item, 48))
                if item.follows(PER):
                    dve.wait_ge(sum_ps.at(item - PER), sum_ps.count(item - PER))
                same_and_carry(dve, item, k, dst_row[s][:, :], same[s][:, :], carry[s][:, :])\
                    .then_inc(same_set.at(item), 1)
                dve.wait_ge(src_in.at(item), src_in.count(item, 16))
                dve.tensor_tensor(x1_src[s][:, :], x1_src[s][:, :], attr[s][:, :], ALU.add)\
                    .then_inc(edge_set.at(item), 1)

            def sum_own(item):
                s = item.slot(PER)
                dve.wait_ge(sum_set.at(item), sum_set.count(item))
                if item.follows(PER):
                    dve.wait_ge(z_turned.at(item - PER), z_turned.count(item - PER))
                dve.tensor_tensor(z[s][:, :], sums[s][:, :], x1_own[s][:, :], ALU.add)\
                    .then_inc(z_set.at(item), 1)

            def make_v(item):
                s, b = item.slot(PER), item.slot(2)
                dve.wait_ge(mlp_ps.at(item), mlp_ps.count(item))
                if item.follows(PER):
                    dve.wait_ge(o_out.at(item - PER), o_out.count(item - PER, 16))
                dve.scalar_tensor_tensor(v[s][:, 0, :], mlp_bank[b][:, 0:D], 0.0, x1_own[s][:, :], ALU.max, ALU.add)\
                    .then_inc(v_set.at(item), 1)
                dve.tensor_tensor(x1b[s][:, :], x1_own[s][:, :], k.beta[:, :], ALU.add)\
                    .then_inc(b_set.at(item), 1)

            def v_sums(item):
                dve.wait_ge(v_set.at(item), v_set.count(item))
                norm_sums(dve, st_v[0], item, v[item.slot(PER)], v_stats[item.slot(PER)])

            def v_mean(item):
                norm_mean(dve, k, st_v[0:2], item, v_stats[item.slot(PER)], v_mv[item.slot(PER)])

            def gain(item):
                s = item.slot(PER)
                dve.wait_ge(st_v[1].at(item), st_v[1].count(item))
                dve.scalar_tensor_tensor(v[s][:, 0, :], v[s][:, 0, :], v_mv[s][:, 0, 0:1], k.gamma[:, :],
                                         ALU.subtract, ALU.mult)\
                    .then_inc(a_set.at(item), 1)

            def make_s(item):
                s = item.slot(PER)
                dve.wait_ge(a_set.at(item), a_set.count(item))
                dve.wait_ge(b_set.at(item), b_set.count(item))
                dve.wait_ge(st_v[3].at(item), st_v[3].count(item))
                dve.scalar_tensor_tensor(v[s][:, 0, :], v[s][:, 0, :], v_rstd[s][:, 0:1], x1b[s][:, :],
                                         ALU.mult, ALU.add)\
                    .then_inc(s_set.at(item), 1)

            def s_sums(item):
                dve.wait_ge(s_set.at(item), s_set.count(item))
                norm_sums(dve, st_s[0], item, v[item.slot(PER)], s_stats[item.slot(PER)])

            def s_mean(item):
                norm_mean(dve, k, st_s[0:2], item, s_stats[item.slot(PER)], s_mv[item.slot(PER)])

            def shift(item):
                s = item.slot(PER)
                norm_shift(dve, st_s[3:5], item, s_mv[s], s_rstd[s][:, :], s_shift[s][:, :])

            each_item(dve, T, PER, (7, gain), (3, front), (8, shift), (7, make_s), (4, sum_own), (7, s_sums),
                             (6, make_v), (7, s_mean), (6, v_sums), (0, index_src), (8, index_last), (6, v_mean))


_INS = ["x", "src", "dst", "edge_attr_256", "L0_gnn_ln_w", "L0_gnn_ln_b", "L0_gnn_W1", "L0_gnn_att_src1",
        "L0_gnn_att_dst1", "L0_gnn_b1", "L0_gnn_W2", "L0_gnn_att_src2", "L0_gnn_att_dst2", "L0_gnn_b2",
        "L1_gnn_W1", "L1_gnn_b1", "L1_gnn_W2", "L1_gnn_b2", "L1_gnn_gamma", "L1_gnn_beta"]


def kernel(**inputs):
    import numpy as _np
    import concourse.bacc as _bacc
    from concourse import mybir as _mybir
    from concourse.bass_utils import run_bass_kernel_spmd as _run

    nc = _bacc.Bacc("TRN2", target_bir_lowering=False, num_devices=1)
    arrays, args = {}, []
    for name in _INS:
        a = _np.ascontiguousarray(inputs[name])
        arrays[f"in_{name}"] = a
        args.append(nc.dram_tensor(f"in_{name}", a.shape, _mybir.dt.from_np(a.dtype), kind="ExternalInput").ap())
    args.append(nc.dram_tensor("out_0", arrays["in_x"].shape, _mybir.dt.float32, kind="ExternalOutput").ap())
    build(nc, *args)
    r = _run(nc, [arrays], core_ids=[0])
    return r.results[0]["out_0"]
```
